# Optimizing a Trainium2 kernel written in Bass

```python
import numpy as np
import jax
import jax.numpy as jnp

def _softmax(x, axis=-1):
    return jax.nn.softmax(x, axis=axis)

def _gelu(x):
    return jax.nn.gelu(x, approximate=True)

def _silu(x):
    return jax.nn.silu(x)

def _sigmoid(x):
    return jax.nn.sigmoid(x)

def _layernorm(x, axis=-1, eps=1e-05):
    m = jnp.mean(x, axis=axis, keepdims=True)
    v = jnp.var(x, axis=axis, keepdims=True)
    return (x - m) / jnp.sqrt(v + eps)

def _scatter_add(tgt, idx, src, axis=0):
    return tgt.at[idx].add(src)

def _segment_sum(src, seg, n):
    return jax.ops.segment_sum(src, seg, n)
kernel_name = 'mk_hybrid_d1_jaxref_r8_881011'

def setup_inputs(seed: int=0):
    np.random.seed(seed)
    _w = jnp.asarray

    def _L0_attn_a_setup():
        import jax, jax.numpy as jnp
        import numpy as np
        from jax import lax
        SPLIT = 8
        DIM = 16
        EPS = 1e-05

        def _branch(q, k, v, cw, cb, H_sp, W_sp, Hg, Wg):
            B, N, C = q.shape
            hd = C
            scale = hd ** (-0.5)
            wsz = H_sp * W_sp
            nh, nw = (Hg // H_sp, Wg // W_sp)

            def part(t):
                t = t.reshape(B, nh, H_sp, nw, W_sp, C).transpose(0, 1, 3, 2, 4, 5)
                return t.reshape(-1, wsz, 1, hd).transpose(0, 2, 1, 3)
            vimg = v.reshape(B, nh, H_sp, nw, W_sp, C).transpose(0, 1, 3, 5, 2, 4)
            vimg = vimg.reshape(-1, C, H_sp, W_sp)
            lepe = lax.conv_general_dilated(vimg, cw, (1, 1), [(1, 1), (1, 1)], dimension_numbers=('NCHW', 'OIHW', 'NCHW'), feature_group_count=C)
            lepe = lepe + cb[None, :, None, None]
            lepe = lepe.reshape(-1, 1, hd, wsz).transpose(0, 1, 3, 2)
            vw = vimg.reshape(-1, 1, hd, wsz).transpose(0, 1, 3, 2)
            attn = jax.nn.softmax(part(q) * scale @ jnp.swapaxes(part(k), -1, -2), axis=-1)
            out = attn @ vw + lepe
            out = out.transpose(0, 2, 1, 3).reshape(B, nh, nw, H_sp, W_sp, C)
            out = out.transpose(0, 1, 3, 2, 4, 5).reshape(B, N, C)
            return out
        key = jax.random.key(seed)
        ks = jax.random.split(key, 8)
        B, H, W = (8, 256, 256)
        d = DIM
        h = d // 2
        return {'x': jax.random.normal(ks[0], (B, H, W), jnp.float32), 'qkv_w': jax.random.normal(ks[1], (d, 3 * d), jnp.float32) * d ** (-0.5), 'conv_w0': jax.random.normal(ks[2], (h, 1, 3, 3), jnp.float32) * 0.3, 'conv_b0': jax.random.normal(ks[3], (h,), jnp.float32) * 0.02, 'conv_w1': jax.random.normal(ks[4], (h, 1, 3, 3), jnp.float32) * 0.3, 'conv_b1': jax.random.normal(ks[5], (h,), jnp.float32) * 0.02, 'proj_w': jax.random.normal(ks[6], (d, d), jnp.float32) * d ** (-0.5), 'proj_b': jax.random.normal(ks[7], (d,), jnp.float32) * 0.02, 'ln_w': jnp.ones((d,), jnp.float32), 'ln_b': jnp.zeros((d,), jnp.float32)}
    _L0_attn_a_in = _L0_attn_a_setup()

    def _L0_attn_b_setup():
        import jax, jax.numpy as jnp
        import numpy as np
        NUM_HEADS = 16
        ROPE_BASE = 10000.0

        def _rotate_half(x):
            half = x.shape[-1] // 2
            x1, x2 = (x[..., :half], x[..., half:])
            return jnp.concatenate((-x2, x1), axis=-1)

        def _rope_cos_sin(seq_len, dim, dtype):
            inv_freq = 1.0 / ROPE_BASE ** (jnp.arange(0, dim, 2, dtype=jnp.float32) / dim)
            t = jnp.arange(seq_len, dtype=jnp.float32)
            freqs = jnp.einsum('i,j->ij', t, inv_freq)
            emb = jnp.concatenate((freqs, freqs), axis=-1)
            return (emb.astype(dtype), None)
        key = jax.random.key(seed)
        k1, k2, k3 = jax.random.split(key, 3)
        B, S, D = (4, 128, 256)
        return {'hidden_states': jax.random.normal(k1, (B, S, D), dtype=jnp.float32), 'w_qkv': jax.random.normal(k2, (3 * D, D), dtype=jnp.float32) * 0.02, 'b_qkv': jax.random.normal(k3, (3 * D,), dtype=jnp.float32) * 0.02}
    _L0_attn_b_in = _L0_attn_b_setup()

    def _L0_ffn_setup():
        import jax, jax.numpy as jnp
        import numpy as np
        BLOCK_SIZE = 32
        HIDDEN_SIZE = 256
        MLP_DIM = 2048
        NVFP4_LUT = jnp.array([0.0, 0.5, 1.0, 1.5, 2.0, 3.0, 4.0, 6.0, 0.0, -0.5, -1.0, -1.5, -2.0, -3.0, -4.0, -6.0], dtype=jnp.float32)

        def dequant_nvfp4(W_packed, scales, block=BLOCK_SIZE):
            N = W_packed.shape[0]
            low = W_packed & 15
            high = W_packed >> 4 & 15
            idx = jnp.stack([low, high], axis=-1).reshape(N, -1)
            vals = NVFP4_LUT[idx]
            K = vals.shape[1]
            vals = vals.reshape(N, K // block, block) * scales[:, :, None]
            return vals.reshape(N, K)
        key = jax.random.key(seed)
        ks = jax.random.split(key, 7)
        x = jax.random.normal(ks[0], (4, 32, HIDDEN_SIZE), dtype=jnp.float32)
        gate_W_packed = jax.random.randint(ks[1], (MLP_DIM, HIDDEN_SIZE // 2), 0, 32, dtype=jnp.int32)
        gate_scales = jax.random.uniform(ks[2], (MLP_DIM, HIDDEN_SIZE // BLOCK_SIZE), dtype=jnp.float32) * 0.1 + 0.001
        up_W_packed = jax.random.randint(ks[3], (MLP_DIM, HIDDEN_SIZE // 2), 0, 32, dtype=jnp.int32)
        up_scales = jax.random.uniform(ks[4], (MLP_DIM, HIDDEN_SIZE // BLOCK_SIZE), dtype=jnp.float32) * 0.1 + 0.001
        down_W_packed = jax.random.randint(ks[5], (HIDDEN_SIZE, MLP_DIM // 2), 0, 32, dtype=jnp.int32)
        down_scales = jax.random.uniform(ks[6], (HIDDEN_SIZE, MLP_DIM // BLOCK_SIZE), dtype=jnp.float32) * 0.1 + 0.001
        return {'x': x, 'gate_W_packed': gate_W_packed, 'gate_scales': gate_scales, 'up_W_packed': up_W_packed, 'up_scales': up_scales, 'down_W_packed': down_W_packed, 'down_scales': down_scales}
    _L0_ffn_in = _L0_ffn_setup()
    _d = {'L0_attn_a_x': _L0_attn_a_in['x'], 'L0_attn_a_qkv_w': _L0_attn_a_in['qkv_w'], 'L0_attn_a_conv_w0': _L0_attn_a_in['conv_w0'], 'L0_attn_a_conv_b0': _L0_attn_a_in['conv_b0'], 'L0_attn_a_conv_w1': _L0_attn_a_in['conv_w1'], 'L0_attn_a_conv_b1': _L0_attn_a_in['conv_b1'], 'L0_attn_a_proj_w': _L0_attn_a_in['proj_w'], 'L0_attn_a_proj_b': _L0_attn_a_in['proj_b'], 'L0_attn_a_ln_w': _L0_attn_a_in['ln_w'], 'L0_attn_a_ln_b': _L0_attn_a_in['ln_b'], 'L0_attn_b_w_qkv': _L0_attn_b_in['w_qkv'], 'L0_attn_b_b_qkv': _L0_attn_b_in['b_qkv'], 'L0_ffn_gate_W_packed': _L0_ffn_in['gate_W_packed'], 'L0_ffn_gate_scales': _L0_ffn_in['gate_scales'], 'L0_ffn_up_W_packed': _L0_ffn_in['up_W_packed'], 'L0_ffn_up_scales': _L0_ffn_in['up_scales'], 'L0_ffn_down_W_packed': _L0_ffn_in['down_W_packed'], 'L0_ffn_down_scales': _L0_ffn_in['down_scales']}
    _x0 = _d['L0_attn_a_x']
    _d['L0_attn_a_x'] = jax.random.normal(jax.random.fold_in(jax.random.key(seed), 1), (4, 512, 256), dtype=_x0.dtype)
    del _x0
    return _d

def reference(L0_attn_a_x, L0_attn_a_qkv_w, L0_attn_a_conv_w0, L0_attn_a_conv_b0, L0_attn_a_conv_w1, L0_attn_a_conv_b1, L0_attn_a_proj_w, L0_attn_a_proj_b, L0_attn_a_ln_w, L0_attn_a_ln_b, L0_attn_b_w_qkv, L0_attn_b_b_qkv, L0_ffn_gate_W_packed, L0_ffn_gate_scales, L0_ffn_up_W_packed, L0_ffn_up_scales, L0_ffn_down_W_packed, L0_ffn_down_scales):

    def _L0_attn_a_ref(x, qkv_w, conv_w0, conv_b0, conv_w1, conv_b1, proj_w, proj_b, ln_w, ln_b):
        import jax, jax.numpy as jnp
        import numpy as np
        from jax import lax
        SPLIT = 8
        DIM = 16
        EPS = 1e-05

        def _branch(q, k, v, cw, cb, H_sp, W_sp, Hg, Wg):
            B, N, C = q.shape
            hd = C
            scale = hd ** (-0.5)
            wsz = H_sp * W_sp
            nh, nw = (Hg // H_sp, Wg // W_sp)

            def part(t):
                t = t.reshape(B, nh, H_sp, nw, W_sp, C).transpose(0, 1, 3, 2, 4, 5)
                return t.reshape(-1, wsz, 1, hd).transpose(0, 2, 1, 3)
            vimg = v.reshape(B, nh, H_sp, nw, W_sp, C).transpose(0, 1, 3, 5, 2, 4)
            vimg = vimg.reshape(-1, C, H_sp, W_sp)
            lepe = lax.conv_general_dilated(vimg, cw, (1, 1), [(1, 1), (1, 1)], dimension_numbers=('NCHW', 'OIHW', 'NCHW'), feature_group_count=C)
            lepe = lepe + cb[None, :, None, None]
            lepe = lepe.reshape(-1, 1, hd, wsz).transpose(0, 1, 3, 2)
            vw = vimg.reshape(-1, 1, hd, wsz).transpose(0, 1, 3, 2)
            attn = jax.nn.softmax(part(q) * scale @ jnp.swapaxes(part(k), -1, -2), axis=-1)
            out = attn @ vw + lepe
            out = out.transpose(0, 2, 1, 3).reshape(B, nh, nw, H_sp, W_sp, C)
            out = out.transpose(0, 1, 3, 2, 4, 5).reshape(B, N, C)
            return out
        B, H, W = x.shape
        Hg, Wg = (H // 4, W // 4)
        C = DIM
        tok = x.reshape(B, H * W // C, C)
        qkv = (tok @ qkv_w).reshape(B, -1, 3, C)
        q, k, v = (qkv[:, :, 0], qkv[:, :, 1], qkv[:, :, 2])
        h = C // 2
        x1 = _branch(q[..., :h], k[..., :h], v[..., :h], conv_w0, conv_b0, 1, SPLIT, Hg, Wg)
        x2 = _branch(q[..., h:], k[..., h:], v[..., h:], conv_w1, conv_b1, SPLIT, 1, Hg, Wg)
        att = jnp.concatenate([x1, x2], axis=-1) @ proj_w + proj_b
        mu = att.mean(-1, keepdims=True)
        var = ((att - mu) ** 2).mean(-1, keepdims=True)
        normed = (att - mu) * lax.rsqrt(var + EPS) * ln_w + ln_b
        tok = tok + normed
        return jnp.transpose(tok, (0, 2, 1)).reshape(B, H, W)

    def _L0_attn_b_ref(hidden_states, w_qkv, b_qkv):
        import jax, jax.numpy as jnp
        import numpy as np
        NUM_HEADS = 16
        ROPE_BASE = 10000.0

        def _rotate_half(x):
            half = x.shape[-1] // 2
            x1, x2 = (x[..., :half], x[..., half:])
            return jnp.concatenate((-x2, x1), axis=-1)

        def _rope_cos_sin(seq_len, dim, dtype):
            inv_freq = 1.0 / ROPE_BASE ** (jnp.arange(0, dim, 2, dtype=jnp.float32) / dim)
            t = jnp.arange(seq_len, dtype=jnp.float32)
            freqs = jnp.einsum('i,j->ij', t, inv_freq)
            emb = jnp.concatenate((freqs, freqs), axis=-1)
            return (emb.astype(dtype), None)
        B, S, D = hidden_states.shape
        H = NUM_HEADS
        hd = D // H
        qkv = jnp.einsum('bsd,ed->bse', hidden_states, w_qkv) + b_qkv
        qkv = qkv.reshape(B, S, H, 3 * hd)
        q = jnp.transpose(qkv[..., :hd], (0, 2, 1, 3))
        k = jnp.transpose(qkv[..., hd:2 * hd], (0, 2, 1, 3))
        v = jnp.transpose(qkv[..., 2 * hd:], (0, 2, 1, 3))
        emb, _ = _rope_cos_sin(S, hd, hidden_states.dtype)
        cos = jnp.cos(emb)[None, None, :, :]
        sin = jnp.sin(emb)[None, None, :, :]
        q = q * cos + _rotate_half(q) * sin
        k = k * cos + _rotate_half(k) * sin
        norm = jnp.sqrt(jnp.asarray(hd, dtype=jnp.float32)).astype(q.dtype)
        scores = jnp.einsum('bhqd,bhkd->bhqk', q, k) / norm
        causal = jnp.tril(jnp.ones((S, S), dtype=bool))[None, None]
        mask_value = jnp.finfo(scores.dtype).min
        scores = jnp.where(causal, scores, mask_value)
        attn = jax.nn.softmax(scores, axis=-1)
        out = jnp.einsum('bhqk,bhkd->bhqd', attn, v)
        return jnp.transpose(out, (0, 2, 1, 3)).reshape(B, S, D)

    def _L0_ffn_ref(x, gate_W_packed, gate_scales, up_W_packed, up_scales, down_W_packed, down_scales):
        import jax, jax.numpy as jnp
        import numpy as np
        BLOCK_SIZE = 32
        HIDDEN_SIZE = 256
        MLP_DIM = 2048
        NVFP4_LUT = jnp.array([0.0, 0.5, 1.0, 1.5, 2.0, 3.0, 4.0, 6.0, 0.0, -0.5, -1.0, -1.5, -2.0, -3.0, -4.0, -6.0], dtype=jnp.float32)

        def dequant_nvfp4(W_packed, scales, block=BLOCK_SIZE):
            N = W_packed.shape[0]
            low = W_packed & 15
            high = W_packed >> 4 & 15
            idx = jnp.stack([low, high], axis=-1).reshape(N, -1)
            vals = NVFP4_LUT[idx]
            K = vals.shape[1]
            vals = vals.reshape(N, K // block, block) * scales[:, :, None]
            return vals.reshape(N, K)
        B, S, H = x.shape
        xt = x.reshape(B * S, H)
        Wg = dequant_nvfp4(gate_W_packed, gate_scales)
        Wu = dequant_nvfp4(up_W_packed, up_scales)
        Wd = dequant_nvfp4(down_W_packed, down_scales)
        gate = jnp.einsum('th,nh->tn', xt, Wg)
        up = jnp.einsum('th,nh->tn', xt, Wu)
        gelu = jnp.tanh(0.7978845608028654 * (gate + 0.044715 * gate ** 3)) * gate * 0.5 + gate * 0.5
        inter = gelu * up
        out = jnp.einsum('tn,hn->th', inter, Wd)
        return out.reshape(B, S, H)
    x = L0_attn_a_x
    x = x + _L0_attn_a_ref(_layernorm(x, axis=-1), L0_attn_a_qkv_w, L0_attn_a_conv_w0, L0_attn_a_conv_b0, L0_attn_a_conv_w1, L0_attn_a_conv_b1, L0_attn_a_proj_w, L0_attn_a_proj_b, L0_attn_a_ln_w, L0_attn_a_ln_b)
    x = x + _L0_ffn_ref(_layernorm(x, axis=-1), L0_ffn_gate_W_packed, L0_ffn_gate_scales, L0_ffn_up_W_packed, L0_ffn_up_scales, L0_ffn_down_W_packed, L0_ffn_down_scales)
    x = x + _L0_attn_b_ref(_layernorm(x, axis=-1), L0_attn_b_w_qkv, L0_attn_b_b_qkv)
    x = x + _L0_ffn_ref(_layernorm(x, axis=-1), L0_ffn_gate_W_packed, L0_ffn_gate_scales, L0_ffn_up_W_packed, L0_ffn_up_scales, L0_ffn_down_W_packed, L0_ffn_down_scales)
    return x

_drawn_inputs = setup_inputs


def setup_inputs(seed=0):
    import zlib

    import numpy as np

    out = dict(_drawn_inputs(seed))
    spreads = {'L0_attn_a_ln_w': (1.0, 0.2), 'L0_attn_a_ln_b': (0.0, 2.0)}
    factors = {'L0_attn_a_conv_b0': 3.536,
     'L0_attn_a_conv_b1': 4.953,
     'L0_attn_a_proj_b': 4.656,
     'L0_attn_b_w_qkv': 8.0,
     'L0_attn_b_b_qkv': 8.0}
    for name, (base, spread) in spreads.items():
        noise = np.random.default_rng([zlib.crc32(name.encode()), seed]).standard_normal(out[name].shape)
        drawn = base * np.exp(spread * noise) if base else spread * noise
        out[name] = jnp.asarray(drawn.astype(out[name].dtype))
    for name, factor in factors.items():
        out[name] = (out[name] * factor).astype(out[name].dtype)
    return out
```

```python
from contextlib import ExitStack

import numpy as np

import concourse.bass as bass
from concourse import mybir

P = 128
B, ROWS, D = 4, 512, 256
RT = ROWS // P
KT = D // P
CH = 16
HCH = CH // 2
WIN = 8
HALVES = D // (WIN * CH)
WG = RT * HALVES
BLK = WIN * HCH
F = 2048
NCH = F // P
QB = 32
NH, HD = 16, 16
HG = P // HD
OW = 32
EPS = 1e-5
NEG = -1e30

X_EXP = 11
W_EXP = 12
I_EXP = -8
MAX_EXP = 8

C_ID, C_ROT, C_MQK, C_MKQ, C_COS, C_SIN = 0, 128, 256, 384, 512, 1024
C_ALL = 1536

QK_STRIP = {3: (0, 512), 2: (512, 384), 0: (896, 128), 1: (1024, 256)}
KQ_STRIP = {0: (0, 512), 1: (512, 384), 3: (896, 128), 2: (1024, 256)}
STRIPS = 1280

MATRICES = ("gate", "up", "down")

SIGNALS = """
consts_in attn_a_weights_in attn_b_weights_in gate_words_in up_words_in down_words_in gate_scale_in up_scale_in down_scale_in zeroed masks_cast
scale_max_ready scale_max_all words_read weight_f32_ready weight_hi_ready weight_lo_ready
x_in x_out_stored var_ready rstd_ready xn_ready xt_ready xt_evacuated xt_lo_ready
dve_chain act_chain pool_chain
a_qkv_ready a_qkv_out a_qk_prod a_score_shifted a_exp_ready a_av_prod a_lepe_ready a_branch_ready
a_branch_t_ready a_branch_t_out a_proj_ready a_sq_ready a_centered a_tok_ready a_stored a_back
gate_ready up_ready square_ready cubic_ready tanh_ready inter_ready inter_hi_ready inter_lo_ready
down_used down_ready down_out down_t_ready f_done
b_proj_ready b_proj_out b_rot_ready b_cos_ready b_rope_ready b_hi_ready b_lo_ready b_stacked
b_v_ready b_v_out b_qk_ready b_max_taken b_max_scaled b_max_t_ready b_max_hi b_max_lo b_max_in
b_kq_ready b_exp_ready b_av_done b_o_ready b_o_out b_o_t_ready b_o_added
""".split()


def program(nc, x, qkv_w, conv_w0, conv_b0, conv_w1, conv_b1, proj_w, proj_b, ln_w, ln_b,
            w_qkv_t, b_qkv, gate_words, gate_scale_t, up_words, up_scale_t, down_words, down_scale_t,
            consts, scratch, out):
    f32, f16, bf16, i32 = mybir.dt.float32, mybir.dt.float16, mybir.dt.bfloat16, mybir.dt.int32
    ALU = mybir.AluOpType
    ACT = mybir.ActivationFunctionType
    AX = mybir.AxisListType

    ctx = ExitStack()
    with ctx:
        def sb(name, shape, dt=f32):
            return ctx.enter_context(nc.sbuf_tensor(name, shape, dt))

        s = {}
        for name in SIGNALS:
            s[name] = ctx.enter_context(nc.semaphore(name))
        all_signals = range(s[SIGNALS[0]].num, s[SIGNALS[-1]].num + 1)
        assert len(all_signals) == len(SIGNALS)

        con = sb("con", [P, C_ALL])
        ident = con[:, C_ID:C_ID + P]
        rot_t = con[:, C_ROT:C_ROT + P]
        cos_t = con[:, C_COS:C_COS + ROWS]
        sin_t = con[:, C_SIN:C_SIN + ROWS]
        masks = sb("masks", [P, 3, P], bf16)
        bd1 = sb("bd1", [P, 3, WIN, HCH])
        bd2 = sb("bd2", [P, 3, WIN, HCH])
        bdp1 = sb("bdp1", [BLK, WIN, CH])
        bdp2 = sb("bdp2", [BLK, WIN, CH])
        conv = sb("conv", [P, 2, 4, HCH])
        pb_ = sb("pb_", [P, CH])
        lw = sb("lw", [P, CH])
        lb = sb("lb", [P, CH])
        wqk = sb("wqk", [P, KT, 2, NH * HD])
        wv = sb("wv", [P, KT, NH * HD])
        bqk = sb("bqk", [P, 2, 2])
        bv = sb("bv", [P, NH, HD])
        w_hi = [sb(f"w_hi{m}", [P, 2 * F], f16) for m in range(3)]
        w_lo = [sb(f"w_lo{m}", [P, 2 * F], f16) for m in range(3)]
        smax = sb("smax", [P, 3])
        gmax = sb("gmax", [P, 3])
        pow2 = sb("pow2", [P, 3])
        rpow2 = sb("rpow2", [P, 3])
        c_sq = sb("c_sq", [P, 1])
        c_th = sb("c_th", [P, 1])
        c_dn = sb("c_dn", [P, 1])
        half_neg = sb("half_neg", [P, 4 * CH])
        va = sb("va", [P, RT, NH, OW])

        X = sb("X", [P, RT, D])
        xn = sb("xn", [P, RT, D])
        stats = sb("stats", [P, RT, 6])
        mv = sb("mv", [P, RT, 2])
        veps = sb("veps", [P, RT])
        rstd = sb("rstd", [P, RT])
        xt = sb("xt", [P, KT, ROWS])
        xh = sb("xh", [P, KT, ROWS], f16)
        xl = sb("xl", [P, KT, ROWS], f16)

        arena = sb("arena", [P, 16384])
        arena_at = [0]

        def part(shape, dt=f32):
            n = int(np.prod(shape[1:]))
            words = n if dt in (f32, i32) else n // 2
            at = arena_at[0]
            arena_at[0] = at + words
            assert arena_at[0] <= 16384
            v = arena[0:shape[0], at:at + words]
            if dt != f32:
                v = v.bitcast(dt)
            names = "abcd"[:len(shape) - 1]
            if len(names) == 1:
                return v
            return v.rearrange(f"p ({' '.join(names)}) -> p {' '.join(names)}",
                               **{k: n for k, n in zip(names, shape[1:])})

        banks = ctx.enter_context(nc.psum_tensor("banks", [P, 8, 512], f32))

        def bank(i, n=1):
            return banks[:, i:i + n, :].rearrange("p a b -> p (a b)")

        def chain(eng, sem):
            count = [0]

            def link(ins):
                count[0] += 1
                ins.then_inc(sem, 1)
                eng.wait_ge(sem, count[0])
            return link

        words = [part([P, F], i32) for _ in range(2)]
        scale = [part([P, F]) for _ in range(2)]
        both = part([P, F], i32)
        magn = part([P, F], i32)
        wf = part([P, 2 * F])
        arena_at[0] = 0

        with nc.Block() as block:
            @block.sync
            def _(sp):
                def load_matrix(m):
                    w, sc, down = ((gate_words, gate_scale_t, False), (up_words, up_scale_t, False),
                                   (down_words, down_scale_t, True))[m]
                    words_in, scale_in = s[MATRICES[m] + "_words_in"], s[MATRICES[m] + "_scale_in"]
                    if not down:
                        sp.dma_start(words[m % 2], w).then_inc(words_in, 16)
                        sp.dma_start(scale[m % 2], sc.unsqueeze(1).broadcast_to([D // QB, QB // 2, F])
                                     ).then_inc(scale_in, 16)
                    else:
                        sp.dma_start(words[m % 2].rearrange("p (c h) -> p c h", h=D),
                                     w.rearrange("(c p) h -> p c h", p=P)).then_inc(words_in, 16)
                        for c in range(F // D):
                            sp.dma_start(scale[m % 2][:, c * D:(c + 1) * D],
                                         sc[8 * c:8 * c + 8, :].unsqueeze(1).broadcast_to([8, QB // 2, D])
                                         ).then_inc(scale_in, 16)

                load_matrix(0)
                load_matrix(1)
                sp.dma_start(con[:], consts).then_inc(s["consts_in"], 16)
                sp.wait_ge(s["zeroed"], 1)
                for t in range(WIN):
                    for which in range(3):
                        c0 = which * CH
                        sp.dma_start(bd1[CH * t:CH * t + CH, which, t, :], qkv_w[:, c0:c0 + HCH]
                                     ).then_inc(s["attn_a_weights_in"], 16)
                        sp.dma_start(bd2[CH * t:CH * t + CH, which, t, :], qkv_w[:, c0 + HCH:c0 + CH]
                                     ).then_inc(s["attn_a_weights_in"], 16)
                    sp.dma_start(bdp1[HCH * t:HCH * t + HCH, t, :], proj_w[0:HCH, :]
                                 ).then_inc(s["attn_a_weights_in"], 16)
                    sp.dma_start(bdp2[HCH * t:HCH * t + HCH, t, :], proj_w[HCH:CH, :]
                                 ).then_inc(s["attn_a_weights_in"], 16)
                for br, (cw, cb) in enumerate(((conv_w0, conv_b0), (conv_w1, conv_b1))):
                    for tap in range(3):
                        src = cw[1, tap, 0, :] if br == 0 else cw[tap, 1, 0, :]
                        sp.dma_start(conv[:, br, tap, :], src.unsqueeze(0).broadcast_to([P, HCH])
                                     ).then_inc(s["attn_a_weights_in"], 16)
                    sp.dma_start(conv[:, br, 3, :], cb.unsqueeze(0).broadcast_to([P, HCH])
                                 ).then_inc(s["attn_a_weights_in"], 16)
                for dst, src in ((pb_, proj_b), (lw, ln_w), (lb, ln_b)):
                    sp.dma_start(dst[:, :], src.unsqueeze(0).broadcast_to([P, CH])
                                 ).then_inc(s["attn_a_weights_in"], 16)
                for kt in range(KT):
                    rows = w_qkv_t[kt * P:(kt + 1) * P, :].rearrange("p (n w c) -> p w n c", w=3, c=HD)
                    for which in range(2):
                        sp.dma_start(wqk[:, kt, which, :].rearrange("p (n c) -> p n c", c=HD), rows[:, which]
                                     ).then_inc(s["attn_b_weights_in"], 16)
                    sp.dma_start(wv[:, kt, :].rearrange("p (n c) -> p n c", c=HD), rows[:, 2]
                                 ).then_inc(s["attn_b_weights_in"], 16)
                bias = b_qkv.rearrange("(n w c) -> w n c", w=3, c=HD)
                for which in range(2):
                    for g in range(2):
                        for n in range(HG):
                            sp.dma_start(bqk[HD * n:HD * n + HD, which, g:g + 1],
                                         bias[which, HG * g + n, :].unsqueeze(1)
                                         ).then_inc(s["attn_b_weights_in"], 16)
                for n in range(NH):
                    sp.dma_start(bv[:, n, :], bias[2, n, :].unsqueeze(0).broadcast_to([P, HD])
                                 ).then_inc(s["attn_b_weights_in"], 16)
                sp.wait_ge(s["words_read"], 1)
                sp.wait_ge(s["weight_f32_ready"], 1)
                load_matrix(2)
                sp.wait_ge(s["consts_in"], 16)
                sp.wait_ge(s["attn_a_weights_in"], 16 * (WIN * 8 + 8 + 3))
                sp.wait_ge(s["attn_b_weights_in"], 16 * (KT * 3 + 4 * HG + NH))

            @block.gpsimd
            def _(pool):
                link = chain(pool, s["pool_chain"])
                for t in (bd1, bd2, bdp1, bdp2):
                    nc.gpsimd.memset(t[:], 0.0)
                nc.gpsimd.memset(half_neg[:], -0.5)
                link(nc.gpsimd.memset(va[:], 0.0))
                nc.gpsimd.memset(va[:, :, :, HD:HD + 1], 1.0).then_inc(s["zeroed"], 1)
                for m in range(3):
                    pool.wait_ge(s["scale_max_ready"], m + 1)
                    nc.gpsimd.partition_all_reduce(gmax[:, m:m + 1], smax[:, m:m + 1], P,
                                                   bass.bass_isa.ReduceOp.max).then_inc(s["scale_max_all"], 1)
                    pool.wait_ge(s["weight_hi_ready"], m + 1)
                    nc.gpsimd.tensor_tensor(w_lo[m][:], wf, w_hi[m][:], ALU.subtract
                                            ).then_inc(s["weight_lo_ready"], 1)

            @block.scalar
            def _(act):
                for m in range(3):
                    act.wait_ge(s["weight_f32_ready"], m + 1)
                    nc.scalar.activation(w_hi[m][:], wf, ACT.Copy).then_inc(s["weight_hi_ready"], 1)

            @block.vector
            def _(dve):
                link = chain(dve, s["dve_chain"])
                dve.wait_ge(s["consts_in"], 16)
                nc.vector.tensor_copy(masks[:, 0, :], ident)
                nc.vector.tensor_copy(masks[:, 1:3, :],
                                      con[:, C_MQK:C_MQK + 2 * P].rearrange("p (a b) -> p a b", a=2)
                                      ).then_inc(s["masks_cast"], 1)
                for m in range(3):
                    w, sc = words[m % 2], scale[m % 2]
                    dve.wait_ge(s[MATRICES[m] + "_scale_in"], 16 if m < 2 else 16 * (F // D))
                    nc.vector.tensor_reduce(smax[:, m:m + 1], sc, AX.X, ALU.max,
                                            apply_absolute_value=True).then_inc(s["scale_max_ready"], 1)
                    dve.wait_ge(s[MATRICES[m] + "_words_in"], 16)
                    ins = nc.vector.scalar_tensor_tensor(both, w, 12, w, ALU.logical_shift_left, ALU.bitwise_or)
                    link(ins)
                    nc.vector.tensor_scalar(magn, both, 0x00070007, 9, ALU.bitwise_and, ALU.logical_shift_left)
                    link(nc.vector.tensor_scalar(w, both, 0x00080008, 12, ALU.bitwise_and,
                                                 ALU.logical_shift_left))
                    link(nc.vector.tensor_tensor(magn, magn, w, ALU.bitwise_or))
                    nc.vector.nop().then_inc(s["words_read"], 1)
                    dve.wait_ge(s["scale_max_all"], m + 1)
                    link(nc.vector.tensor_scalar(gmax[:, m:m + 1], gmax[:, m:m + 1], 1e-30, None, ALU.max))
                    link(nc.vector.tensor_scalar(pow2[:, m:m + 1].bitcast(i32), gmax[:, m:m + 1].bitcast(i32),
                                                 0x7F800000, None, ALU.bitwise_and))
                    link(nc.vector.reciprocal(rpow2[:, m:m + 1], pow2[:, m:m + 1]))
                    link(nc.vector.tensor_scalar(sc, sc, rpow2[:, m:m + 1], 2.0 ** (W_EXP + 14),
                                                 ALU.mult, ALU.mult))
                    if m >= 1:
                        dve.wait_ge(s["weight_lo_ready"], m)
                    val = magn.bitcast(f16)
                    for nib in range(2):
                        if m < 2:
                            o = wf[:, nib * F:(nib + 1) * F].rearrange("p (c e u) -> p c e u", e=2, u=P)
                            v = val.rearrange("p (c u e k) -> p k c e u", e=2, u=P, k=2)[:, nib]
                            g = sc.rearrange("p (c u e) -> p c e u", e=2, u=P)
                            for e in range(2):
                                ins = nc.vector.tensor_tensor(o[:, :, e], v[:, :, e], g[:, :, e], ALU.mult)
                        else:
                            o = wf.rearrange("p (c e h) -> p c e h", e=2, h=D)[:, :, nib]
                            v = val.rearrange("p (c h e) -> p e c h", e=2, h=D)[:, nib]
                            ins = nc.vector.tensor_tensor(o, v, sc.rearrange("p (c h) -> p c h", h=D), ALU.mult)
                    ins.then_inc(s["weight_f32_ready"], 1)
                back = 2.0 ** -(X_EXP + W_EXP)
                link(nc.vector.tensor_scalar(c_th[:], pow2[:, 0:1], 0.7978845608028654 * back, None, ALU.mult))
                link(nc.vector.tensor_scalar(c_sq[:], pow2[:, 0:1], 0.044715 ** 0.5 * back, None, ALU.mult))
                link(nc.vector.tensor_tensor(c_dn[:], pow2[:, 0:1], pow2[:, 1:2], ALU.mult))
                link(nc.vector.tensor_scalar(c_dn[:], c_dn[:], pow2[:, 2:3], 2.0 ** -(W_EXP + I_EXP),
                                             ALU.mult, ALU.mult))

        nc.all_engine_barrier(sems_to_clear=all_signals)

        def ln_stats(dve, link, src):
            for j in range(RT):
                ins = nc.vector.bn_stats(stats[:, j, :], src[:, j, :])
            link(ins)
            for j in range(RT):
                ins = nc.vector.bn_aggr(mv[:, j, :], stats[:, j, :])
            link(ins)
            nc.vector.tensor_scalar(veps[:], mv[:, :, 1], EPS, None, ALU.add).then_inc(s["var_ready"], 1)

        def ln_root(pool):
            pool.wait_ge(s["var_ready"], 1)
            nc.gpsimd.tensor_tensor(rstd[:], veps[:], half_neg[:, 0:RT], ALU.pow).then_inc(s["rstd_ready"], 1)

        def ln_apply(dve, link, src, factor):
            dve.wait_ge(s["rstd_ready"], 1)
            if factor != 1.0:
                link(nc.vector.tensor_scalar(rstd[:], rstd[:], factor, None, ALU.mult))
            for j in range(RT):
                nc.vector.tensor_scalar(xn[:, j, :], src[:, j, :], mv[:, j, 0:1], rstd[:, j:j + 1],
                                        ALU.subtract, ALU.mult).then_inc(s["xn_ready"], 1)

        def transpose_rows(pe, columns):
            for j in range(RT):
                pe.wait_ge(s["xn_ready"], j + 1)
                for kt in range(KT):
                    ins = nc.tensor.transpose(bank(6 + kt)[:, j * P:(j + 1) * P], columns(xn[:, j, :], kt), ident)
            ins.then_inc(s["xt_ready"], 1)

        arena_at[0] = 0
        qkv = [part([P, WG, 3, BLK]) for _ in range(2)]
        prod = [part([P, WG // 2, WIN * WIN * HCH]) for _ in range(2)]
        score = part([P, WG, WIN, WIN])
        smx = part([P, WG * WIN])
        ssum = part([P, WG * WIN])
        lepe = part([P, WG, WIN, HCH])
        tap = part([P, WG, WIN, HCH])
        xbr = [part([P, WG, WIN, HCH]) for _ in range(2)]
        brt = [part([BLK, HALVES, ROWS]) for _ in range(2)]
        att = part([P, RT * D])
        m16 = part([P, RT * CH])
        v16 = part([P, RT * CH])
        xta = part([P, HALVES, WIN, ROWS // WIN])
        att2 = prod[1].rearrange("p a b -> p (a b)")[:, 0:RT * D]
        tok = prod[1].rearrange("p a b -> p (a b)")[:, RT * D:2 * RT * D]

        def window_view(t, br, which=None):
            v = t[:, :, which, :] if which is not None else t[:].rearrange("p a b c -> p a (b c)")
            v = v.rearrange("p a (b c) -> p a b c", c=HCH)
            return v if br == 0 else v.rearrange("p a b c -> p b a c")

        def attention_a(b):
            scale_a = float(HCH) ** -0.5
            with nc.Block() as block:
                @block.sync
                def _(sp):
                    sp.dma_start(X[:], x[bass.ds(b, 1)].rearrange("o (j p) w -> p (o j) w", p=P)
                                 ).then_inc(s["x_in"], 16)
                    sp.wait_ge(s["a_tok_ready"], 1)
                    t4 = tok.rearrange("p (j c w) -> p j c w", j=RT, c=CH)
                    for j in range(RT):
                        dst = scratch[:, j * P * CH:(j + 1) * P * CH].rearrange("c (p w) -> p c w", w=CH)
                        sp.dma_start(dst, t4[:, j]).then_inc(s["a_stored"], 16)
                    sp.wait_ge(s["a_stored"], 16 * RT)
                    sp.dma_start(att.rearrange("p (j w) -> p j w", w=D),
                                 scratch.rearrange("c (q w) -> (c q) w", w=D).rearrange("(j p) w -> p j w", p=P)
                                 ).then_inc(s["a_back"], 16)

                @block.gpsimd
                def _(pool):
                    link = chain(pool, s["pool_chain"])
                    ln_root(pool)
                    for br in range(2):
                        q, k, v = (window_view(qkv[br], br, w) for w in range(3))
                        pool.wait_ge(s["a_qkv_out"], 4 * (br + 1))
                        for g in range(WG):
                            if br and g % 4 == 0:
                                pool.wait_ge(s["a_branch_ready"], 1)
                            nc.gpsimd.tensor_tensor(
                                prod[g // 4][:, g % 4, :].rearrange("p (i j c) -> p i j c", i=WIN, j=WIN),
                                q[:, g].unsqueeze(2).broadcast_to([P, WIN, WIN, HCH]),
                                k[:, g].unsqueeze(1).broadcast_to([P, WIN, WIN, HCH]), ALU.mult
                            ).then_inc(s["a_qk_prod"], 1)
                        w0, w1, w2, cb = (conv[:, br, t, :].unsqueeze(1).unsqueeze(1) for t in range(4))
                        if br:
                            pool.wait_ge(s["a_branch_ready"], 1)
                        link(nc.gpsimd.tensor_tensor(lepe[:], v, w1.broadcast_to([P, WG, WIN, HCH]), ALU.mult))
                        link(nc.gpsimd.tensor_tensor(tap[:, :, 1:WIN, :], v[:, :, 0:WIN - 1, :],
                                                     w0.broadcast_to([P, WG, WIN - 1, HCH]), ALU.mult))
                        link(nc.gpsimd.tensor_tensor(lepe[:, :, 1:WIN, :], lepe[:, :, 1:WIN, :],
                                                     tap[:, :, 1:WIN, :], ALU.add))
                        link(nc.gpsimd.tensor_tensor(tap[:, :, 0:WIN - 1, :], v[:, :, 1:WIN, :],
                                                     w2.broadcast_to([P, WG, WIN - 1, HCH]), ALU.mult))
                        link(nc.gpsimd.tensor_tensor(lepe[:, :, 0:WIN - 1, :], lepe[:, :, 0:WIN - 1, :],
                                                     tap[:, :, 0:WIN - 1, :], ALU.add))
                        nc.gpsimd.tensor_tensor(lepe[:], lepe[:], cb.broadcast_to([P, WG, WIN, HCH]), ALU.add
                                                ).then_inc(s["a_lepe_ready"], 1)
                        pool.wait_ge(s["a_exp_ready"], br + 1)
                        for g in range(WG):
                            nc.gpsimd.tensor_tensor(
                                prod[g // 4][:, g % 4, :].rearrange("p (i c j) -> p i c j", i=WIN, j=WIN),
                                score[:, g].unsqueeze(2).broadcast_to([P, WIN, HCH, WIN]),
                                v[:, g].rearrange("p j c -> p c j").unsqueeze(1).broadcast_to([P, WIN, HCH, WIN]),
                                ALU.mult).then_inc(s["a_av_prod"], 1)
                    pool.wait_ge(s["var_ready"], 2)
                    nc.gpsimd.tensor_tensor(v16, v16, half_neg[:], ALU.pow).then_inc(s["rstd_ready"], 1)

                @block.scalar
                def _(act):
                    act.wait_ge(s["xt_ready"], 1)
                    for kt in range(KT):
                        nc.scalar.copy(xt[:, kt, :], bank(6 + kt)).then_inc(s["xt_evacuated"], 1)
                    for kt in range(KT):
                        nc.scalar.copy(xta[:, kt].rearrange("p a (i r) -> p a i r", r=4),
                                       bank(6 + kt).rearrange("p (i a r) -> p a i r", a=WIN, r=4)
                                       ).then_inc(s["xt_evacuated"], 1)
                    for j in range(RT):
                        act.wait_ge(s["a_qkv_ready"], j + 1)
                        nc.scalar.copy(qkv[0][:, 2 * j:2 * j + 2].rearrange("p a w b -> p (a w b)"),
                                       bank(j)[:, 0:6 * BLK]).then_inc(s["a_qkv_out"], 1)
                    for a in range(0, WIN, 2):
                        act.wait_ge(s["a_qkv_ready"], RT + a // 2 + 1)
                        nc.scalar.copy(qkv[1][:, a:a + 2].rearrange("p a w b -> p (a w b)"),
                                       bank(4 + a // 2)[:, 0:6 * BLK]).then_inc(s["a_qkv_out"], 1)
                    for br in range(2):
                        act.wait_ge(s["a_score_shifted"], br + 1)
                        nc.scalar.activation(score[:], score[:], ACT.Exp, scale=scale_a
                                             ).then_inc(s["a_exp_ready"], 1)
                    act.wait_ge(s["a_branch_t_ready"], 1)
                    nc.scalar.copy(brt[0][:].rearrange("p a b -> p (a b)"), bank(0, 2)[0:BLK]
                                   ).then_inc(s["a_branch_t_out"], 1)
                    act.wait_ge(s["a_branch_t_ready"], 2)
                    for a in range(WIN):
                        ins = nc.scalar.copy(
                            brt[1][:].rearrange("p f (i a r) -> p a f i r", a=WIN, r=4)[:, a],
                            bank(2, 2)[0:BLK, a * P:(a + 1) * P].rearrange("p (f i r) -> p f i r", f=2, r=4))
                    ins.then_inc(s["a_branch_t_out"], 1)
                    act.wait_ge(s["a_centered"], 1)
                    nc.scalar.activation(att2, att, ACT.Square).then_inc(s["a_sq_ready"], 1)

                @block.tensor
                def _(pe):
                    transpose_rows(pe, lambda r, kt: r[:, kt * P:(kt + 1) * P])
                    pe.wait_ge(s["xt_evacuated"], KT)
                    for j in range(RT):
                        for h in range(HALVES):
                            ins = nc.tensor.matmul(bank(j)[:, h * 3 * BLK:(h + 1) * 3 * BLK],
                                                   xt[:, h, j * P:(j + 1) * P],
                                                   bd1[:].rearrange("p w t c -> p (w t c)"), start=True, stop=True)
                        ins.then_inc(s["a_qkv_ready"], 1)
                    pe.wait_ge(s["xt_evacuated"], 2 * KT)
                    for a in range(WIN):
                        for h in range(HALVES):
                            ins = nc.tensor.matmul(bank(4 + a // 2)[64 * h:64 * h + 64,
                                                                    (a % 2) * 3 * BLK:(a % 2 + 1) * 3 * BLK],
                                                   xta[:, h, a, :], bd2[:].rearrange("p w t c -> p (w t c)"),
                                                   start=True, stop=True)
                        if a % 2:
                            ins.then_inc(s["a_qkv_ready"], 1)
                    pe.wait_ge(s["a_branch_ready"], 1)
                    pe.wait_ge(s["a_qkv_out"], RT)
                    for g in range(WG):
                        j, h = divmod(g, HALVES)
                        ins = nc.tensor.transpose(bank(h)[0:BLK, j * P:(j + 1) * P],
                                                  xbr[0][:, g].rearrange("p a b -> p (a b)"), ident)
                    ins.then_inc(s["a_branch_t_ready"], 1)
                    pe.wait_ge(s["a_branch_ready"], 2)
                    for a in range(WIN):
                        ins = nc.tensor.transpose(bank(2, 2)[0:BLK, a * P:(a + 1) * P],
                                                  xbr[1][:, a].rearrange("p a b -> p (a b)"), ident)
                    ins.then_inc(s["a_branch_t_ready"], 1)
                    pe.wait_ge(s["a_branch_t_out"], 2)
                    for j in range(RT):
                        for h in range(HALVES):
                            o = bank(4, 2)[:, (j * HALVES + h) * P:(j * HALVES + h + 1) * P]
                            for br, w in ((0, bdp1), (1, bdp2)):
                                ins = nc.tensor.matmul(o, brt[br][:, h, j * P:(j + 1) * P],
                                                       w[:].rearrange("p a b -> p (a b)"),
                                                       start=br == 0, stop=br == 1)
                    ins.then_inc(s["a_proj_ready"], 1)

                @block.vector
                def _(dve):
                    link = chain(dve, s["dve_chain"])
                    dve.wait_ge(s["x_in"], 16)
                    ln_stats(dve, link, X)
                    ln_apply(dve, link, X, 1.0)
                    for br in range(2):
                        for hf in range(2):
                            dve.wait_ge(s["a_qk_prod"], WG * br + 4 * (hf + 1))
                            ins = nc.vector.tensor_reduce(
                                score[:, 4 * hf:4 * hf + 4].rearrange("p g i j -> p (g i j)"),
                                prod[hf].rearrange("p g (s c) -> p (g s) c", c=HCH), AX.X, ALU.add)
                        link(ins)
                        s64 = score[:].rearrange("p g i j -> p (g i) j")
                        link(nc.vector.tensor_reduce(smx, s64, AX.X, ALU.max))
                        nc.vector.tensor_tensor(s64, s64, smx.unsqueeze(2).broadcast_to([P, WG * WIN, WIN]),
                                                ALU.subtract).then_inc(s["a_score_shifted"], 1)
                        dve.wait_ge(s["a_exp_ready"], br + 1)
                        link(nc.vector.tensor_reduce(ssum, s64, AX.X, ALU.add))
                        link(nc.vector.reciprocal(ssum, ssum))
                        o = window_view(xbr[br], br)
                        for hf in range(2):
                            dve.wait_ge(s["a_av_prod"], WG * br + 4 * (hf + 1))
                            for g in range(4 * hf, 4 * hf + 4):
                                ins = nc.vector.tensor_reduce(
                                    o[:, g], prod[hf][:, g % 4, :].rearrange("p (i c j) -> p i c j", c=HCH, j=WIN),
                                    AX.X, ALU.add)
                        link(ins)
                        link(nc.vector.tensor_tensor(
                            o, o, ssum.rearrange("p (g i) -> p g i", i=WIN).unsqueeze(3).broadcast_to(
                                [P, WG, WIN, HCH]), ALU.mult))
                        dve.wait_ge(s["a_lepe_ready"], br + 1)
                        nc.vector.tensor_tensor(o, o, lepe[:], ALU.add).then_inc(s["a_branch_ready"], 1)
                    dve.wait_ge(s["a_proj_ready"], 1)
                    a3 = att.rearrange("p (t c) -> p t c", c=CH)
                    full = [P, RT * CH, CH]
                    link(nc.vector.tensor_tensor(a3, bank(4, 2).rearrange("p (t c) -> p t c", c=CH),
                                                 pb_[:].unsqueeze(1).broadcast_to(full), ALU.add))
                    link(nc.vector.tensor_reduce(m16, a3, AX.X, ALU.add))
                    link(nc.vector.tensor_scalar(m16, m16, 1.0 / CH, None, ALU.mult))
                    nc.vector.tensor_tensor(a3, a3, m16.unsqueeze(2).broadcast_to(full), ALU.subtract
                                            ).then_inc(s["a_centered"], 1)
                    dve.wait_ge(s["a_sq_ready"], 1)
                    link(nc.vector.tensor_reduce(v16, att2.rearrange("p (t c) -> p t c", c=CH), AX.X, ALU.add))
                    nc.vector.tensor_scalar(v16, v16, 1.0 / CH, EPS, ALU.mult, ALU.add
                                            ).then_inc(s["var_ready"], 1)
                    dve.wait_ge(s["rstd_ready"], 2)
                    link(nc.vector.tensor_tensor(a3, a3, v16.unsqueeze(2).broadcast_to(full), ALU.mult))
                    link(nc.vector.tensor_tensor(a3, a3, lw[:].unsqueeze(1).broadcast_to(full), ALU.mult))
                    link(nc.vector.tensor_tensor(a3, a3, lb[:].unsqueeze(1).broadcast_to(full), ALU.add))
                    for j in range(RT):
                        ins = nc.vector.tensor_tensor(
                            tok.rearrange("p (j c w) -> p j w c", j=RT, c=CH)[:, j],
                            att.rearrange("p (j w c) -> p j w c", j=RT, c=CH)[:, j],
                            xn[:, j, :].rearrange("p (w c) -> p w c", c=CH), ALU.add)
                    ins.then_inc(s["a_tok_ready"], 1)
                    dve.wait_ge(s["a_back"], 16)
                    link(nc.vector.tensor_tensor(X[:].rearrange("p j w -> p (j w)"),
                                                 X[:].rearrange("p j w -> p (j w)"), att, ALU.add))
            nc.all_engine_barrier(sems_to_clear=all_signals)

        arena_at[0] = 0
        R = 3
        sq = [part([P, ROWS]) for _ in range(R)]
        cub = [part([P, ROWS]) for _ in range(R)]
        th = [part([P, ROWS]) for _ in range(R)]
        gl = [part([P, ROWS]) for _ in range(R)]
        inter = [part([P, ROWS]) for _ in range(R)]
        ih = [part([P, ROWS], f16) for _ in range(R)]
        il = [part([P, ROWS], f16) for _ in range(R)]
        yt = part([P, 2, ROWS])
        LAG = 2

        def feed_forward(b, last):
            with nc.Block() as block:
                if last:
                    @block.sync
                    def _(sp):
                        sp.wait_ge(s["f_done"], 1)
                        sp.dma_start(out[bass.ds(b, 1)].rearrange("o (j p) w -> p (o j) w", p=P), X[:]
                                     ).then_inc(s["x_out_stored"], 16)
                        sp.wait_ge(s["x_out_stored"], 16)

                @block.gpsimd
                def _(pool):
                    ln_root(pool)
                    for i in range(NCH):
                        pool.wait_ge(s["inter_hi_ready"], i + 1)
                        if i >= R:
                            pool.wait_ge(s["down_used"], i - R + 1)
                        nc.gpsimd.tensor_tensor(il[i % R], inter[i % R], ih[i % R], ALU.subtract
                                                ).then_inc(s["inter_lo_ready"], 1)

                @block.scalar
                def _(act):
                    act.wait_ge(s["xt_ready"], 1)
                    for kt in range(KT):
                        nc.scalar.copy(xh[:, kt, :], bank(6 + kt)).then_inc(s["xt_evacuated"], 1)

                    def square(i):
                        act.wait_ge(s["gate_ready"], i + 1)
                        if i >= R:
                            act.wait_ge(s["cubic_ready"], i - R + 1)
                        nc.scalar.activation(sq[i % R], bank(i % 2), ACT.Square, scale=c_sq[:, 0:1]
                                             ).then_inc(s["square_ready"], 1)

                    square(0)
                    for i in range(NCH):
                        act.wait_ge(s["cubic_ready"], i + 1)
                        if i >= R:
                            act.wait_ge(s["inter_ready"], i - R + 1)
                        nc.scalar.activation(th[i % R], cub[i % R], ACT.Tanh, scale=c_th[:, 0:1]
                                             ).then_inc(s["tanh_ready"], 1)
                        if i + 1 < NCH:
                            square(i + 1)
                        act.wait_ge(s["inter_ready"], i + 1)
                        if i >= R:
                            act.wait_ge(s["down_used"], i - R + 1)
                        nc.scalar.copy(ih[i % R], inter[i % R]).then_inc(s["inter_hi_ready"], 1)
                    act.wait_ge(s["down_ready"], 1)
                    for ht in range(KT):
                        nc.scalar.activation(yt[:, ht, :], bank(4 + ht), ACT.Copy, scale=c_dn[:, 0:1]
                                             ).then_inc(s["down_out"], 1)

                @block.tensor
                def _(pe):
                    transpose_rows(pe, lambda r, kt: r.rearrange("p (m k) -> p k m", k=KT)[:, kt])
                    pe.wait_ge(s["xt_evacuated"], KT)
                    pe.wait_ge(s["xt_lo_ready"], KT)

                    def hidden(m, i, o):
                        n = 0
                        for kt in range(KT):
                            c = kt * F + i * P
                            for w, xx in ((w_hi[m], xh), (w_hi[m], xl), (w_lo[m], xh)):
                                ins = nc.tensor.matmul(o, w[:, c:c + P], xx[:, kt, :],
                                                       start=n == 0, stop=n == 3 * KT - 1)
                                n += 1
                        return ins

                    def down(i):
                        pe.wait_ge(s["inter_lo_ready"], i + 1)
                        for ht in range(KT):
                            c = i * D + ht * P
                            for n, (w, v) in enumerate(((w_hi[2], ih), (w_hi[2], il), (w_lo[2], ih))):
                                ins = nc.tensor.matmul(bank(4 + ht), w[:, c:c + P], v[i % R],
                                                       start=i == 0 and n == 0, stop=i == NCH - 1 and n == 2)
                        ins.then_inc(s["down_used"], 1)
                        return ins

                    for i in range(NCH + LAG):
                        if i < NCH:
                            if i >= 2:
                                pe.wait_ge(s["inter_ready"], i - 1)
                            hidden(0, i, bank(i % 2)).then_inc(s["gate_ready"], 1)
                            hidden(1, i, bank(2 + i % 2)).then_inc(s["up_ready"], 1)
                        if i >= LAG:
                            down(i - LAG)
                    pe.wait_ge(s["down_used"], NCH)
                    nc.tensor.nop().then_inc(s["down_ready"], 1)
                    pe.wait_ge(s["down_out"], KT)
                    for j in range(RT):
                        for ht in range(KT):
                            ins = nc.tensor.transpose(bank(6 + j // 2)[:, (j % 2) * D + ht * P:
                                                                       (j % 2) * D + (ht + 1) * P],
                                                      yt[:, ht, j * P:(j + 1) * P], ident)
                        if j % 2:
                            ins.then_inc(s["down_t_ready"], 1)

                @block.vector
                def _(dve):
                    link = chain(dve, s["dve_chain"])
                    ln_stats(dve, link, X)
                    ln_apply(dve, link, X, 2.0 ** X_EXP)
                    for kt in range(KT):
                        dve.wait_ge(s["xt_evacuated"], kt + 1)
                        nc.vector.tensor_tensor(xl[:, kt, :], bank(6 + kt), xh[:, kt, :], ALU.subtract
                                                ).then_inc(s["xt_lo_ready"], 1)

                    def cubic(i):
                        dve.wait_ge(s["square_ready"], i + 1)
                        if i >= R:
                            dve.wait_ge(s["tanh_ready"], i - R + 1)
                        nc.vector.scalar_tensor_tensor(cub[i % R], sq[i % R], 1.0, bank(i % 2), ALU.add, ALU.mult
                                                       ).then_inc(s["cubic_ready"], 1)

                    cubic(0)
                    for i in range(NCH):
                        dve.wait_ge(s["tanh_ready"], i + 1)
                        link(nc.vector.scalar_tensor_tensor(gl[i % R], th[i % R], 1.0, bank(i % 2),
                                                            ALU.add, ALU.mult))
                        dve.wait_ge(s["up_ready"], i + 1)
                        if i >= R:
                            dve.wait_ge(s["inter_lo_ready"], i - R + 1)
                        nc.vector.scalar_tensor_tensor(inter[i % R], gl[i % R],
                                                       0.5 * 2.0 ** (I_EXP - 2 * (X_EXP + W_EXP)),
                                                       bank(2 + i % 2), ALU.mult, ALU.mult
                                                       ).then_inc(s["inter_ready"], 1)
                        if i + 1 < NCH:
                            cubic(i + 1)
                    for j in range(2):
                        dve.wait_ge(s["down_t_ready"], j + 1)
                        o = X[:, 2 * j:2 * j + 2, :].rearrange("p a b -> p (a b)")
                        link(nc.vector.tensor_tensor(o, o, bank(6 + j), ALU.add))
                    nc.vector.nop().then_inc(s["f_done"], 1)
            nc.all_engine_barrier(sems_to_clear=all_signals)

        arena_at[0] = 0
        qs = part([66, NH, ROWS], f16)
        ks = part([66, NH, ROWS], f16)
        pt = [part([P, STRIPS]) for _ in range(2)]
        qf = part([P, 4, ROWS])
        rsin = pt[1][:, 0:ROWS]
        rope = [pt[0][:, 0:ROWS], pt[0][:, ROWS:2 * ROWS]]
        rh = part([P, 4, ROWS], f16)
        rl = part([P, 4, ROWS], f16)
        ot = qf[:, 0, :]
        nmax = sb("nmax", [P, NH * RT])
        mxh = sb("mxh", [NH * RT, 2, P], f16)
        rec = sb("rec", [P, RT, 4])
        osc = sb("osc", [P, RT, 4, HD])

        def attention_b(b):
            def out_group(act, g):
                act.wait_ge(s["b_av_done"], 4 * g + 4)
                if g:
                    act.wait_ge(s["b_o_t_ready"], g)
                nc.scalar.copy(ot, bank(6 + g % 2)).then_inc(s["b_o_out"], 1)

            with nc.Block() as block:
                @block.sync
                def _(sp):
                    for which, dst, order in ((0, qs, (0, 0, 1, 1)), (1, ks, (0, 1, 0, 1))):
                        for g in range(2):
                            t = 2 * which + g
                            sp.wait_ge(s["b_hi_ready"], t + 1)
                            sp.wait_ge(s["b_lo_ready"], t + 1)
                            for c, lo in enumerate(order):
                                for n in range(HG):
                                    sp.dma_start(dst[HD * c:HD * c + HD, HG * g + n, :],
                                                 (rl if lo else rh)[HD * n:HD * n + HD, t, :]
                                                 ).then_inc(s["b_stacked"], 16)
                    for lo in range(2):
                        sp.wait_ge(s["b_max_lo"] if lo else s["b_max_hi"], 1)
                        sp.dma_start(qs[64 + lo:65 + lo].rearrange("o n (t r) -> o (n t) r", r=P),
                                     mxh[:, lo, :]).then_inc(s["b_max_in"], 16)

                @block.gpsimd
                def _(pool):
                    ln_root(pool)
                    pool.wait_ge(s["rstd_ready"], 1)
                    nc.gpsimd.memset(ks[64:66], 2.0 ** MAX_EXP).then_inc(s["zeroed"], 1)
                    pool.wait_ge(s["zeroed"], 1)
                    for t in range(4):
                        pool.wait_ge(s["b_proj_out"], t + 1)
                        pool.wait_ge(s["b_rot_ready"], t + 1)
                        nc.gpsimd.tensor_tensor(qf[:, t, :], qf[:, t, :], cos_t, ALU.mult
                                                ).then_inc(s["b_cos_ready"], 1)
                    for t in range(4):
                        pool.wait_ge(s["b_hi_ready"], t + 1)
                        nc.gpsimd.tensor_tensor(rl[:, t, :], qf[:, t, :], rh[:, t, :], ALU.subtract
                                                ).then_inc(s["b_lo_ready"], 1)

                @block.scalar
                def _(act):
                    act.wait_ge(s["xt_ready"], 1)
                    for kt in range(KT):
                        nc.scalar.copy(xt[:, kt, :], bank(6 + kt)).then_inc(s["xt_evacuated"], 1)
                    for t in range(4):
                        act.wait_ge(s["b_proj_ready"], t + 1)
                        nc.scalar.activation(qf[:, t, :], bank(t), ACT.Identity,
                                             bias=bqk[:, t // 2, t % 2:t % 2 + 1]).then_inc(s["b_proj_out"], 1)
                    for t in range(4):
                        act.wait_ge(s["b_rope_ready"], t + 1)
                        nc.scalar.copy(rh[:, t, :], qf[:, t, :]).then_inc(s["b_hi_ready"], 1)
                    act.wait_ge(s["b_max_t_ready"], 1)
                    nc.scalar.copy(mxh[:, 0, :], bank(6)[0:NH * RT, 0:P]).then_inc(s["b_max_hi"], 1)
                    for n in range(NH):
                        act.wait_ge(s["b_kq_ready"], n + 1)
                        if n >= 2:
                            act.wait_ge(s["b_av_done"], n - 1)
                        nc.scalar.activation(pt[n % 2], bank(3 * (n % 2), 3)[:, 0:STRIPS], ACT.Exp,
                                             scale=float(HD) ** -0.5).then_inc(s["b_exp_ready"], 1)
                        if n % 4 == 0 and n:
                            out_group(act, n // 4 - 1)
                    out_group(act, NH // 4 - 1)

                @block.tensor
                def _(pe):
                    transpose_rows(pe, lambda r, kt: r[:, kt * P:(kt + 1) * P])
                    pe.wait_ge(s["xt_evacuated"], KT)
                    for t in range(4):
                        for kt in range(KT):
                            ins = nc.tensor.matmul(bank(t), wqk[:, kt, t // 2, (t % 2) * P:(t % 2 + 1) * P],
                                                   xt[:, kt, :], start=kt == 0, stop=kt == KT - 1)
                        ins.then_inc(s["b_proj_ready"], 1)
                    for j in range(RT):
                        for kt in range(KT):
                            ins = nc.tensor.matmul(bank(4 + j // 2)[:, (j % 2) * D:(j % 2 + 1) * D],
                                                   xt[:, kt, j * P:(j + 1) * P], wv[:, kt, :],
                                                   start=kt == 0, stop=kt == KT - 1)
                    ins.then_inc(s["b_v_ready"], 1)
                    for t in range(4):
                        pe.wait_ge(s["b_proj_out"], t + 1)
                        nc.tensor.matmul(bank(t), rot_t, qf[:, t, :], start=True, stop=True
                                         ).then_inc(s["b_rot_ready"], 1)
                    pe.wait_ge(s["b_stacked"], 16 * 2 * 4 * NH)
                    pe.wait_ge(s["b_v_out"], 1)
                    pe.wait_ge(s["zeroed"], 1)
                    for n in range(NH):
                        if n >= 2:
                            pe.wait_ge(s["b_max_taken"], 4 * (n - 1))
                        S = bank(3 * (n % 2), 3)
                        for t, (o, w) in QK_STRIP.items():
                            nc.tensor.matmul(S[:, o:o + w], qs[0:64, n, t * P:(t + 1) * P], ks[0:64, n, 0:w],
                                             start=True, stop=False, skip_group_check=True)
                            ins = nc.tensor.matmul(S[:, o + w - P:o + w], masks[:, 0, :], masks[:, 1, :],
                                                   start=False, stop=True, skip_group_check=True)
                        ins.then_inc(s["b_qk_ready"], 1)
                    pe.wait_ge(s["b_max_scaled"], 1)
                    nc.tensor.transpose(bank(6)[0:NH * RT, 0:P], nmax[:], ident).then_inc(s["b_max_t_ready"], 1)
                    pe.wait_ge(s["b_max_in"], 32)
                    pe.wait_ge(s["b_max_lo"], 1)

                    def scores(n):
                        if n >= 2:
                            pe.wait_ge(s["b_exp_ready"], n - 1)
                        S = bank(3 * (n % 2), 3)
                        for t, (o, w) in KQ_STRIP.items():
                            nc.tensor.matmul(S[:, o:o + w], ks[0:66, n, t * P:(t + 1) * P],
                                             qs[0:66, n, t * P:ROWS], start=True, stop=False,
                                             skip_group_check=True)
                            ins = nc.tensor.matmul(S[:, o:o + P], masks[:, 0, :], masks[:, 2, :],
                                                   start=False, stop=True, skip_group_check=True)
                        ins.then_inc(s["b_kq_ready"], 1)

                    def values(n):
                        g, r = divmod(n, 4)
                        if r == 0 and g >= 2:
                            pe.wait_ge(s["b_o_added"], g - 1)
                        pe.wait_ge(s["b_exp_ready"], n + 1)
                        for t in range(RT):
                            o, w = KQ_STRIP[t]
                            ins = nc.tensor.matmul(bank(6 + g % 2)[OW * r:OW * r + OW, t * P:ROWS],
                                                   va[:, t, n, :], pt[n % 2][:, o:o + w],
                                                   start=t == 0, stop=t == RT - 1, skip_group_check=True)
                        ins.then_inc(s["b_av_done"], 1)

                    def turn(g):
                        pe.wait_ge(s["b_o_out"], g + 1)
                        for j in range(RT):
                            ins = nc.tensor.transpose(bank(6 + g % 2)[:, j * P:(j + 1) * P],
                                                      ot[:, j * P:(j + 1) * P], ident)
                        ins.then_inc(s["b_o_t_ready"], 1)

                    scores(0)
                    for n in range(NH):
                        if n + 1 < NH:
                            scores(n + 1)
                        if n % 4 == 1 and n > 4:
                            turn(n // 4 - 1)
                        values(n)
                    turn(NH // 4 - 1)

                @block.vector
                def _(dve):
                    link = chain(dve, s["dve_chain"])
                    ln_stats(dve, link, X)
                    ln_apply(dve, link, X, 1.0)
                    for t in range(4):
                        dve.wait_ge(s["b_rot_ready"], t + 1)
                        link(nc.vector.tensor_tensor(rsin, bank(t), sin_t, ALU.mult))
                        dve.wait_ge(s["b_cos_ready"], t + 1)
                        nc.vector.tensor_tensor(qf[:, t, :], qf[:, t, :], rsin, ALU.add
                                                ).then_inc(s["b_rope_ready"], 1)
                        if t == 0:
                            dve.wait_ge(s["b_v_ready"], 1)
                            for j in range(RT):
                                ins = nc.vector.tensor_tensor(
                                    va[:, j, :, 0:HD],
                                    bank(4 + j // 2)[:, (j % 2) * D:(j % 2 + 1) * D].rearrange(
                                        "p (n c) -> p n c", c=HD), bv[:], ALU.add)
                            ins.then_inc(s["b_v_out"], 1)
                        dve.wait_ge(s["b_rope_ready"], t + 1)
                    for n in range(NH):
                        dve.wait_ge(s["b_qk_ready"], n + 1)
                        for t, (o, w) in QK_STRIP.items():
                            nc.vector.tensor_reduce(nmax[:, RT * n + t:RT * n + t + 1],
                                                    bank(3 * (n % 2), 3)[:, o:o + w], AX.X, ALU.max, negate=True
                                                    ).then_inc(s["b_max_taken"], 1)
                    dve.wait_ge(s["b_max_taken"], NH * RT)
                    nc.vector.tensor_scalar(nmax[:], nmax[:], 2.0 ** -MAX_EXP, None, ALU.mult
                                            ).then_inc(s["b_max_scaled"], 1)
                    dve.wait_ge(s["b_max_hi"], 1)
                    nc.vector.tensor_tensor(mxh[:, 1, :], bank(6)[0:NH * RT, 0:P], mxh[:, 0, :], ALU.subtract
                                            ).then_inc(s["b_max_lo"], 1)
                    for g in range(NH // 4):
                        dve.wait_ge(s["b_o_t_ready"], g + 1)
                        T = bank(6 + g % 2).rearrange("p (j r c) -> p j r c", j=RT, r=4)
                        link(nc.vector.reciprocal(rec[:], T[:, :, :, HD]))
                        link(nc.vector.tensor_tensor(osc[:], T[:, :, :, 0:HD],
                                                     rec[:].unsqueeze(3).broadcast_to([P, RT, 4, HD]), ALU.mult))
                        xo = X[:, :, 4 * HD * g:4 * HD * (g + 1)].rearrange("p j (r c) -> p j r c", c=HD)
                        nc.vector.tensor_tensor(xo, xo, osc[:], ALU.add).then_inc(s["b_o_added"], 1)
            nc.all_engine_barrier(sems_to_clear=all_signals)

        with nc.Fori(0, B) as b:
            attention_a(b)
            feed_forward(b, False)
            attention_b(b)
            feed_forward(b, True)


def shape_constants():
    c = np.zeros((P, C_ALL), np.float32)
    i = np.arange(P)
    c[i, C_ID + i] = 1
    lo = i[i % HD < HD // 2]
    c[lo + HD // 2, C_ROT + lo] = -1
    c[lo, C_ROT + lo + HD // 2] = 1
    c[:, C_MQK:C_MQK + P] = np.where(i[None, :] > i[:, None], NEG, 0)
    c[:, C_MKQ:C_MKQ + P] = np.where(i[:, None] > i[None, :], NEG, 0)
    inv = (1.0 / np.float32(10000.0) ** (np.arange(0, HD, 2, dtype=np.float32) / np.float32(HD))).astype(np.float32)
    angle = (np.arange(ROWS, dtype=np.float32)[None, :] * inv[i % (HD // 2)][:, None]).astype(np.float32)
    c[:, C_COS:C_COS + ROWS] = np.cos(angle.astype(np.float64))
    c[:, C_SIN:C_SIN + ROWS] = np.sin(angle.astype(np.float64))
    return c


def kernel(**inputs):
    import concourse.bacc as bacc
    from concourse.bass_utils import run_bass_kernel_spmd

    a, f = "L0_attn_a_", "L0_ffn_"
    arrays = {n: np.ascontiguousarray(inputs[a + n]) for n in (
        "x", "qkv_w", "conv_w0", "conv_b0", "conv_w1", "conv_b1", "proj_w", "proj_b", "ln_w", "ln_b")}
    for n in ("conv_w0", "conv_w1"):
        arrays[n] = np.ascontiguousarray(arrays[n].transpose(2, 3, 1, 0))
    arrays["w_qkv_t"] = np.ascontiguousarray(np.asarray(inputs["L0_attn_b_w_qkv"]).T)
    arrays["b_qkv"] = np.ascontiguousarray(inputs["L0_attn_b_b_qkv"])
    for n in ("gate", "up", "down"):
        arrays[n + "_words"] = np.ascontiguousarray(np.asarray(inputs[f + n + "_W_packed"]).T)
        arrays[n + "_scale_t"] = np.ascontiguousarray(np.asarray(inputs[f + n + "_scales"]).T)
    arrays["consts"] = shape_constants()

    nc = bacc.Bacc("TRN2", target_bir_lowering=False, num_devices=1)
    aps = [nc.dram_tensor(f"in_{n}", v.shape, mybir.dt.from_np(v.dtype), kind="ExternalInput").ap()
           for n, v in arrays.items()]
    scratch = nc.dram_tensor("scratch", (CH, ROWS * CH), mybir.dt.float32, kind="Internal").ap()
    out = nc.dram_tensor("out_dram", (B, ROWS, D), mybir.dt.float32, kind="ExternalOutput").ap()
    program(nc, *aps, scratch, out)
    r = run_bass_kernel_spmd(nc, [{f"in_{n}": v for n, v in arrays.items()}], core_ids=[0])
    return r.results[0]["out_dram"]
```

```python
from contextlib import ExitStack

import numpy as np

import concourse.bass as bass
from concourse import mybir

P = 128
B, ROWS, D = 4, 512, 256
RT = ROWS // P
KT = D // P
CH = 16
HCH = CH // 2
WIN = 8
HALVES = D // (WIN * CH)
WG = RT * HALVES
BLK = WIN * HCH
F = 2048
NCH = F // P
QB = 32
NH, HD = 16, 16
HG = P // HD
OW = 64
PR = 3
EPS = 1e-5
NEG = -1e30

X_EXP = 11
W_EXP = 12
I_EXP = -8
MAX_EXP = 8

C_ID, C_ROT, C_MQK, C_MKQ, C_COS, C_SIN = 0, 128, 256, 384, 512, 1024
C_ALL = 1536

QK_STRIP = {3: (0, 512), 2: (512, 384), 0: (896, 128), 1: (1024, 256)}
KQ_STRIP = {0: (0, 512), 1: (512, 384), 3: (896, 128), 2: (1024, 256)}
STRIPS = 1280

MATRICES = ("gate", "up", "down")

SIGNALS = """
consts_in attn_a_weights_in attn_b_weights_in gate_words_in up_words_in down_words_in
gate_scale_in up_scale_in down_scale_in zeroed masks_cast conv_bias_ready conv_bias_projected
scale_max_ready scale_max_all words_read weight_f32_ready weight_hi_ready weight_lo_ready
x_out_stored var_ready rstd_ready xn_ready xt_ready xt_evacuated xt_lo_ready
dve_chain act_chain pool_chain
x_taken a_x_in a_var_ready a_rstd_ready a_xn_ready a_xt_ready a_xt_out a_xt_placed
a_qkv_ready a_qkv_out a_qk_ready a_qk_summed a_score_shifted a_exp_ready a_prob_ready a_xn_biased
a_av_ready a_av_summed a_branch_ready a_branch_t_ready a_branch_t_out a_proj_ready a_att_read
a_centered a_sq_ready a_var16_ready a_rstd16_ready a_tok_ready a_stored a_back
gate_ready up_ready square_ready cubic_ready tanh_ready inter_ready inter_hi_ready inter_lo_ready
down_used down_ready down_out down_t_ready f_done
b_proj_ready b_proj_out b_rot_ready b_cos_ready b_rope_ready b_hi_ready b_lo_ready
b_spilled0 b_spilled1 b_spilled2 b_spilled3 b_stacked
b_v_ready b_v_out b_vhi_ready b_vlo_ready b_qk_ready b_max_taken b_max_scaled b_max_t_ready b_max_hi b_max_lo
b_max_in0 b_max_in1 b_kq_ready b_exp_ready b_phi_ready b_plo_ready b_av_done
b_o_out b_o_t_ready b_o_added
""".split()


def program(nc, x, qkv_w, conv_w0, conv_b0, conv_w1, conv_b1, proj_w, proj_b, ln_w, ln_b,
            w_qkv_t, b_qkv, gate_words, gate_scale_t, up_words, up_scale_t, down_words, down_scale_t,
            consts, scratch, spill, out):
    f32, f16, bf16, i32 = mybir.dt.float32, mybir.dt.float16, mybir.dt.bfloat16, mybir.dt.int32
    ALU = mybir.AluOpType
    ACT = mybir.ActivationFunctionType
    AX = mybir.AxisListType

    ctx = ExitStack()
    with ctx:
        def sb(name, shape, dt=f32):
            return ctx.enter_context(nc.sbuf_tensor(name, shape, dt))

        s = {}
        for name in SIGNALS:
            s[name] = ctx.enter_context(nc.semaphore(name))
        all_signals = range(s[SIGNALS[0]].num, s[SIGNALS[-1]].num + 1)
        assert len(all_signals) == len(SIGNALS)

        con = sb("con", [P, C_ALL])
        ident = con[:, C_ID:C_ID + P]
        rot_t = con[:, C_ROT:C_ROT + P]
        cos_t = con[:, C_COS:C_COS + ROWS]
        sin_t = con[:, C_SIN:C_SIN + ROWS]
        masks = sb("masks", [P, 3, P], bf16)
        bd1 = sb("bd1", [P, 4, WIN, HCH])
        bd2 = sb("bd2", [P, 3 + 3, WIN, HCH])
        bdp1 = sb("bdp1", [BLK, WIN, CH])
        bdp2 = sb("bdp2", [BLK, WIN, CH])
        conv = sb("conv", [P, 2, 3, HCH])
        proj = sb("proj", [CH, CH])
        conv_bias = sb("conv_bias", [CH, 1])
        conv_bias_wide = sb("conv_bias_wide", [CH, P])
        pb_ = sb("pb_", [P, CH])
        lw = sb("lw", [P, CH])
        lb = sb("lb", [P, CH])
        wqk = sb("wqk", [P, KT, 2, NH * HD])
        wv = sb("wv", [P, KT, NH * HD])
        bqk = sb("bqk", [P, 2, 2])
        bv = sb("bv", [P, NH, HD])
        w_hi = [sb(f"w_hi{m}", [P, 2 * F], f16) for m in range(3)]
        w_lo = [sb(f"w_lo{m}", [P, 2 * F], f16) for m in range(3)]
        smax = sb("smax", [P, 3])
        gmax = sb("gmax", [P, 3])
        pow2 = sb("pow2", [P, 3])
        rpow2 = sb("rpow2", [P, 3])
        c_sq = sb("c_sq", [P, 1])
        c_th = sb("c_th", [P, 1])
        c_dn = sb("c_dn", [P, 1])
        half_neg = sb("half_neg", [P, 4 * CH])
        va = sb("va", [P, RT, NH, OW], f16)

        X = sb("X", [P, RT, D])
        xn = sb("xn", [P, RT, D])
        stats = sb("stats", [P, RT, 6])
        mv = sb("mv", [P, RT, 2])
        veps = sb("veps", [P, RT])
        rstd = sb("rstd", [P, RT])
        xt = sb("xt", [P, KT, ROWS])
        xh = sb("xh", [P, KT, ROWS], f16)
        xl = sb("xl", [P, KT, ROWS], f16)

        arena = sb("arena", [P, 16384])
        arena_at = [0]

        def part(shape, dt=f32):
            n = int(np.prod(shape[1:]))
            words = n if dt in (f32, i32) else n // 2
            at = arena_at[0]
            arena_at[0] = at + words
            assert arena_at[0] <= 16384
            v = arena[0:shape[0], at:at + words]
            if dt != f32:
                v = v.bitcast(dt)
            names = "abcd"[:len(shape) - 1]
            if len(names) == 1:
                return v
            return v.rearrange(f"p ({' '.join(names)}) -> p {' '.join(names)}",
                               **{k: n for k, n in zip(names, shape[1:])})

        banks = ctx.enter_context(nc.psum_tensor("banks", [P, 8, 512], f32))

        def bank(i, n=1):
            return banks[:, i:i + n, :].rearrange("p a b -> p (a b)")

        def chain(eng, sem):
            count = [0]

            def link(ins):
                count[0] += 1
                ins.then_inc(sem, 1)
                eng.wait_ge(sem, count[0])
            return link

        A_WEIGHTS = WIN * 8 + 8 + 3 + 1 + 3 * WIN - 2
        shifted = xt[:].rearrange("p a b -> p (a b)")[:, 0:3 * BLK].rearrange(
            "p (k t c) -> p k t c", k=3, c=HCH)
        words = [part([P, F], i32) for _ in range(2)]
        scale = [part([P, F]) for _ in range(2)]
        both = part([P, F], i32)
        magn = part([P, F], i32)
        wf = part([P, 2 * F])
        arena_at[0] = 0

        with nc.Block() as block:
            @block.sync
            def _(sp):
                def load_matrix(m):
                    w, sc, down = ((gate_words, gate_scale_t, False), (up_words, up_scale_t, False),
                                   (down_words, down_scale_t, True))[m]
                    words_in, scale_in = s[MATRICES[m] + "_words_in"], s[MATRICES[m] + "_scale_in"]
                    if not down:
                        sp.dma_start(words[m % 2], w).then_inc(words_in, 16)
                        sp.dma_start(scale[m % 2], sc.unsqueeze(1).broadcast_to([D // QB, QB // 2, F])
                                     ).then_inc(scale_in, 16)
                    else:
                        sp.dma_start(words[m % 2].rearrange("p (c h) -> p c h", h=D),
                                     w.rearrange("(c p) h -> p c h", p=P)).then_inc(words_in, 16)
                        for c in range(F // D):
                            sp.dma_start(scale[m % 2][:, c * D:(c + 1) * D],
                                         sc[8 * c:8 * c + 8, :].unsqueeze(1).broadcast_to([8, QB // 2, D])
                                         ).then_inc(scale_in, 16)

                load_matrix(0)
                load_matrix(1)
                sp.dma_start(con[:], consts).then_inc(s["consts_in"], 16)
                sp.wait_ge(s["zeroed"], 1)
                for t in range(WIN):
                    for which in range(3):
                        c0 = which * CH
                        sp.dma_start(bd1[CH * t:CH * t + CH, which, t, :], qkv_w[:, c0:c0 + HCH]
                                     ).then_inc(s["attn_a_weights_in"], 16)
                        sp.dma_start(bd2[CH * t:CH * t + CH, which, t, :], qkv_w[:, c0 + HCH:c0 + CH]
                                     ).then_inc(s["attn_a_weights_in"], 16)
                    sp.dma_start(bdp1[HCH * t:HCH * t + HCH, t, :], proj_w[0:HCH, :]
                                 ).then_inc(s["attn_a_weights_in"], 16)
                    sp.dma_start(bdp2[HCH * t:HCH * t + HCH, t, :], proj_w[HCH:CH, :]
                                 ).then_inc(s["attn_a_weights_in"], 16)
                for br, (cw, cb) in enumerate(((conv_w0, conv_b0), (conv_w1, conv_b1))):
                    for tap in range(3):
                        src = cw[1, tap, 0, :] if br == 0 else cw[tap, 1, 0, :]
                        sp.dma_start(conv[:, br, tap, :], src.unsqueeze(0).broadcast_to([P, HCH])
                                     ).then_inc(s["attn_a_weights_in"], 16)
                    sp.dma_start(conv_bias[HCH * br:HCH * br + HCH, :], cb.unsqueeze(1)
                                 ).then_inc(s["attn_a_weights_in"], 16)
                sp.dma_start(proj[:], proj_w).then_inc(s["attn_a_weights_in"], 16)
                for tap in range(3):
                    for t in range(max(0, 1 - tap), min(WIN, WIN + 1 - tap)):
                        u = t + tap - 1
                        sp.dma_start(shifted[CH * u:CH * u + CH, tap, t, :], qkv_w[:, 2 * CH:2 * CH + HCH]
                                     ).then_inc(s["attn_a_weights_in"], 16)
                for dst, src in ((pb_, proj_b), (lw, ln_w), (lb, ln_b)):
                    sp.dma_start(dst[:, :], src.unsqueeze(0).broadcast_to([P, CH])
                                 ).then_inc(s["attn_a_weights_in"], 16)
                for kt in range(KT):
                    rows = w_qkv_t[kt * P:(kt + 1) * P, :].rearrange("p (n w c) -> p w n c", w=3, c=HD)
                    for which in range(2):
                        sp.dma_start(wqk[:, kt, which, :].rearrange("p (n c) -> p n c", c=HD), rows[:, which]
                                     ).then_inc(s["attn_b_weights_in"], 16)
                    sp.dma_start(wv[:, kt, :].rearrange("p (n c) -> p n c", c=HD), rows[:, 2]
                                 ).then_inc(s["attn_b_weights_in"], 16)
                bias = b_qkv.rearrange("(n w c) -> w n c", w=3, c=HD)
                for which in range(2):
                    for g in range(2):
                        for n in range(HG):
                            sp.dma_start(bqk[HD * n:HD * n + HD, which, g:g + 1],
                                         bias[which, HG * g + n, :].unsqueeze(1)
                                         ).then_inc(s["attn_b_weights_in"], 16)
                for n in range(NH):
                    sp.dma_start(bv[:, n, :], bias[2, n, :].unsqueeze(0).broadcast_to([P, HD])
                                 ).then_inc(s["attn_b_weights_in"], 16)
                sp.wait_ge(s["words_read"], 1)
                sp.wait_ge(s["weight_f32_ready"], 1)
                load_matrix(2)
                sp.wait_ge(s["consts_in"], 16)
                sp.wait_ge(s["attn_a_weights_in"], 16 * A_WEIGHTS)
                sp.wait_ge(s["attn_b_weights_in"], 16 * (KT * 3 + 4 * HG + NH))

            @block.gpsimd
            def _(pool):
                link = chain(pool, s["pool_chain"])
                for t in (bd1[:], bd2[:], bdp1[:], bdp2[:], shifted):
                    nc.gpsimd.memset(t, 0.0)
                nc.gpsimd.memset(half_neg[:], -0.5)
                link(nc.gpsimd.memset(va[:], 0.0))
                nc.gpsimd.memset(va[:, :, :, 2 * HD:2 * HD + 1], 1.0).then_inc(s["zeroed"], 1)
                for m in range(3):
                    pool.wait_ge(s["scale_max_ready"], m + 1)
                    nc.gpsimd.partition_all_reduce(gmax[:, m:m + 1], smax[:, m:m + 1], P,
                                                   bass.bass_isa.ReduceOp.max).then_inc(s["scale_max_all"], 1)
                    pool.wait_ge(s["weight_hi_ready"], m + 1)
                    nc.gpsimd.tensor_tensor(w_lo[m][:], wf, w_hi[m][:], ALU.subtract
                                            ).then_inc(s["weight_lo_ready"], 1)

            @block.tensor
            def _(pe):
                pe.wait_ge(s["conv_bias_ready"], 1)
                pe.wait_ge(s["attn_a_weights_in"], 16 * A_WEIGHTS)
                nc.tensor.matmul(bank(0)[:, 0:CH], conv_bias_wide[:], proj[:], start=True, stop=True
                                 ).then_inc(s["conv_bias_projected"], 1)

            @block.scalar
            def _(act):
                for m in range(3):
                    act.wait_ge(s["weight_f32_ready"], m + 1)
                    nc.scalar.activation(w_hi[m][:], wf, ACT.Copy).then_inc(s["weight_hi_ready"], 1)

            @block.vector
            def _(dve):
                link = chain(dve, s["dve_chain"])
                dve.wait_ge(s["consts_in"], 16)
                nc.vector.tensor_copy(masks[:, 0, :], ident)
                nc.vector.tensor_copy(masks[:, 1:3, :],
                                      con[:, C_MQK:C_MQK + 2 * P].rearrange("p (a b) -> p a b", a=2)
                                      ).then_inc(s["masks_cast"], 1)
                for m in range(3):
                    w, sc = words[m % 2], scale[m % 2]
                    dve.wait_ge(s[MATRICES[m] + "_scale_in"], 16 if m < 2 else 16 * (F // D))
                    nc.vector.tensor_reduce(smax[:, m:m + 1], sc, AX.X, ALU.max,
                                            apply_absolute_value=True).then_inc(s["scale_max_ready"], 1)
                    dve.wait_ge(s[MATRICES[m] + "_words_in"], 16)
                    ins = nc.vector.scalar_tensor_tensor(both, w, 12, w, ALU.logical_shift_left, ALU.bitwise_or)
                    link(ins)
                    nc.vector.tensor_scalar(magn, both, 0x00070007, 9, ALU.bitwise_and, ALU.logical_shift_left)
                    link(nc.vector.tensor_scalar(w, both, 0x00080008, 12, ALU.bitwise_and,
                                                 ALU.logical_shift_left))
                    link(nc.vector.tensor_tensor(magn, magn, w, ALU.bitwise_or))
                    nc.vector.nop().then_inc(s["words_read"], 1)
                    dve.wait_ge(s["scale_max_all"], m + 1)
                    link(nc.vector.tensor_scalar(gmax[:, m:m + 1], gmax[:, m:m + 1], 1e-30, None, ALU.max))
                    link(nc.vector.tensor_scalar(pow2[:, m:m + 1].bitcast(i32), gmax[:, m:m + 1].bitcast(i32),
                                                 0x7F800000, None, ALU.bitwise_and))
                    link(nc.vector.reciprocal(rpow2[:, m:m + 1], pow2[:, m:m + 1]))
                    link(nc.vector.tensor_scalar(sc, sc, rpow2[:, m:m + 1], 2.0 ** (W_EXP + 14),
                                                 ALU.mult, ALU.mult))
                    if m >= 1:
                        dve.wait_ge(s["weight_lo_ready"], m)
                    val = magn.bitcast(f16)
                    for nib in range(2):
                        if m < 2:
                            o = wf[:, nib * F:(nib + 1) * F].rearrange("p (c e u) -> p c e u", e=2, u=P)
                            v = val.rearrange("p (c u e k) -> p k c e u", e=2, u=P, k=2)[:, nib]
                            g = sc.rearrange("p (c u e) -> p c e u", e=2, u=P)
                            for e in range(2):
                                ins = nc.vector.tensor_tensor(o[:, :, e], v[:, :, e], g[:, :, e], ALU.mult)
                        else:
                            o = wf.rearrange("p (c e h) -> p c e h", e=2, h=D)[:, :, nib]
                            v = val.rearrange("p (c h e) -> p e c h", e=2, h=D)[:, nib]
                            ins = nc.vector.tensor_tensor(o, v, sc.rearrange("p (c h) -> p c h", h=D), ALU.mult)
                    ins.then_inc(s["weight_f32_ready"], 1)
                dve.wait_ge(s["attn_a_weights_in"], 16 * A_WEIGHTS)
                for tap in range(3):
                    taps = [conv[:, br, tap, :].unsqueeze(1).broadcast_to([P, WIN, HCH]) for br in range(2)]
                    nc.vector.tensor_tensor(bd2[:, 3 + tap], bd2[:, 2], taps[1], ALU.mult)
                    ins = nc.vector.tensor_tensor(shifted[:, tap], shifted[:, tap], taps[0], ALU.mult)
                nc.vector.tensor_copy(conv_bias_wide[:], conv_bias[:].broadcast_to([CH, P])
                                      ).then_inc(s["conv_bias_ready"], 1)
                link(ins)
                link(nc.vector.tensor_tensor(bd1[:, 3], shifted[:, 0], shifted[:, 1], ALU.add))
                link(nc.vector.tensor_tensor(bd1[:, 3], bd1[:, 3], shifted[:, 2], ALU.add))
                dve.wait_ge(s["conv_bias_projected"], 1)
                link(nc.vector.tensor_tensor(pb_[:], pb_[:], bank(0)[:, 0:CH], ALU.add))
                back = 2.0 ** -(X_EXP + W_EXP)
                link(nc.vector.tensor_scalar(c_th[:], pow2[:, 0:1], 0.7978845608028654 * back, None, ALU.mult))
                link(nc.vector.tensor_scalar(c_sq[:], pow2[:, 0:1], 0.044715 ** 0.5 * back, None, ALU.mult))
                link(nc.vector.tensor_tensor(c_dn[:], pow2[:, 0:1], pow2[:, 1:2], ALU.mult))
                link(nc.vector.tensor_scalar(c_dn[:], c_dn[:], pow2[:, 2:3], 2.0 ** -(W_EXP + I_EXP),
                                             ALU.mult, ALU.mult))

        nc.all_engine_barrier(sems_to_clear=all_signals)

        def ln_stats(dve, link, src):
            for j in range(RT):
                ins = nc.vector.bn_stats(stats[:, j, :], src[:, j, :])
            link(ins)
            for j in range(RT):
                ins = nc.vector.bn_aggr(mv[:, j, :], stats[:, j, :])
            link(ins)
            nc.vector.tensor_scalar(veps[:], mv[:, :, 1], EPS, None, ALU.add).then_inc(s["var_ready"], 1)

        def ln_root(pool):
            pool.wait_ge(s["var_ready"], 1)
            nc.gpsimd.tensor_tensor(rstd[:], veps[:], half_neg[:, 0:RT], ALU.pow).then_inc(s["rstd_ready"], 1)

        def ln_apply(dve, link, src, factor):
            dve.wait_ge(s["rstd_ready"], 1)
            if factor != 1.0:
                link(nc.vector.tensor_scalar(rstd[:], rstd[:], factor, None, ALU.mult))
            for j in range(RT):
                nc.vector.tensor_scalar(xn[:, j, :], src[:, j, :], mv[:, j, 0:1], rstd[:, j:j + 1],
                                        ALU.subtract, ALU.mult).then_inc(s["xn_ready"], 1)

        def transpose_rows(pe, columns):
            for j in range(RT):
                pe.wait_ge(s["xn_ready"], j + 1)
                for kt in range(KT):
                    ins = nc.tensor.transpose(bank(6 + kt)[:, j * P:(j + 1) * P], columns(xn[:, j, :], kt), ident)
            ins.then_inc(s["xt_ready"], 1)

        xa = sb("xa", [P, RT, D])
        a_back = sb("a_back", [P, RT, D])
        xna = sb("xna", [P, RT, D])
        a_stats = sb("a_stats", [P, RT, 6])
        a_mv = sb("a_mv", [P, RT, 2])
        a_veps = sb("a_veps", [P, RT])
        a_rstd = sb("a_rstd", [P, RT])
        qkv = [sb(f"qkv{br}", [P, WG, 4, BLK]) for br in range(2)]
        score = [sb(f"score{br}", [P, WG, WIN, WIN]) for br in range(2)]
        smx = sb("smx", [P, WG * WIN])
        rsum = [sb(f"rsum{br}", [P, WG, WIN]) for br in range(2)]
        m16 = sb("m16", [P, RT * CH])
        v16 = sb("v16", [P, RT * CH])

        arena_at[0] = 0
        R = 3
        sq = [part([P, ROWS]) for _ in range(2)]
        cub = [part([P, ROWS]) for _ in range(2)]
        th = [part([P, ROWS]) for _ in range(2)]
        gl = [part([P, ROWS]) for _ in range(2)]
        inter = [part([P, ROWS]) for _ in range(R)]
        ih = [part([P, ROWS], f16) for _ in range(R)]
        il = [part([P, ROWS], f16) for _ in range(R)]
        yt = part([P, 2, ROWS])
        LAG = 2

        prod = part([P, WG, WIN * WIN * HCH])
        flat = prod.rearrange("p a b -> p (a b)")
        att, att2, tok = (flat[:, n * RT * D:(n + 1) * RT * D] for n in range(3))
        xbr = [part([P, WG, WIN, HCH]) for _ in range(2)]
        second_at = arena_at[0]
        xta = part([P, KT, ROWS])
        xtp = part([P, HALVES, WIN, ROWS // WIN])
        arena_at[0] = second_at
        brt = [part([BLK, HALVES, ROWS]) for _ in range(2)]

        def window_view(t, br, which=None):
            v = t[:, :, which, :] if which is not None else t.rearrange("p a b c -> p a (b c)")
            v = v.rearrange("p a (b c) -> p a b c", c=HCH)
            return v if br == 0 else v.rearrange("p a b c -> p b a c")

        A_STEPS = 16

        def a_sync(sp, stage, b, running):
            if stage == 0:
                if running:
                    sp.wait_ge(s["x_taken"], 1)
                sp.dma_start(xa[:], x[bass.ds(b, 1)].rearrange("o (j p) w -> p (o j) w", p=P)
                             ).then_inc(s["a_x_in"], 16)
                sp.wait_ge(s["a_x_in"], 16)
            else:
                sp.wait_ge(s["a_tok_ready"], 1)
                t4 = tok.rearrange("p (j c w) -> p j c w", j=RT, c=CH)
                for j in range(RT):
                    dst = scratch[:, j * P * CH:(j + 1) * P * CH].rearrange("c (p w) -> p c w", w=CH)
                    sp.dma_start(dst, t4[:, j]).then_inc(s["a_stored"], 16)
                sp.wait_ge(s["a_stored"], 16 * RT)
                sp.dma_start(a_back[:], scratch.rearrange("c (q w) -> (c q) w", w=D).rearrange(
                    "(j p) w -> p j w", p=P)).then_inc(s["a_back"], 16)
                sp.wait_ge(s["a_back"], 16)

        def a_qk_products(pool, br, gs):
            q, k = (window_view(qkv[br], br, w) for w in range(2))
            for g in gs:
                if br:
                    pool.wait_ge(s["a_qk_summed"], g // 2 + 1)
                nc.gpsimd.tensor_tensor(
                    prod[:, g, :].rearrange("p (i j c) -> p i j c", i=WIN, j=WIN),
                    q[:, g].unsqueeze(2).broadcast_to([P, WIN, WIN, HCH]),
                    k[:, g].unsqueeze(1).broadcast_to([P, WIN, WIN, HCH]), ALU.mult
                ).then_inc(s["a_qk_ready"], 1)

        def a_av_products(pool, br, gs):
            v = window_view(qkv[br], br, 2)
            for g in gs:
                if br:
                    pool.wait_ge(s["a_av_summed"], g // 2 + 1)
                nc.gpsimd.tensor_tensor(
                    prod[:, g, :].rearrange("p (i c j) -> p i c j", i=WIN, j=WIN),
                    score[br][:, g].unsqueeze(2).broadcast_to([P, WIN, HCH, WIN]),
                    v[:, g].rearrange("p j c -> p c j").unsqueeze(1).broadcast_to([P, WIN, HCH, WIN]),
                    ALU.mult).then_inc(s["a_av_ready"], 1)

        def a_gpsimd(pool, stage, i):
            if stage == 0:
                if i == 1:
                    pool.wait_ge(s["a_var_ready"], 1)
                    nc.gpsimd.tensor_tensor(a_rstd[:], a_veps[:], half_neg[:, 0:RT], ALU.pow
                                            ).then_inc(s["a_rstd_ready"], 1)
                if 6 <= i < 10:
                    pool.wait_ge(s["a_qkv_out"], 2 * (i - 6) // 2 + 1)
                    a_qk_products(pool, 0, (2 * (i - 6), 2 * (i - 6) + 1))
                if 10 <= i < 14:
                    pool.wait_ge(s["a_qkv_out"], 8)
                    a_qk_products(pool, 1, (2 * (i - 10), 2 * (i - 10) + 1))
                if i == 15:
                    pool.wait_ge(s["a_xt_ready"], 1)
                    xt3 = xna[:].rearrange("p j (t c) -> p (j t) c", c=CH)
                    nc.gpsimd.tensor_tensor(xt3, xt3, lb[:].unsqueeze(1).broadcast_to([P, RT * CH, CH]), ALU.add
                                            ).then_inc(s["a_xn_biased"], 1)
            else:
                if i < 4:
                    a_av_products(pool, 0, (2 * i, 2 * i + 1))
                if 4 <= i < 8:
                    pool.wait_ge(s["a_exp_ready"], 1)
                    a_av_products(pool, 1, (2 * (i - 4), 2 * (i - 4) + 1))
                if i == 14:
                    pool.wait_ge(s["a_var16_ready"], 1)
                    nc.gpsimd.tensor_tensor(v16[:], v16[:], half_neg[:], ALU.pow
                                            ).then_inc(s["a_rstd16_ready"], 1)

        def a_scalar(act, stage, i):
            scale_a = float(HCH) ** -0.5
            if stage == 0:
                if i == 3:
                    act.wait_ge(s["a_xt_ready"], 1)
                    for kt in range(KT):
                        nc.scalar.copy(xta[:, kt, :], bank(6 + kt)).then_inc(s["a_xt_out"], 1)
                if i == 4:
                    for kt in range(KT):
                        nc.scalar.copy(xtp[:, kt].rearrange("p a (i r) -> p a i r", r=4),
                                       bank(6 + kt).rearrange("p (i a r) -> p a i r", a=WIN, r=4)
                                       ).then_inc(s["a_xt_placed"], 1)
                if 5 <= i < 9:
                    br, n = divmod(i - 5, 2)
                    for m in range(2):
                        act.wait_ge(s["a_qkv_ready"], 2 * (i - 5) + m + 1)
                        a = 4 * n + 2 * m
                        nc.scalar.copy(qkv[br][:, a:a + 2].rearrange("p a w b -> p (a w b)"), bank(6 + m)
                                       ).then_inc(s["a_qkv_out"], 1)
                if i == 12:
                    act.wait_ge(s["a_score_shifted"], 1)
                    nc.scalar.activation(score[0][:], score[0][:], ACT.Exp, scale=scale_a
                                         ).then_inc(s["a_exp_ready"], 1)
            else:
                if i == 0:
                    nc.scalar.activation(score[1][:], score[1][:], ACT.Exp, scale=scale_a
                                         ).then_inc(s["a_exp_ready"], 1)
                if i == 6:
                    act.wait_ge(s["a_branch_t_ready"], 1)
                    nc.scalar.copy(brt[0].rearrange("p a b -> p (a b)"), bank(6, 2)[0:BLK]
                                   ).then_inc(s["a_branch_t_out"], 1)
                if i == 10:
                    act.wait_ge(s["a_branch_t_ready"], 2)
                    for m in range(2):
                        o = brt[1].rearrange("p f (i a r) -> p f a i r", a=WIN, r=4)
                        for f in range(HALVES):
                            ins = nc.scalar.copy(o[:, f, 4 * m:4 * m + 4], bank(6 + m)[0:BLK].rearrange(
                                "p (a f i r) -> p f a i r", f=2, i=16, r=4)[:, f])
                    ins.then_inc(s["a_branch_t_out"], 1)
                if i == 13:
                    act.wait_ge(s["a_centered"], 1)
                    nc.scalar.activation(att2, att, ACT.Square).then_inc(s["a_sq_ready"], 1)

        def a_tensor(pe, stage, i):
            if stage == 0:
                if i == 3:
                    pe.wait_ge(s["a_xn_ready"], 1)
                    for j in range(RT):
                        for kt in range(KT):
                            ins = nc.tensor.transpose(bank(6 + kt)[:, j * P:(j + 1) * P],
                                                      xna[:, j, kt * P:(kt + 1) * P], ident)
                    ins.then_inc(s["a_xt_ready"], 1)
                if 5 <= i < 7:
                    pe.wait_ge(s["a_xt_placed"], KT)
                    w = bd1[:].rearrange("p w t c -> p (w t c)")
                    for m in range(2):
                        j = 2 * (i - 5) + m
                        if j >= 2:
                            pe.wait_ge(s["a_qkv_out"], j - 1)
                        for h in range(HALVES):
                            ins = nc.tensor.matmul(bank(6 + m)[:, h * 4 * BLK:(h + 1) * 4 * BLK],
                                                   xta[:, h, j * P:(j + 1) * P], w, start=True, stop=True)
                        ins.then_inc(s["a_qkv_ready"], 1)
                if 7 <= i < 9:
                    w = bd2[:].rearrange("p w t c -> p (w t c)")
                    for m in range(2):
                        n = 2 * (i - 7) + m
                        pe.wait_ge(s["a_qkv_out"], 2 + n + 1)
                        for a in (2 * n, 2 * n + 1):
                            for h in range(HALVES):
                                o = bank(6 + m)[64 * h:64 * h + 64, (a % 2) * 4 * BLK:(a % 2 + 1) * 4 * BLK]
                                nc.tensor.matmul(o[:, 0:3 * BLK], xtp[:, h, a, :], w[:, 0:3 * BLK],
                                                 start=True, stop=True)
                                taps = [t for t in range(3) if 0 <= a + t - 1 < WIN]
                                for t in taps:
                                    ins = nc.tensor.matmul(o[:, 3 * BLK:4 * BLK], xtp[:, h, a + t - 1, :],
                                                           w[:, (3 + t) * BLK:(4 + t) * BLK],
                                                           start=t == taps[0], stop=t == taps[-1])
                        ins.then_inc(s["a_qkv_ready"], 1)
            else:
                if i == 6:
                    pe.wait_ge(s["a_branch_ready"], 1)
                    for g in range(WG):
                        j, h = divmod(g, HALVES)
                        ins = nc.tensor.transpose(bank(6 + h)[0:BLK, j * P:(j + 1) * P],
                                                  xbr[0][:, g].rearrange("p a b -> p (a b)"), ident)
                    ins.then_inc(s["a_branch_t_ready"], 1)
                if i == 10:
                    pe.wait_ge(s["a_branch_ready"], 2)
                    pe.wait_ge(s["a_branch_t_out"], 1)
                    for a in range(WIN):
                        ins = nc.tensor.transpose(bank(6, 2)[0:BLK, a * P:(a + 1) * P],
                                                  xbr[1][:, a].rearrange("p a b -> p (a b)"), ident)
                    ins.then_inc(s["a_branch_t_ready"], 1)
                if i == 11:
                    pe.wait_ge(s["a_branch_t_out"], 2)
                    for j in range(RT):
                        for h in range(HALVES):
                            o = bank(6, 2)[:, (j * HALVES + h) * P:(j * HALVES + h + 1) * P]
                            for br, w in ((0, bdp1), (1, bdp2)):
                                ins = nc.tensor.matmul(o, brt[br][:, h, j * P:(j + 1) * P],
                                                       w[:].rearrange("p a b -> p (a b)"),
                                                       start=br == 0, stop=br == 1)
                        if j % 2:
                            ins.then_inc(s["a_proj_ready"], 1)

        def a_qk_sums(dve, link, br, n):
            dve.wait_ge(s["a_qk_ready"], WG * br + 2 * n + 2)
            nc.vector.tensor_reduce(score[br][:, 2 * n:2 * n + 2].rearrange("p g i j -> p (g i j)"),
                                    prod[:, 2 * n:2 * n + 2].rearrange("p g (s c) -> p (g s) c", c=HCH),
                                    AX.X, ALU.add).then_inc(s["a_qk_summed"], 1)

        def a_score_shift(dve, link, br):
            dve.wait_ge(s["a_qk_summed"], 4 * (br + 1))
            s64 = score[br][:].rearrange("p g i j -> p (g i) j")
            link(nc.vector.tensor_reduce(smx[:], s64, AX.X, ALU.max))
            nc.vector.tensor_tensor(s64, s64, smx[:].unsqueeze(2).broadcast_to([P, WG * WIN, WIN]),
                                    ALU.subtract).then_inc(s["a_score_shifted"], 1)

        def a_prob_sums(dve, link, br):
            dve.wait_ge(s["a_exp_ready"], 1)
            r = rsum[br][:].rearrange("p g i -> p (g i)")
            link(nc.vector.tensor_reduce(r, score[br][:].rearrange("p g i j -> p (g i) j"), AX.X, ALU.add))
            link(nc.vector.reciprocal(r, r))

        def a_av_sums(dve, link, br, n):
            o = window_view(xbr[br], br)
            dve.wait_ge(s["a_av_ready"], WG * br + 2 * n + 2)
            for g in (2 * n, 2 * n + 1):
                ins = nc.vector.tensor_reduce(
                    o[:, g], prod[:, g, :].rearrange("p (i c j) -> p i c j", c=HCH, j=WIN), AX.X, ALU.add)
            ins.then_inc(s["a_av_summed"], 1)

        def a_branch_end(dve, link, br):
            o = window_view(xbr[br], br)
            dve.wait_ge(s["a_av_summed"], 4 * (br + 1))
            link(nc.vector.tensor_tensor(o, o, rsum[br][:].unsqueeze(3).broadcast_to([P, WG, WIN, HCH]), ALU.mult))
            nc.vector.tensor_tensor(o, o, window_view(qkv[br], br, 3), ALU.add).then_inc(s["a_branch_ready"], 1)

        def a_vector(dve, link, stage, i):
            full = [P, RT * CH, CH]
            a3 = att.rearrange("p (t c) -> p t c", c=CH)
            if stage == 0:
                if i == 0:
                    dve.wait_ge(s["a_x_in"], 16)
                    for j in range(RT):
                        ins = nc.vector.bn_stats(a_stats[:, j, :], xa[:, j, :])
                    link(ins)
                    for j in range(RT):
                        ins = nc.vector.bn_aggr(a_mv[:, j, :], a_stats[:, j, :])
                    link(ins)
                    nc.vector.tensor_scalar(a_veps[:], a_mv[:, :, 1], EPS, None, ALU.add
                                            ).then_inc(s["a_var_ready"], 1)
                if i == 2:
                    dve.wait_ge(s["a_rstd_ready"], 1)
                    for j in range(RT):
                        ins = nc.vector.tensor_scalar(xna[:, j, :], xa[:, j, :], a_mv[:, j, 0:1],
                                                      a_rstd[:, j:j + 1], ALU.subtract, ALU.mult)
                    ins.then_inc(s["a_xn_ready"], 1)
                if 7 <= i < 11:
                    a_qk_sums(dve, link, 0, i - 7)
                if i == 11:
                    a_score_shift(dve, link, 0)
                if i == 13:
                    a_prob_sums(dve, link, 0)
                if 11 <= i < 15:
                    a_qk_sums(dve, link, 1, i - 11)
                if i == 15:
                    a_score_shift(dve, link, 1)
            else:
                if i == 1:
                    a_prob_sums(dve, link, 1)
                if 1 <= i < 5:
                    a_av_sums(dve, link, 0, i - 1)
                if i == 5:
                    a_branch_end(dve, link, 0)
                if 5 <= i < 9:
                    a_av_sums(dve, link, 1, i - 5)
                if i == 9:
                    a_branch_end(dve, link, 1)
                if i == 12:
                    for m in range(2):
                        dve.wait_ge(s["a_proj_ready"], 2)
                        ins = nc.vector.tensor_tensor(
                            a3[:, 32 * m:32 * m + 32], bank(6 + m).rearrange("p (t c) -> p t c", c=CH),
                            pb_[:].unsqueeze(1).broadcast_to([P, 32, CH]), ALU.add)
                    ins.then_inc(s["a_att_read"], 1)
                    dve.wait_ge(s["a_att_read"], 1)
                    link(nc.vector.tensor_reduce(m16[:], a3, AX.X, ALU.add))
                if i == 13:
                    link(nc.vector.tensor_scalar(m16[:], m16[:], 1.0 / CH, None, ALU.mult))
                    nc.vector.tensor_tensor(a3, a3, m16[:].unsqueeze(2).broadcast_to(full), ALU.subtract
                                            ).then_inc(s["a_centered"], 1)
                if i == 14:
                    dve.wait_ge(s["a_sq_ready"], 1)
                    link(nc.vector.tensor_reduce(v16[:], att2.rearrange("p (t c) -> p t c", c=CH), AX.X, ALU.add))
                    nc.vector.tensor_scalar(v16[:], v16[:], 1.0 / CH, EPS, ALU.mult, ALU.add
                                            ).then_inc(s["a_var16_ready"], 1)
                    link(nc.vector.tensor_tensor(a3, a3, lw[:].unsqueeze(1).broadcast_to(full), ALU.mult))
                if i == 15:
                    dve.wait_ge(s["a_rstd16_ready"], 1)
                    link(nc.vector.tensor_tensor(a3, a3, v16[:].unsqueeze(2).broadcast_to(full), ALU.mult))
                    for j in range(RT):
                        ins = nc.vector.tensor_tensor(
                            tok.rearrange("p (j c w) -> p j w c", j=RT, c=CH)[:, j],
                            att.rearrange("p (j w c) -> p j w c", j=RT, c=CH)[:, j],
                            xna[:, j, :].rearrange("p (w c) -> p w c", c=CH), ALU.add)
                    ins.then_inc(s["a_tok_ready"], 1)

        def attention_a_alone(b):
            for stage in range(2):
                with nc.Block() as block:
                    @block.sync
                    def _(sp):
                        a_sync(sp, stage, b, False)

                    @block.gpsimd
                    def _(pool):
                        for i in range(A_STEPS):
                            a_gpsimd(pool, stage, i)

                    @block.scalar
                    def _(act):
                        for i in range(A_STEPS):
                            a_scalar(act, stage, i)

                    @block.tensor
                    def _(pe):
                        for i in range(A_STEPS):
                            a_tensor(pe, stage, i)

                    @block.vector
                    def _(dve):
                        link = chain(dve, s["dve_chain"])
                        for i in range(A_STEPS):
                            a_vector(dve, link, stage, i)
                nc.all_engine_barrier(sems_to_clear=all_signals)

        def feed_forward(b, stage, next_b):
            last = stage == 1
            side = next_b is not None
            with nc.Block() as block:
                @block.sync
                def _(sp):
                    if side:
                        a_sync(sp, stage, next_b, True)
                    if last:
                        sp.wait_ge(s["f_done"], 1)
                        sp.dma_start(out[bass.ds(b, 1)].rearrange("o (j p) w -> p (o j) w", p=P), X[:]
                                     ).then_inc(s["x_out_stored"], 16)
                        sp.wait_ge(s["x_out_stored"], 16)

                @block.gpsimd
                def _(pool):
                    ln_root(pool)
                    for i in range(NCH):
                        pool.wait_ge(s["inter_hi_ready"], i + 1)
                        if i >= R:
                            pool.wait_ge(s["down_used"], i - R + 1)
                        nc.gpsimd.tensor_tensor(il[i % R], inter[i % R], ih[i % R], ALU.subtract
                                                ).then_inc(s["inter_lo_ready"], 1)
                        if side:
                            a_gpsimd(pool, stage, i)

                @block.scalar
                def _(act):
                    act.wait_ge(s["xt_ready"], 1)
                    for kt in range(KT):
                        nc.scalar.copy(xh[:, kt, :], bank(6 + kt)).then_inc(s["xt_evacuated"], 1)

                    def square(i):
                        act.wait_ge(s["gate_ready"], i + 1)
                        if i >= 2:
                            act.wait_ge(s["cubic_ready"], i - 1)
                        nc.scalar.activation(sq[i % 2], bank(i % 2), ACT.Square, scale=c_sq[:, 0:1]
                                             ).then_inc(s["square_ready"], 1)

                    square(0)
                    for i in range(NCH):
                        act.wait_ge(s["cubic_ready"], i + 1)
                        if i >= 2:
                            act.wait_ge(s["inter_ready"], i - 1)
                        nc.scalar.activation(th[i % 2], cub[i % 2], ACT.Tanh, scale=c_th[:, 0:1]
                                             ).then_inc(s["tanh_ready"], 1)
                        if i + 1 < NCH:
                            square(i + 1)
                        act.wait_ge(s["inter_ready"], i + 1)
                        if i >= R:
                            act.wait_ge(s["down_used"], i - R + 1)
                        nc.scalar.copy(ih[i % R], inter[i % R]).then_inc(s["inter_hi_ready"], 1)
                        if side:
                            a_scalar(act, stage, i)
                    act.wait_ge(s["down_used"], NCH)
                    for ht in range(KT):
                        nc.scalar.activation(yt[:, ht, :], bank(4 + ht), ACT.Copy, scale=c_dn[:, 0:1]
                                             ).then_inc(s["down_out"], 1)

                @block.tensor
                def _(pe):
                    transpose_rows(pe, lambda r, kt: r.rearrange("p (m k) -> p k m", k=KT)[:, kt])
                    pe.wait_ge(s["xt_evacuated"], KT)
                    pe.wait_ge(s["xt_lo_ready"], KT)

                    def hidden(m, i, o):
                        n = 0
                        for kt in range(KT):
                            c = kt * F + i * P
                            for w, xx in ((w_hi[m], xh), (w_hi[m], xl), (w_lo[m], xh)):
                                ins = nc.tensor.matmul(o, w[:, c:c + P], xx[:, kt, :],
                                                       start=n == 0, stop=n == 3 * KT - 1)
                                n += 1
                        return ins

                    def down(i):
                        pe.wait_ge(s["inter_lo_ready"], i + 1)
                        for ht in range(KT):
                            c = i * D + ht * P
                            for n, (w, v) in enumerate(((w_hi[2], ih), (w_hi[2], il), (w_lo[2], ih))):
                                ins = nc.tensor.matmul(bank(4 + ht), w[:, c:c + P], v[i % R],
                                                       start=i == 0 and n == 0, stop=i == NCH - 1 and n == 2)
                        ins.then_inc(s["down_used"], 1)

                    for i in range(NCH + LAG):
                        if i < NCH:
                            if i >= 2:
                                pe.wait_ge(s["inter_ready"], i - 1)
                            hidden(0, i, bank(i % 2)).then_inc(s["gate_ready"], 1)
                            hidden(1, i, bank(2 + i % 2)).then_inc(s["up_ready"], 1)
                        if i >= LAG:
                            down(i - LAG)
                        if side and i < A_STEPS:
                            a_tensor(pe, stage, i)
                    if side and stage == 1:
                        pe.wait_ge(s["a_att_read"], 1)
                    pe.wait_ge(s["down_out"], KT)
                    for j in range(RT):
                        for ht in range(KT):
                            ins = nc.tensor.transpose(bank(6 + j // 2)[:, (j % 2) * D + ht * P:
                                                                       (j % 2) * D + (ht + 1) * P],
                                                      yt[:, ht, j * P:(j + 1) * P], ident)
                        if j % 2:
                            ins.then_inc(s["down_t_ready"], 1)

                @block.vector
                def _(dve):
                    link = chain(dve, s["dve_chain"])
                    if stage == 0:
                        link(nc.vector.tensor_tensor(X[:], xa[:], a_back[:], ALU.add))
                        nc.vector.nop().then_inc(s["x_taken"], 1)
                    ln_stats(dve, link, X)
                    ln_apply(dve, link, X, 2.0 ** X_EXP)
                    for kt in range(KT):
                        dve.wait_ge(s["xt_evacuated"], kt + 1)
                        nc.vector.tensor_tensor(xl[:, kt, :], bank(6 + kt), xh[:, kt, :], ALU.subtract
                                                ).then_inc(s["xt_lo_ready"], 1)

                    def cubic(i):
                        dve.wait_ge(s["square_ready"], i + 1)
                        if i >= 2:
                            dve.wait_ge(s["tanh_ready"], i - 1)
                        nc.vector.scalar_tensor_tensor(cub[i % 2], sq[i % 2], 1.0, bank(i % 2), ALU.add, ALU.mult
                                                       ).then_inc(s["cubic_ready"], 1)

                    cubic(0)
                    for i in range(NCH):
                        dve.wait_ge(s["tanh_ready"], i + 1)
                        link(nc.vector.scalar_tensor_tensor(gl[i % 2], th[i % 2], 1.0, bank(i % 2),
                                                            ALU.add, ALU.mult))
                        dve.wait_ge(s["up_ready"], i + 1)
                        if i >= R:
                            dve.wait_ge(s["inter_lo_ready"], i - R + 1)
                        nc.vector.scalar_tensor_tensor(inter[i % R], gl[i % 2],
                                                       0.5 * 2.0 ** (I_EXP - 2 * (X_EXP + W_EXP)),
                                                       bank(2 + i % 2), ALU.mult, ALU.mult
                                                       ).then_inc(s["inter_ready"], 1)
                        if i + 1 < NCH:
                            cubic(i + 1)
                        if side:
                            a_vector(dve, link, stage, i)
                    for j in range(2):
                        dve.wait_ge(s["down_t_ready"], j + 1)
                        o = X[:, 2 * j:2 * j + 2, :].rearrange("p a b -> p (a b)")
                        ins = nc.vector.tensor_tensor(o, o, bank(6 + j), ALU.add)
                    ins.then_inc(s["f_done"], 1)
            nc.all_engine_barrier(sems_to_clear=all_signals)

        arena_at[0] = 0
        qs = part([66, NH, ROWS], f16)
        ks = part([66, NH, ROWS], f16)
        heads_at = arena_at[0]
        qf = part([P, 4, ROWS])
        rsin = part([P, ROWS])
        rh = part([P, 4, ROWS], f16)
        rl = part([P, 4, ROWS], f16)
        arena_at[0] = heads_at
        pt = [part([P, STRIPS]) for _ in range(2)]
        ph = [part([P, STRIPS], f16) for _ in range(PR)]
        pl = [part([P, STRIPS], f16) for _ in range(PR)]
        ot = [part([P, ROWS]) for _ in range(2)]
        vf = xn[:].rearrange("p j (n c) -> p j n c", c=HD)
        nmax = sb("nmax", [P, NH * RT])
        mxh = sb("mxh", [2 * RT, 2, 2, P], f16)
        rec = sb("rec", [P, RT, 2])
        osc = sb("osc", [P, RT, 2, HD])
        max_bank = 2
        steps = NH + 4

        def attention_b():
            with nc.Block() as block:
                @block.sync
                def _(sp):
                    for t in range(4):
                        spilled = s[f"b_spilled{t}"]
                        for lo, src, ready in ((0, rh, "b_hi_ready"), (1, rl, "b_lo_ready")):
                            sp.wait_ge(s[ready], t + 1)
                            sp.dma_start(spill[t, lo], src[:, t, :]).then_inc(spilled, 16)
                    for t in range(4):
                        which, g = divmod(t, 2)
                        dst, order = ((qs, (0, 0, 1, 1)), (ks, (0, 1, 0, 1)))[which]
                        sp.wait_ge(s[f"b_spilled{t}"], 32)
                        for c, lo in enumerate(order):
                            sp.dma_start(dst[HD * c:HD * c + HD, HG * g:HG * g + HG, :],
                                         spill[t, lo].rearrange("(n c) r -> c n r", c=HD)
                                         ).then_inc(s["b_stacked"], 16)
                    for q in range(NH // 2):
                        max_in = s[f"b_max_in{q % 2}"]
                        if q >= 2:
                            sp.wait_ge(max_in, 32 * (q // 2))
                        for lo in range(2):
                            sp.wait_ge(s["b_max_lo"] if lo else s["b_max_hi"], q + 1)
                            sp.dma_start(qs[64 + lo:65 + lo, 2 * q:2 * q + 2, :].rearrange(
                                "o n (t r) -> o (n t) r", r=P), mxh[:, q % 2, lo, :]).then_inc(max_in, 16)

                @block.gpsimd
                def _(pool):
                    ln_root(pool)
                    pool.wait_ge(s["rstd_ready"], 1)
                    nc.gpsimd.memset(ks[64:66], 2.0 ** MAX_EXP).then_inc(s["zeroed"], 1)
                    pool.wait_ge(s["zeroed"], 1)
                    for t in range(4):
                        pool.wait_ge(s["b_rot_ready"], t + 1)
                        nc.gpsimd.tensor_tensor(qf[:, t, :], qf[:, t, :], cos_t, ALU.mult
                                                ).then_inc(s["b_cos_ready"], 1)
                    for t in range(4):
                        pool.wait_ge(s["b_hi_ready"], t + 1)
                        nc.gpsimd.tensor_tensor(rl[:, t, :], qf[:, t, :], rh[:, t, :], ALU.subtract
                                                ).then_inc(s["b_lo_ready"], 1)
                    for n in range(NH):
                        pool.wait_ge(s["b_phi_ready"], n + 1)
                        if n >= PR:
                            pool.wait_ge(s["b_av_done"], n - PR + 1)
                        nc.gpsimd.tensor_tensor(pl[n % PR], pt[n % 2], ph[n % PR], ALU.subtract
                                                ).then_inc(s["b_plo_ready"], 1)

                @block.scalar
                def _(act):
                    act.wait_ge(s["xt_ready"], 1)
                    for kt in range(KT):
                        nc.scalar.copy(xt[:, kt, :], bank(6 + kt)).then_inc(s["xt_evacuated"], 1)
                    for t in range(4):
                        act.wait_ge(s["b_proj_ready"], t + 1)
                        nc.scalar.activation(qf[:, t, :], bank(t), ACT.Identity,
                                             bias=bqk[:, t // 2, t % 2:t % 2 + 1]).then_inc(s["b_proj_out"], 1)
                    for t in range(4):
                        act.wait_ge(s["b_rope_ready"], t + 1)
                        nc.scalar.copy(rh[:, t, :], qf[:, t, :]).then_inc(s["b_hi_ready"], 1)
                    act.wait_ge(s["b_v_out"], 1)
                    nc.scalar.copy(va[:, :, :, 0:HD], vf).then_inc(s["b_vhi_ready"], 1)

                    def max_hi(q):
                        act.wait_ge(s["b_max_t_ready"], q + 1)
                        if q >= 2:
                            act.wait_ge(s[f"b_max_in{q % 2}"], 32 * (q // 2))
                        nc.scalar.copy(mxh[:, q % 2, 0, :], bank(max_bank)[0:2 * RT, 256:256 + P]
                                       ).then_inc(s["b_max_hi"], 1)

                    max_hi(0)
                    max_hi(1)
                    for n in range(steps):
                        if n < NH:
                            act.wait_ge(s["b_kq_ready"], n + 1)
                            if n >= 2:
                                act.wait_ge(s["b_plo_ready"], n - 1)
                            nc.scalar.activation(pt[n % 2], bank(3, 3)[:, 0:STRIPS], ACT.Exp,
                                                 scale=float(HD) ** -0.5).then_inc(s["b_exp_ready"], 1)
                        if n % 2 == 0 and 2 <= n and n // 2 + 1 < NH // 2:
                            max_hi(n // 2 + 1)
                        if n % 2 == 0 and n >= 4:
                            p = (n - 4) // 2
                            act.wait_ge(s["b_av_done"], 2 * p + 2)
                            if p >= 2:
                                act.wait_ge(s["b_o_t_ready"], p - 1)
                            if p < NH // 2:
                                nc.scalar.copy(ot[p % 2], bank(6 + p % 2)).then_inc(s["b_o_out"], 1)

                @block.tensor
                def _(pe):
                    transpose_rows(pe, lambda r, kt: r[:, kt * P:(kt + 1) * P])
                    pe.wait_ge(s["xt_evacuated"], KT)
                    for t in range(4):
                        for kt in range(KT):
                            ins = nc.tensor.matmul(bank(t), wqk[:, kt, t // 2, (t % 2) * P:(t % 2 + 1) * P],
                                                   xt[:, kt, :], start=kt == 0, stop=kt == KT - 1)
                        ins.then_inc(s["b_proj_ready"], 1)
                    for t in range(4):
                        pe.wait_ge(s["b_proj_out"], t + 1)
                        nc.tensor.matmul(bank(t), rot_t, qf[:, t, :], start=True, stop=True
                                         ).then_inc(s["b_rot_ready"], 1)
                    for j in range(RT):
                        for kt in range(KT):
                            ins = nc.tensor.matmul(bank(4 + j // 2)[:, (j % 2) * D:(j % 2 + 1) * D],
                                                   xt[:, kt, j * P:(j + 1) * P], wv[:, kt, :],
                                                   start=kt == 0, stop=kt == KT - 1)
                    ins.then_inc(s["b_v_ready"], 1)
                    pe.wait_ge(s["b_stacked"], 16 * 16)
                    pe.wait_ge(s["b_rope_ready"], 4)
                    pe.wait_ge(s["b_v_out"], 1)
                    pe.wait_ge(s["zeroed"], 1)

                    def row_scores(n, turned):
                        if n >= 1:
                            pe.wait_ge(s["b_max_taken"], 4 * n)
                        S = bank(0, 3)
                        for t, (o, w) in QK_STRIP.items():
                            if o >= 1024 and turned:
                                pe.wait_ge(s["b_max_lo"], turned)
                            nc.tensor.matmul(S[:, o:o + w], qs[0:64, n, t * P:(t + 1) * P], ks[0:64, n, 0:w],
                                             start=True, stop=False, skip_group_check=True)
                            ins = nc.tensor.matmul(S[:, o + w - P:o + w], masks[:, 0, :], masks[:, 1, :],
                                                   start=False, stop=True, skip_group_check=True)
                        ins.then_inc(s["b_qk_ready"], 1)

                    def max_turn(q):
                        pe.wait_ge(s["b_max_scaled"], q + 1)
                        if q:
                            pe.wait_ge(s["b_max_lo"], q)
                        nc.tensor.transpose(bank(max_bank)[0:2 * RT, 256:256 + P],
                                            nmax[:, 2 * RT * q:2 * RT * (q + 1)], ident
                                            ).then_inc(s["b_max_t_ready"], 1)

                    def column_scores(n):
                        if n % 2 == 0:
                            pe.wait_ge(s[f"b_max_in{n // 2 % 2}"], 32 * (n // 4 + 1))
                        if n >= 1:
                            pe.wait_ge(s["b_exp_ready"], n)
                        S = bank(3, 3)
                        for t, (o, w) in KQ_STRIP.items():
                            nc.tensor.matmul(S[:, o:o + w], ks[0:66, n, t * P:(t + 1) * P],
                                             qs[0:66, n, t * P:ROWS], start=True, stop=False,
                                             skip_group_check=True)
                            ins = nc.tensor.matmul(S[:, o:o + P], masks[:, 0, :], masks[:, 2, :],
                                                   start=False, stop=True, skip_group_check=True)
                        ins.then_inc(s["b_kq_ready"], 1)

                    def values(n):
                        p, r = divmod(n, 2)
                        if r == 0 and p >= 2:
                            pe.wait_ge(s["b_o_added"], p - 1)
                        pe.wait_ge(s["b_plo_ready"], n + 1)
                        for t in range(RT):
                            o, w = KQ_STRIP[t]
                            for x, part_ in enumerate((ph, pl)):
                                ins = nc.tensor.matmul(bank(6 + p % 2)[OW * r:OW * r + OW, t * P:ROWS],
                                                       va[:, t, n, :], part_[n % PR][:, o:o + w],
                                                       start=t == 0 and x == 0, stop=t == RT - 1 and x == 1,
                                                       skip_group_check=True)
                        ins.then_inc(s["b_av_done"], 1)

                    def turn(p):
                        pe.wait_ge(s["b_o_out"], p + 1)
                        for j in range(RT):
                            ins = nc.tensor.transpose(bank(6 + p % 2)[:, j * P:(j + 1) * P],
                                                      ot[p % 2][:, j * P:(j + 1) * P], ident)
                        ins.then_inc(s["b_o_t_ready"], 1)

                    row_scores(0, 0)
                    row_scores(1, 0)
                    max_turn(0)
                    row_scores(2, 1)
                    row_scores(3, 1)
                    max_turn(1)
                    pe.wait_ge(s["b_vlo_ready"], 1)
                    for n in range(steps):
                        if n < NH:
                            column_scores(n)
                        if n % 2 == 0 and 2 <= n and n // 2 + 1 < NH // 2:
                            max_turn(n // 2 + 1)
                        if n + 4 < NH:
                            row_scores(n + 4, n // 2 + 2)
                        if n % 2 and n >= 5:
                            turn((n - 5) // 2)
                        if 0 <= n - 2 < NH:
                            values(n - 2)

                @block.vector
                def _(dve):
                    link = chain(dve, s["dve_chain"])
                    ln_stats(dve, link, X)
                    ln_apply(dve, link, X, 1.0)
                    for t in range(4):
                        dve.wait_ge(s["b_rot_ready"], t + 1)
                        link(nc.vector.tensor_tensor(rsin, bank(t), sin_t, ALU.mult))
                        dve.wait_ge(s["b_cos_ready"], t + 1)
                        nc.vector.tensor_tensor(qf[:, t, :], qf[:, t, :], rsin, ALU.add
                                                ).then_inc(s["b_rope_ready"], 1)
                        dve.wait_ge(s["b_rope_ready"], t + 1)
                    dve.wait_ge(s["b_v_ready"], 1)
                    for j in range(RT):
                        ins = nc.vector.tensor_tensor(
                            vf[:, j],
                            bank(4 + j // 2)[:, (j % 2) * D:(j % 2 + 1) * D].rearrange(
                                "p (n c) -> p n c", c=HD), bv[:], ALU.add)
                    ins.then_inc(s["b_v_out"], 1)
                    dve.wait_ge(s["b_vhi_ready"], 1)
                    nc.vector.tensor_tensor(va[:, :, :, HD:2 * HD], vf, va[:, :, :, 0:HD], ALU.subtract
                                            ).then_inc(s["b_vlo_ready"], 1)

                    def maxima(n):
                        dve.wait_ge(s["b_qk_ready"], n + 1)
                        for t, (o, w) in QK_STRIP.items():
                            nc.vector.tensor_reduce(nmax[:, RT * n + t:RT * n + t + 1],
                                                    bank(0, 3)[:, o:o + w], AX.X, ALU.max, negate=True
                                                    ).then_inc(s["b_max_taken"], 1)
                        if n % 2:
                            m = nmax[:, RT * (n - 1):RT * (n + 1)]
                            dve.wait_ge(s["b_max_taken"], RT * (n + 1))
                            nc.vector.tensor_scalar(m, m, 2.0 ** -MAX_EXP, None, ALU.mult
                                                    ).then_inc(s["b_max_scaled"], 1)

                    def max_lo(q):
                        dve.wait_ge(s["b_max_hi"], q + 1)
                        if q >= 2:
                            dve.wait_ge(s[f"b_max_in{q % 2}"], 32 * (q // 2))
                        nc.vector.tensor_tensor(mxh[:, q % 2, 1, :], bank(max_bank)[0:2 * RT, 256:256 + P],
                                                mxh[:, q % 2, 0, :], ALU.subtract).then_inc(s["b_max_lo"], 1)

                    maxima(0)
                    maxima(1)
                    max_lo(0)
                    maxima(2)
                    maxima(3)
                    max_lo(1)
                    for n in range(steps):
                        if n % 2 == 0 and 2 <= n and n // 2 + 1 < NH // 2:
                            max_lo(n // 2 + 1)
                        if n + 4 < NH:
                            maxima(n + 4)
                        if n < NH:
                            dve.wait_ge(s["b_exp_ready"], n + 1)
                            if n >= PR:
                                dve.wait_ge(s["b_av_done"], n - PR + 1)
                            nc.vector.tensor_copy(ph[n % PR], pt[n % 2]).then_inc(s["b_phi_ready"], 1)
                        if n % 2 and n >= 5:
                            p = (n - 5) // 2
                            dve.wait_ge(s["b_o_t_ready"], p + 1)
                            T = bank(6 + p % 2).rearrange("p (j r c) -> p j r c", j=RT, r=2)
                            nc.vector.reciprocal(rec[:], T[:, :, :, 2 * HD])
                            link(nc.vector.tensor_copy(osc[:], T[:, :, :, 0:HD]))
                            link(nc.vector.tensor_tensor(osc[:], osc[:], T[:, :, :, HD:2 * HD], ALU.add))
                            link(nc.vector.tensor_tensor(osc[:], osc[:],
                                                         rec[:].unsqueeze(3).broadcast_to([P, RT, 2, HD]),
                                                         ALU.mult))
                            xo = X[:, :, 2 * HD * p:2 * HD * (p + 1)].rearrange("p j (r c) -> p j r c", c=HD)
                            nc.vector.tensor_tensor(xo, xo, osc[:], ALU.add).then_inc(s["b_o_added"], 1)
                            dve.wait_ge(s["b_o_added"], p + 1)
            nc.all_engine_barrier(sems_to_clear=all_signals)

        attention_a_alone(0)
        with nc.Fori(0, B - 1) as b:
            feed_forward(None, 0, b + 1)
            attention_b()
            feed_forward(b, 1, b + 1)
        feed_forward(None, 0, None)
        attention_b()
        feed_forward(B - 1, 1, None)


def shape_constants():
    c = np.zeros((P, C_ALL), np.float32)
    i = np.arange(P)
    c[i, C_ID + i] = 1
    lo = i[i % HD < HD // 2]
    c[lo + HD // 2, C_ROT + lo] = -1
    c[lo, C_ROT + lo + HD // 2] = 1
    c[:, C_MQK:C_MQK + P] = np.where(i[None, :] > i[:, None], NEG, 0)
    c[:, C_MKQ:C_MKQ + P] = np.where(i[:, None] > i[None, :], NEG, 0)
    inv = (1.0 / np.float32(10000.0) ** (np.arange(0, HD, 2, dtype=np.float32) / np.float32(HD))).astype(np.float32)
    angle = (np.arange(ROWS, dtype=np.float32)[None, :] * inv[i % (HD // 2)][:, None]).astype(np.float32)
    c[:, C_COS:C_COS + ROWS] = np.cos(angle.astype(np.float64))
    c[:, C_SIN:C_SIN + ROWS] = np.sin(angle.astype(np.float64))
    return c


def kernel(**inputs):
    import concourse.bacc as bacc
    from concourse.bass_utils import run_bass_kernel_spmd

    a, f = "L0_attn_a_", "L0_ffn_"
    arrays = {n: np.ascontiguousarray(inputs[a + n]) for n in (
        "x", "qkv_w", "conv_w0", "conv_b0", "conv_w1", "conv_b1", "proj_w", "proj_b", "ln_w", "ln_b")}
    for n in ("conv_w0", "conv_w1"):
        arrays[n] = np.ascontiguousarray(arrays[n].transpose(2, 3, 1, 0))
    arrays["w_qkv_t"] = np.ascontiguousarray(np.asarray(inputs["L0_attn_b_w_qkv"]).T)
    arrays["b_qkv"] = np.ascontiguousarray(inputs["L0_attn_b_b_qkv"])
    for n in ("gate", "up", "down"):
        arrays[n + "_words"] = np.ascontiguousarray(np.asarray(inputs[f + n + "_W_packed"]).T)
        arrays[n + "_scale_t"] = np.ascontiguousarray(np.asarray(inputs[f + n + "_scales"]).T)
    arrays["consts"] = shape_constants()

    nc = bacc.Bacc("TRN2", target_bir_lowering=False, num_devices=1)
    aps = [nc.dram_tensor(f"in_{n}", v.shape, mybir.dt.from_np(v.dtype), kind="ExternalInput").ap()
           for n, v in arrays.items()]
    scratch = nc.dram_tensor("scratch", (CH, ROWS * CH), mybir.dt.float32, kind="Internal").ap()
    spill = nc.dram_tensor("spill", (4, 2, P, ROWS), mybir.dt.float16, kind="Internal").ap()
    out = nc.dram_tensor("out_dram", (B, ROWS, D), mybir.dt.float32, kind="ExternalOutput").ap()
    program(nc, *aps, scratch, spill, out)
    r = run_bass_kernel_spmd(nc, [{f"in_{n}": v for n, v in arrays.items()}], core_ids=[0])
    return r.results[0]["out_dram"]
```

```python
from contextlib import ExitStack

import numpy as np

import concourse.bass as bass
from concourse import mybir

P = 128
B, ROWS, D = 4, 512, 256
RT = ROWS // P
KT = D // P
CH = 16
HCH = CH // 2
WIN = 8
HALVES = D // (WIN * CH)
WG = RT * HALVES
BLK = WIN * HCH
F = 2048
NCH = F // P
QB = 32
NH, HD = 16, 16
HG = P // HD
OW = 64
OUT = 2 * (HD + 1)
PR = 3
EPS = 1e-5
NEG = -1e30

X_EXP = 11
W_EXP = 12
I_EXP = -8
WB_EXP = 6
MAX_EXP = 8

C_ID, C_MQK, C_MKQ, C_COS, C_SIN = 0, 128, 256, 384, 896
C_BOTH = 1408
C_ALL = C_BOTH + OUT

QK_STRIP = {3: (0, 512), 2: (512, 384), 0: (896, 128), 1: (1024, 256)}
KQ_STRIP = {0: (0, 512), 1: (512, 384), 3: (896, 128), 2: (1024, 256)}
STRIPS = 1280
TAKEN = (1, 3, 3, 4)

MATRICES = ("gate", "up", "down")

SIGNALS = """
consts_in attn_a_weights_in attn_b_weights_in gate_words_in up_words_in down_words_in
gate_scale_in up_scale_in down_scale_in constants_set blocks_ready conv_bias_ready conv_bias_projected
raw_scales_in scale_max_ready scale_max_all scale_factor_ready scale_scaled weight_f32_ready weight_hi_ready weight_lo_ready
var_ready rstd_ready xn_ready xt_ready xt_evacuated xt_lo_ready
dve_chain pool_chain
x_taken a_x_in a_var_ready a_rstd_ready a_xn_ready a_xt_ready a_xt_out a_xt_placed
a_qkv_ready a_qkv_out a_qk_ready a_qk_summed a_score_shifted a_exp_ready a_exp2_ready a_xn_biased
a_av_ready a_av_own_ready a_av_summed a_branch_ready a_branch_t_ready a_branch_t_out a_proj_ready
a_centered a_sq_ready a_tok_ready a_stored
gate_ready up_ready square_ready cubic_ready tanh_ready inter_ready inter_hi_ready inter_lo_ready
down_used down_out down_out_v down_t_ready f_done
b_weights_f32_in wb_scaled wb_hi_ready wb_lo_ready
b_qk_projected b_rope_sum b_rope_ready b_hi_ready b_lo_ready b_max_row_in
b_spilled0 b_spilled1 b_spilled2 b_spilled3 b_stacked0 b_stacked1
b_v_ready b_v_out b_vhi_ready b_vlo_ready b_qk_ready b_max_taken b_max_scaled b_max_t_ready b_max_hi b_max_lo
b_max_in0 b_max_in1 b_kq_ready b_exp_ready b_phi_ready b_plo_ready b_phi_end_ready b_plo_end_ready b_av_done
b_o_out b_o_t_ready b_o_added
a_back x_out_stored
""".split()


def program(nc, x, a_qkv_blocks, a_shifted_blocks, a_proj_blocks, a_taps, a_conv_bias, a_proj_w, a_rows,
            b_qkv_t, b_bias_t, bv_row, ring_rows, gate_words, gate_scale_t, up_words, up_scale_t, down_words, down_scale_t,
            consts, scratch, spill, out):
    f32, f16, bf16, i32 = mybir.dt.float32, mybir.dt.float16, mybir.dt.bfloat16, mybir.dt.int32
    ALU = mybir.AluOpType
    ACT = mybir.ActivationFunctionType
    AX = mybir.AxisListType

    ctx = ExitStack()
    with ctx:
        def sb(name, shape, dt=f32):
            return ctx.enter_context(nc.sbuf_tensor(name, shape, dt))

        s = {}
        for name in SIGNALS:
            s[name] = ctx.enter_context(nc.semaphore(name))
        all_signals = range(s[SIGNALS[0]].num, s[SIGNALS[-1]].num + 1)
        assert len(all_signals) == len(SIGNALS)
        stage_signals = all_signals[:-2]

        con = sb("con", [P, C_ALL])
        ident = con[:, C_ID:C_ID + P]
        cos_t = con[:, C_COS:C_COS + ROWS]
        sin_t = con[:, C_SIN:C_SIN + ROWS]
        both_parts = con[:, C_BOTH:C_BOTH + OUT]
        masks = sb("masks", [P, 3, P], bf16)
        bd1 = sb("bd1", [P, 4, WIN, HCH])
        bd2 = sb("bd2", [P, 3 + 3, WIN, HCH])
        shifted = sb("shifted", [P, 3, WIN, HCH])
        bdp = sb("bdp", [P, WIN, CH])
        conv = sb("conv", [P, 2, 3, HCH])
        proj = sb("proj", [CH, CH])
        conv_bias = sb("conv_bias", [CH, 1])
        conv_bias_wide = sb("conv_bias_wide", [CH, P])
        a_row = sb("a_row", [P, 3, CH])
        pb_, lw, lb = (a_row[:, n, :] for n in range(3))
        wb_hi = sb("wb_hi", [P, KT, 5, NH * HD], f16)
        wb_lo = sb("wb_lo", [P, KT, 5, NH * HD], f16)
        bqk = sb("bqk", [P, 2, 2, 2])
        bv = sb("bv", [P, NH, HD])
        w_hi = [sb(f"w_hi{m}", [P, 2 * F], f16) for m in range(3)]
        w_lo = [sb(f"w_lo{m}", [P, 2 * F], f16) for m in range(3)]
        smax = sb("smax", [P, 3])
        gmax = sb("gmax", [P, 3])
        pow2 = sb("pow2", [P, 3])
        rpow2 = sb("rpow2", [P, 3])
        c_sq = sb("c_sq", [P, 1])
        c_th = sb("c_th", [P, 1])
        c_dn = sb("c_dn", [P, 1])
        half_neg = sb("half_neg", [P, RT])
        va = sb("va", [P, RT, NH, OW], f16)

        row_memory = sb("row_memory", [P, 4 * RT * D])
        X, xn = (row_memory[:, n * RT * D:(n + 1) * RT * D].rearrange("p (j d) -> p j d", j=RT) for n in range(2))
        xt = row_memory[:, 2 * RT * D:3 * RT * D].rearrange("p (k r) -> p k r", k=KT)
        xh, xl = (row_memory[:, (6 + n) * ROWS:(7 + n) * ROWS].bitcast(f16).rearrange("p (k r) -> p k r", k=KT)
                  for n in range(2))
        stats = sb("stats", [P, RT, 6])
        mv = sb("mv", [P, RT, 2])
        veps = sb("veps", [P, RT])
        rstd = sb("rstd", [P, RT])

        arena = sb("arena", [P, 16384])
        arena_at = [0]

        def part(shape, dt=f32):
            n = int(np.prod(shape[1:]))
            words = n if dt in (f32, i32) else n // 2
            at = arena_at[0]
            arena_at[0] = at + words
            assert arena_at[0] <= 16384
            v = arena[0:shape[0], at:at + words]
            if dt != f32:
                v = v.bitcast(dt)
            names = "abcd"[:len(shape) - 1]
            if len(names) == 1:
                return v
            return v.rearrange(f"p ({' '.join(names)}) -> p {' '.join(names)}",
                               **{k: n for k, n in zip(names, shape[1:])})

        banks = ctx.enter_context(nc.psum_tensor("banks", [P, 8, 512], f32))

        def bank(i, n=1):
            return banks[:, i:i + n, :].rearrange("p a b -> p (a b)")

        def chain(eng, sem):
            count = [0]

            def link(ins):
                count[0] += 1
                ins.then_inc(sem, 1)
                eng.wait_ge(sem, count[0])
            return link

        def ln_gather(dve, link):
            for j in range(RT):
                ins = nc.vector.bn_aggr(mv[:, j, :], stats[:, j, :])
            link(ins)
            nc.vector.tensor_scalar(veps[:], mv[:, :, 1], EPS, 2.0 ** (-2 * X_EXP), ALU.add, ALU.mult
                                    ).then_inc(s["var_ready"], 1)

        def ln_root(pool):
            pool.wait_ge(s["var_ready"], 1)
            nc.gpsimd.tensor_tensor(rstd[:], veps[:], half_neg[:, 0:RT], ALU.pow).then_inc(s["rstd_ready"], 1)

        def ln_apply(dve, src):
            dve.wait_ge(s["rstd_ready"], 1)
            for j in range(RT):
                nc.vector.tensor_scalar(xn[:, j, :], src[:, j, :], mv[:, j, 0:1], rstd[:, j:j + 1],
                                        ALU.subtract, ALU.mult).then_inc(s["xn_ready"], 1)

        def keep_clock(o, count):
            for _ in range(count):
                nc.tensor.matmul(o, w_hi[0][:, 0:P], w_hi[0][:, 0:ROWS], start=True, stop=True)

        def transpose_rows(pe, columns, wait_products):
            keep_clock(bank(0), wait_products)
            for j in range(RT):
                pe.wait_ge(s["xn_ready"], j + 1)
                for kt in range(KT):
                    ins = nc.tensor.transpose(bank(6 + kt)[:, j * P:(j + 1) * P], columns(xn[:, j, :], kt), ident)
            ins.then_inc(s["xt_ready"], 1)
            keep_clock(bank(0), 3)

        xa = sb("xa", [P, RT, D])
        a_back = sb("a_back", [P, RT, D])
        xna = sb("xna", [P, RT, D])
        a_stats = sb("a_stats", [P, RT, 6])
        a_mv = sb("a_mv", [P, RT, 2])
        a_veps = sb("a_veps", [P, RT])
        a_rstd = sb("a_rstd", [P, RT])
        qkv = [sb(f"qkv{br}", [P, WG, 4, BLK]) for br in range(2)]
        score = [sb(f"score{br}", [P, WG, WIN, WIN]) for br in range(2)]
        smx = sb("smx", [P, WG * WIN])
        rsum = [sb(f"rsum{br}", [P, WG, WIN]) for br in range(2)]
        centre = sb("centre", [P, WIN])
        v16, r16, t16 = (sb(name, [P, RT * CH]) for name in ("v16", "r16", "t16"))

        arena_at[0] = 0
        R = 3
        sq = [part([P, ROWS]) for _ in range(2)]
        cub = [part([P, ROWS]) for _ in range(2)]
        th = [part([P, ROWS]) for _ in range(2)]
        gl = [part([P, ROWS]) for _ in range(2)]
        inter = [part([P, ROWS]) for _ in range(R)]
        ih = [part([P, ROWS], f16) for _ in range(R)]
        il = [part([P, ROWS], f16) for _ in range(R)]
        yt = part([P, 2, ROWS])
        LAG = 2
        ffn_end = arena_at[0]

        prod = part([P, WG, WIN * WIN * HCH])
        flat = prod.rearrange("p a b -> p (a b)")
        att, att2, tok = (flat[:, n * RT * D:(n + 1) * RT * D] for n in range(3))
        xbr = [part([P, WG, WIN, HCH]) for _ in range(2)]
        second_at = arena_at[0]
        xta = part([P, KT, ROWS])
        xtp = part([P, WIN, HALVES, ROWS // WIN])
        arena_at[0] = second_at
        brt = part([P, HALVES, ROWS])

        def window_view(t, br, which=None):
            v = t[:, :, which, :] if which is not None else t.rearrange("p a b c -> p a (b c)")
            v = v.rearrange("p a (b c) -> p a b c", c=HCH)
            return v if br == 0 else v.rearrange("p a b c -> p b a c")

        A_STEPS = 16

        def a_sync(sp, stage, b, running):
            if stage == 0:
                if running:
                    sp.wait_ge(s["x_taken"], RT)
                sp.dma_start(xa[:], x[bass.ds(b, 1)].rearrange("o (j p) w -> p (o j) w", p=P)
                             ).then_inc(s["a_x_in"], 16)
                sp.wait_ge(s["a_x_in"], 16)
            else:
                t4 = tok.rearrange("p (j c w) -> p j c w", j=RT, c=CH)
                for j in range(RT):
                    dst = scratch[:, j * P * CH:(j + 1) * P * CH].rearrange("c (p w) -> p c w", w=CH)
                    sp.wait_ge(s["a_tok_ready"], j + 1)
                    sp.dma_start(dst, t4[:, j]).then_inc(s["a_stored"], 16)
                sp.wait_ge(s["a_stored"], 16 * RT)
                sp.dma_start(a_back[:], scratch.rearrange("c (q w) -> (c q) w", w=D).rearrange(
                    "(j p) w -> p j w", p=P)).then_inc(s["a_back"], 16)

        def a_qk_products(pool, br, gs):
            q, k = (window_view(qkv[br], br, w) for w in range(2))
            for g in gs:
                if br:
                    pool.wait_ge(s["a_qk_summed"], g // 2 + 1)
                nc.gpsimd.tensor_tensor(
                    prod[:, g, :].rearrange("p (i j c) -> p i j c", i=WIN, j=WIN),
                    q[:, g].unsqueeze(2).broadcast_to([P, WIN, WIN, HCH]),
                    k[:, g].unsqueeze(1).broadcast_to([P, WIN, WIN, HCH]), ALU.mult
                ).then_inc(s["a_qk_ready"], 1)

        def a_av_products(eng, br, gs, ready):
            v = window_view(qkv[br], br, 2)
            for g in gs:
                if br:
                    eng.wait_ge(s["a_av_summed"], g // 2 + 1)
                (nc.gpsimd if ready == "a_av_ready" else nc.vector).tensor_tensor(
                    prod[:, g, :].rearrange("p (i c j) -> p i c j", i=WIN, j=WIN),
                    score[br][:, g].unsqueeze(2).broadcast_to([P, WIN, HCH, WIN]),
                    v[:, g].rearrange("p j c -> p c j").unsqueeze(1).broadcast_to([P, WIN, HCH, WIN]),
                    ALU.mult).then_inc(s[ready], 1)

        def a_gpsimd(pool, stage, i):
            if stage == 0:
                if i == 1:
                    pool.wait_ge(s["a_var_ready"], 1)
                    nc.gpsimd.tensor_tensor(a_rstd[:], a_veps[:], half_neg[:, 0:RT], ALU.pow
                                            ).then_inc(s["a_rstd_ready"], 1)
                if 6 <= i < 10:
                    pool.wait_ge(s["a_qkv_out"], 2 * (i - 6) // 2 + 1)
                    a_qk_products(pool, 0, (2 * (i - 6), 2 * (i - 6) + 1))
                if 10 <= i < 14:
                    pool.wait_ge(s["a_qkv_out"], 8)
                    a_qk_products(pool, 1, (2 * (i - 10), 2 * (i - 10) + 1))
                if i == 15:
                    pool.wait_ge(s["a_xt_ready"], 1)
                    xt3 = xna[:].rearrange("p j (t c) -> p (j t) c", c=CH)
                    nc.gpsimd.tensor_tensor(xt3, xt3, lb.unsqueeze(1).broadcast_to([P, RT * CH, CH]), ALU.add
                                            ).then_inc(s["a_xn_biased"], 1)
            else:
                if i < 6:
                    br, k = divmod(i, 3)
                    if i == 3:
                        pool.wait_ge(s["a_exp2_ready"], 1)
                    a_av_products(pool, br, ((0, 1), (2, 4), (5, 6))[k], "a_av_ready")

        def a_scalar(act, stage, i):
            scale_a = float(HCH) ** -0.5
            if stage == 0:
                if i == 3:
                    act.wait_ge(s["a_xt_ready"], 1)
                    for kt in range(KT):
                        nc.scalar.copy(xta[:, kt, :], bank(6 + kt)).then_inc(s["a_xt_out"], 1)
                if i == 4:
                    for kt in range(KT):
                        nc.scalar.copy(xtp[:, :, kt].rearrange("p a (i r) -> p a i r", r=4),
                                       bank(6 + kt).rearrange("p (i a r) -> p a i r", a=WIN, r=4)
                                       ).then_inc(s["a_xt_placed"], 1)
                if 5 <= i < 9:
                    br, n = divmod(i - 5, 2)
                    for m in range(2):
                        act.wait_ge(s["a_qkv_ready"], 2 * (i - 5) + m + 1)
                        a = 4 * n + 2 * m
                        nc.scalar.copy(qkv[br][:, a:a + 2].rearrange("p a w b -> p (a w b)"), bank(6 + m)
                                       ).then_inc(s["a_qkv_out"], 1)
                if i == 12:
                    act.wait_ge(s["a_score_shifted"], 1)
                    nc.scalar.activation(score[0][:], score[0][:], ACT.Exp, scale=scale_a
                                         ).then_inc(s["a_exp_ready"], 1)
            else:
                if i == 0:
                    nc.scalar.activation(score[1][:], score[1][:], ACT.Exp, scale=scale_a
                                         ).then_inc(s["a_exp2_ready"], 1)
                if i == 6:
                    act.wait_ge(s["a_branch_t_ready"], 1)
                    nc.scalar.copy(brt[0:BLK].rearrange("p a b -> p (a b)"), bank(6, 2)[0:BLK]
                                   ).then_inc(s["a_branch_t_out"], 1)
                if i == 9:
                    act.wait_ge(s["a_branch_t_ready"], 2)
                    for m in range(2):
                        o = brt[BLK:].rearrange("p f (i a r) -> p f a i r", a=WIN, r=4)
                        for f in range(HALVES):
                            ins = nc.scalar.copy(o[:, f, 4 * m:4 * m + 4], bank(6 + m)[BLK:].rearrange(
                                "p (a f i r) -> p f a i r", f=2, i=16, r=4)[:, f])
                    ins.then_inc(s["a_branch_t_out"], 1)
                if i == 11:
                    act.wait_ge(s["a_centered"], 1)
                    nc.scalar.activation(att2, att, ACT.Square).then_inc(s["a_sq_ready"], 1)

        def a_tensor(pe, stage, i):
            if stage == 0:
                if i == 3:
                    pe.wait_ge(s["a_xn_ready"], 1)
                    for j in range(RT):
                        for kt in range(KT):
                            ins = nc.tensor.transpose(bank(6 + kt)[:, j * P:(j + 1) * P],
                                                      xna[:, j, kt * P:(kt + 1) * P], ident)
                    ins.then_inc(s["a_xt_ready"], 1)
                if 5 <= i < 7:
                    pe.wait_ge(s["a_xt_placed"], KT)
                    w = bd1[:].rearrange("p w t c -> p (w t c)")
                    for m in range(2):
                        j = 2 * (i - 5) + m
                        if j >= 2:
                            pe.wait_ge(s["a_qkv_out"], j - 1)
                        for h in range(HALVES):
                            ins = nc.tensor.matmul(bank(6 + m)[:, h * 4 * BLK:(h + 1) * 4 * BLK],
                                                   xta[:, h, j * P:(j + 1) * P], w, start=True, stop=True)
                        ins.then_inc(s["a_qkv_ready"], 1)
                if 7 <= i < 9:
                    w = bd2[:].rearrange("p w t c -> p (w t c)")
                    for m in range(2):
                        n = 2 * (i - 7) + m
                        pe.wait_ge(s["a_qkv_out"], 2 + n + 1)
                        for a in (2 * n, 2 * n + 1):
                            o = bank(6 + m)[:, (a % 2) * 4 * BLK:(a % 2 + 1) * 4 * BLK]
                            rows = xtp.rearrange("p a h r -> p a (h r)")
                            nc.tensor.matmul(o[:, 0:3 * BLK], rows[:, a, :], w[:, 0:3 * BLK], start=True, stop=True)
                            taps = [t for t in range(3) if 0 <= a + t - 1 < WIN]
                            for t in taps:
                                ins = nc.tensor.matmul(o[:, 3 * BLK:4 * BLK], rows[:, a + t - 1, :],
                                                       w[:, (3 + t) * BLK:(4 + t) * BLK],
                                                       start=t == taps[0], stop=t == taps[-1])
                        ins.then_inc(s["a_qkv_ready"], 1)
            else:
                if i == 6:
                    pe.wait_ge(s["a_branch_ready"], 1)
                    for g in range(WG):
                        j, h = divmod(g, HALVES)
                        ins = nc.tensor.transpose(bank(6 + h)[0:BLK, j * P:(j + 1) * P],
                                                  xbr[0][:, g].rearrange("p a b -> p (a b)"), ident)
                    ins.then_inc(s["a_branch_t_ready"], 1)
                if i == 9:
                    pe.wait_ge(s["a_branch_ready"], 2)
                    pe.wait_ge(s["a_branch_t_out"], 1)
                    for a in range(WIN):
                        ins = nc.tensor.matmul(bank(6, 2)[BLK:, a * P:(a + 1) * P],
                                               xbr[1][:, a].rearrange("p a b -> p (a b)"), ident,
                                               start=True, stop=True)
                    ins.then_inc(s["a_branch_t_ready"], 1)
                if i == 10:
                    pe.wait_ge(s["a_branch_t_out"], 2)
                    for j in range(RT):
                        for h in range(HALVES):
                            o = bank(6, 2)[:, (j * HALVES + h) * P:(j * HALVES + h + 1) * P]
                            ins = nc.tensor.matmul(o, brt[:, h, j * P:(j + 1) * P],
                                                   bdp[:].rearrange("p a b -> p (a b)"), start=True, stop=True)
                        if j % 2:
                            ins.then_inc(s["a_proj_ready"], 1)

        def a_qk_sums(dve, link, br, n):
            dve.wait_ge(s["a_qk_ready"], WG * br + 2 * n + 2)
            nc.vector.tensor_reduce(score[br][:, 2 * n:2 * n + 2].rearrange("p g i j -> p (g i j)"),
                                    prod[:, 2 * n:2 * n + 2].rearrange("p g (s c) -> p (g s) c", c=HCH),
                                    AX.X, ALU.add).then_inc(s["a_qk_summed"], 1)

        def a_score_shift(dve, link, br):
            dve.wait_ge(s["a_qk_summed"], 4 * (br + 1))
            s64 = score[br][:].rearrange("p g i j -> p (g i) j")
            link(nc.vector.tensor_reduce(smx[:], s64, AX.X, ALU.max))
            nc.vector.tensor_tensor(s64, s64, smx[:].unsqueeze(2).broadcast_to([P, WG * WIN, WIN]),
                                    ALU.subtract).then_inc(s["a_score_shifted"], 1)

        def a_prob_sums(dve, link, br):
            dve.wait_ge(s["a_exp2_ready" if br else "a_exp_ready"], 1)
            r = rsum[br][:].rearrange("p g i -> p (g i)")
            link(nc.vector.tensor_reduce(r, score[br][:].rearrange("p g i j -> p (g i) j"), AX.X, ALU.add))
            link(nc.vector.reciprocal(r, r))

        def a_av_sums(dve, link, br, n):
            o = window_view(xbr[br], br)
            dve.wait_ge(s["a_av_ready"], 6 * br + (2, 3, 5, 6)[n])
            if n % 2:
                dve.wait_ge(s["a_av_own_ready"], 2 * br + n // 2 + 1)
            for g in (2 * n, 2 * n + 1):
                ins = nc.vector.tensor_reduce(
                    o[:, g], prod[:, g, :].rearrange("p (i c j) -> p i c j", c=HCH, j=WIN), AX.X, ALU.add)
            ins.then_inc(s["a_av_summed"], 1)

        def a_branch_end(dve, link, br):
            o = window_view(xbr[br], br)
            dve.wait_ge(s["a_av_summed"], 4 * (br + 1))
            link(nc.vector.tensor_tensor(o, o, rsum[br][:].unsqueeze(3).broadcast_to([P, WG, WIN, HCH]), ALU.mult))
            nc.vector.tensor_tensor(o, o, window_view(qkv[br], br, 3), ALU.add).then_inc(s["a_branch_ready"], 1)

        def a_vector(dve, link, stage, i):
            full = [P, RT * CH, CH]
            a3 = att.rearrange("p (t c) -> p t c", c=CH)
            if stage == 0:
                if i == 0:
                    dve.wait_ge(s["a_x_in"], 16)
                    for j in range(RT):
                        ins = nc.vector.bn_stats(a_stats[:, j, :], xa[:, j, :])
                    link(ins)
                    for j in range(RT):
                        ins = nc.vector.bn_aggr(a_mv[:, j, :], a_stats[:, j, :])
                    link(ins)
                    nc.vector.tensor_scalar(a_veps[:], a_mv[:, :, 1], EPS, None, ALU.add
                                            ).then_inc(s["a_var_ready"], 1)
                if i == 2:
                    dve.wait_ge(s["a_rstd_ready"], 1)
                    for j in range(RT):
                        ins = nc.vector.tensor_scalar(xna[:, j, :], xa[:, j, :], a_mv[:, j, 0:1],
                                                      a_rstd[:, j:j + 1], ALU.subtract, ALU.mult)
                    ins.then_inc(s["a_xn_ready"], 1)
                if 7 <= i < 11:
                    a_qk_sums(dve, link, 0, i - 7)
                if i == 11:
                    a_score_shift(dve, link, 0)
                if i == 13:
                    a_prob_sums(dve, link, 0)
                if 11 <= i < 15:
                    a_qk_sums(dve, link, 1, i - 11)
                if i == 15:
                    a_score_shift(dve, link, 1)
            else:
                if i == 0:
                    a_av_products(dve, 0, (3, 7), "a_av_own_ready")
                if 1 <= i < 5:
                    a_av_sums(dve, link, 0, i - 1)
                if i in (3, 4):
                    dve.wait_ge(s["a_exp2_ready"], 1)
                    a_av_products(dve, 1, ((3,), (7,))[i - 3], "a_av_own_ready")
                if i == 5:
                    a_branch_end(dve, link, 0)
                    a_prob_sums(dve, link, 1)
                if 6 <= i < 9:
                    for n in ((0, 1), (2,), (3,))[i - 6]:
                        a_av_sums(dve, link, 1, n)
                if i == 8:
                    a_branch_end(dve, link, 1)
                if i == 11:
                    for m in range(2):
                        dve.wait_ge(s["a_proj_ready"], 2)
                        ins = nc.vector.tensor_tensor(
                            a3[:, 32 * m:32 * m + 32], bank(6 + m).rearrange("p (t c) -> p t c", c=CH),
                            pb_.unsqueeze(1).broadcast_to([P, 32, CH]), ALU.add)
                    ins.then_inc(s["a_centered"], 1)
                if i == 12:
                    dve.wait_ge(s["a_sq_ready"], 1)
                    link(nc.vector.tensor_reduce(v16[:], att2.rearrange("p (t c) -> p t c", c=CH), AX.X, ALU.add))
                    link(nc.vector.tensor_scalar(v16[:], v16[:], 1.0 / CH, EPS, ALU.mult, ALU.add))
                    link(nc.vector.tensor_scalar(r16[:].bitcast(i32), v16[:].bitcast(i32), 1, None,
                                                 ALU.logical_shift_right))
                    link(nc.vector.tensor_scalar(r16[:].bitcast(i32), r16[:].bitcast(i32), -1.0, float(0x5F3759DF),
                                                 ALU.mult, ALU.add))
                for _ in range({12: 1, 13: 2}.get(i, 0)):
                    link(nc.vector.scalar_tensor_tensor(t16[:], r16[:], -0.5, r16[:], ALU.mult, ALU.mult))
                    link(nc.vector.tensor_tensor(t16[:], t16[:], v16[:], ALU.mult))
                    link(nc.vector.scalar_tensor_tensor(r16[:], t16[:], 1.5, r16[:], ALU.add, ALU.mult))
                if i == 13:
                    link(nc.vector.tensor_tensor(a3, a3, r16[:].unsqueeze(2).broadcast_to(full), ALU.mult))
                if i == 14:
                    link(nc.vector.tensor_tensor(a3, a3, lw.unsqueeze(1).broadcast_to(full), ALU.mult))
                if i == 14:
                    for j in range(RT):
                        nc.vector.tensor_tensor(
                            tok.rearrange("p (j c w) -> p j w c", j=RT, c=CH)[:, j],
                            att.rearrange("p (j w c) -> p j w c", j=RT, c=CH)[:, j],
                            xna[:, j, :].rearrange("p (w c) -> p w c", c=CH), ALU.add
                        ).then_inc(s["a_tok_ready"], 1)

        arena_at[0] = 0
        words, scale = zip(*((part([P, F], i32), part([P, F])) for _ in range(2)))
        assert arena_at[0] <= ffn_end
        wb32 = arena[:, 2 * F:2 * F + KT * 5 * NH * HD].rearrange("p (k n) -> p k n", k=KT)
        raw_scales = a_back[:].rearrange("p a b -> p (a b)")[:, 0:3 * P].rearrange("p (m n) -> p m n", m=3)
        wf = row_memory[:]
        wb_parts = [w[:].rearrange("p k w n -> p k (w n)") for w in (wb_hi, wb_lo)]
        magn = w_lo[2][:].bitcast(i32)

        CODES_AT = {(0, 0): 0, (0, 3): 1, (0, 10): 2}
        BITS_AT = {(0, 1): 0, (0, 4): 1, (0, 12): 2}
        VALUES_AT = {(0, 2): 0, (0, 8): 1, (1, 3): 2}
        SCALE_AT = {(0, 0): 0, (0, 3): 1, (0, 8): 2}
        HIGH_AT = {(0, 2): 0, (0, 8): 1, (1, 3): 2}
        LOW_AT = {(0, 3): 0, (0, 13): 1, (1, 5): 2}

        def weights_vector(dve, link, at):
            if at in CODES_AT:
                m = CODES_AT[at]
                w = words[m % 2]
                dve.wait_ge(s[MATRICES[m] + "_words_in"], 16)
                link(nc.vector.scalar_tensor_tensor(w, w, 12, w, ALU.logical_shift_left, ALU.bitwise_or))
            if at in BITS_AT:
                w = words[BITS_AT[at] % 2]
                link(nc.vector.tensor_scalar(magn, w, 0x00070007, 9, ALU.bitwise_and, ALU.logical_shift_left))
                link(nc.vector.tensor_scalar(w, w, 0x00080008, 12, ALU.bitwise_and, ALU.logical_shift_left))
                link(nc.vector.tensor_tensor(magn, magn, w, ALU.bitwise_or))
            if at in VALUES_AT:
                m = VALUES_AT[at]
                sc = scale[m % 2]
                dve.wait_ge(s["scale_scaled"], m + 1)
                if m >= 1:
                    dve.wait_ge(s["weight_lo_ready"], m)
                val = magn.bitcast(f16)
                for nib in range(2):
                    if m < 2:
                        o = wf[:, nib * F:(nib + 1) * F].rearrange("p (c e u) -> p c e u", e=2, u=P)
                        v = val.rearrange("p (c u e k) -> p k c e u", e=2, u=P, k=2)[:, nib]
                        g = sc.rearrange("p (c u e) -> p c e u", e=2, u=P)
                        for e in range(2):
                            ins = nc.vector.tensor_tensor(o[:, :, e], v[:, :, e], g[:, :, e], ALU.mult)
                    else:
                        o = wf.rearrange("p (c e h) -> p c e h", e=2, h=D)[:, :, nib]
                        v = val.rearrange("p (c h e) -> p e c h", e=2, h=D)[:, nib]
                        ins = nc.vector.tensor_tensor(o, v, sc.rearrange("p (c h) -> p c h", h=D), ALU.mult)
                ins.then_inc(s["weight_f32_ready"], 1)
                dve.wait_ge(s["weight_f32_ready"], m + 1)

        def prepare(b):
            with nc.Block() as block:
                @block.sync
                def _(sp):
                    def load_matrix(m):
                        w, sc = ((gate_words, gate_scale_t), (up_words, up_scale_t), (down_words, down_scale_t))[m]
                        words_in, scale_in = s[MATRICES[m] + "_words_in"], s[MATRICES[m] + "_scale_in"]
                        if m < 2:
                            sp.dma_start(words[m % 2], w).then_inc(words_in, 16)
                            sp.dma_start(scale[m % 2], sc.unsqueeze(1).broadcast_to([D // QB, QB // 2, F])
                                         ).then_inc(scale_in, 16)
                        else:
                            for c in range(F // D):
                                sp.dma_start(scale[m % 2][:, c * D:(c + 1) * D],
                                             sc[8 * c:8 * c + 8].unsqueeze(1).broadcast_to([8, QB // 2, D])
                                             ).then_inc(scale_in, 16)
                            sp.dma_start(words[m % 2].rearrange("p (c h) -> p c h", h=D),
                                         w.rearrange("(c p) h -> p c h", p=P)).then_inc(words_in, 16)

                    def attn_a(dst, src):
                        sp.dma_start(dst, src).then_inc(s["attn_a_weights_in"], 16)

                    def attn_b(dst, src):
                        sp.dma_start(dst, src).then_inc(s["attn_b_weights_in"], 16)

                    sp.dma_start(xa[:], x[bass.ds(b, 1)].rearrange("o (j p) w -> p (o j) w", p=P)
                                 ).then_inc(s["a_x_in"], 16)
                    for m, sc in enumerate((gate_scale_t, up_scale_t, down_scale_t)):
                        sp.dma_start(raw_scales[:, m, :], sc.rearrange("a (b n) -> (a b) n", n=P)
                                     ).then_inc(s["raw_scales_in"], 16)
                    load_matrix(0)
                    sp.dma_start(con[:], consts).then_inc(s["consts_in"], 16)
                    blocks = a_qkv_blocks.rearrange("p (b w t c) -> p b w t c", b=2, w=3, c=HCH)
                    attn_a(bd1[:, 0:3], blocks[:, 0])
                    attn_a(bd2[:, 0:3], blocks[:, 1])
                    attn_a(shifted[:].rearrange("p a b c -> p (a b c)"), a_shifted_blocks)
                    attn_a(bdp[:].rearrange("p a b -> p (a b)"), a_proj_blocks)
                    attn_a(conv[:].rearrange("p a b c -> p (a b c)"),
                           a_taps.unsqueeze(0).broadcast_to([P, 2 * 3 * HCH]))
                    attn_a(conv_bias[:], a_conv_bias)
                    attn_a(proj[:], a_proj_w)
                    attn_a(a_row[:].rearrange("p a b -> p (a b)"), a_rows.unsqueeze(0).broadcast_to([P, 3 * CH]))
                    load_matrix(1)
                    attn_b(bqk[:].rearrange("p a b c -> p (a b c)"), b_bias_t)
                    attn_b(bv[:].rearrange("p a b -> p (a b)"), bv_row.unsqueeze(0).broadcast_to([P, NH * HD]))
                    sp.wait_ge(s["weight_f32_ready"], 1)
                    load_matrix(2)
                    sp.wait_ge(s["weight_f32_ready"], 2)
                    sp.dma_start(wb32, b_qkv_t.rearrange("(k p) w n -> p k (w n)", p=P)
                                 ).then_inc(s["b_weights_f32_in"], 16)
                    sp.wait_ge(s["attn_b_weights_in"], 16 * 2)
                    sp.wait_ge(s["consts_in"], 16)
                    a_sync(sp, 1, b, False)
                    sp.nop().then_inc(s["x_out_stored"], 16)

                @block.gpsimd
                def _(pool):
                    link = chain(pool, s["pool_chain"])
                    nc.gpsimd.memset(half_neg[:], -0.5)
                    link(nc.gpsimd.memset(va[:].bitcast(f32), 0.0))
                    nc.gpsimd.memset(va[:, :, :, 2 * HD:2 * HD + 1], 1.0).then_inc(s["constants_set"], 1)
                    pool.wait_ge(s["constants_set"], 1)

                    def between(at):
                        if at in LOW_AT:
                            m = LOW_AT[at]
                            pool.wait_ge(s["weight_hi_ready"], m + 1)
                            nc.gpsimd.tensor_tensor(w_lo[m][:], wf, w_hi[m][:], ALU.subtract
                                                    ).then_inc(s["weight_lo_ready"], 1)

                    pool.wait_ge(s["scale_max_ready"], 1)
                    nc.gpsimd.partition_all_reduce(gmax[:], smax[:], P, bass.bass_isa.ReduceOp.max
                                                   ).then_inc(s["scale_max_all"], 1)
                    for i in range(A_STEPS):
                        a_gpsimd(pool, 0, i)
                        between((0, i))
                    pool.wait_ge(s["a_exp_ready"], 1)
                    pool.wait_ge(s["a_qk_summed"], WG)
                    for i in range(A_STEPS):
                        a_gpsimd(pool, 1, i)
                        between((1, i))
                        if i == 7:
                            pool.wait_ge(s["wb_hi_ready"], 1)
                            nc.gpsimd.tensor_tensor(wb_parts[1], wb32, wb_parts[0], ALU.subtract
                                                    ).then_inc(s["wb_lo_ready"], 1)

                @block.scalar
                def _(act):
                    def between(at):
                        if at in SCALE_AT:
                            m = SCALE_AT[at]
                            act.wait_ge(s["scale_factor_ready"], 1)
                            act.wait_ge(s[MATRICES[m] + "_scale_in"], 16 if m < 2 else 16 * (F // D))
                            nc.scalar.activation(scale[m % 2], scale[m % 2], ACT.Copy, scale=rpow2[:, m:m + 1]
                                                 ).then_inc(s["scale_scaled"], 1)
                        if at in HIGH_AT:
                            m = HIGH_AT[at]
                            act.wait_ge(s["weight_f32_ready"], m + 1)
                            nc.scalar.activation(w_hi[m][:], wf, ACT.Copy).then_inc(s["weight_hi_ready"], 1)

                    for i in range(A_STEPS):
                        a_scalar(act, 0, i)
                        between((0, i))
                    act.wait_ge(s["a_score_shifted"], 2)
                    for i in range(A_STEPS):
                        a_scalar(act, 1, i)
                        between((1, i))
                        if i == 3:
                            act.wait_ge(s["b_weights_f32_in"], 16)
                            nc.scalar.activation(wb32, wb32, ACT.Copy, scale=2.0 ** WB_EXP
                                                 ).then_inc(s["wb_scaled"], 1)
                            act.wait_ge(s["wb_scaled"], 1)
                            nc.scalar.activation(wb_parts[0], wb32, ACT.Copy).then_inc(s["wb_hi_ready"], 1)

                @block.tensor
                def _(pe):
                    pe.wait_ge(s["conv_bias_ready"], 1)
                    pe.wait_ge(s["attn_a_weights_in"], 16 * 8)
                    nc.tensor.matmul(bank(0)[:, 0:CH], conv_bias_wide[:], proj[:], start=True, stop=True
                                     ).then_inc(s["conv_bias_projected"], 1)
                    pe.wait_ge(s["consts_in"], 16)
                    pe.wait_ge(s["blocks_ready"], 1)
                    for i in range(A_STEPS):
                        a_tensor(pe, 0, i)
                    pe.wait_ge(s["a_qkv_out"], WG)
                    for i in range(A_STEPS):
                        a_tensor(pe, 1, i)

                @block.vector
                def _(dve):
                    link = chain(dve, s["dve_chain"])
                    dve.wait_ge(s["raw_scales_in"], 16 * 3)
                    nc.vector.tensor_reduce(smax[:], raw_scales, AX.X, ALU.max, apply_absolute_value=True
                                            ).then_inc(s["scale_max_ready"], 1)
                    a_vector(dve, link, 0, 0)
                    dve.wait_ge(s["scale_max_all"], 1)
                    link(nc.vector.tensor_scalar(gmax[:], gmax[:], 1e-30, None, ALU.max))
                    link(nc.vector.tensor_scalar(pow2[:].bitcast(i32), gmax[:].bitcast(i32), 0x7F800000, None,
                                                 ALU.bitwise_and))
                    link(nc.vector.reciprocal(rpow2[:], pow2[:]))
                    nc.vector.tensor_scalar(rpow2[:], rpow2[:], 2.0 ** (W_EXP + 14), None, ALU.mult
                                            ).then_inc(s["scale_factor_ready"], 1)
                    weights_vector(dve, link, (0, 0))
                    dve.wait_ge(s["attn_a_weights_in"], 16 * 8)
                    for tap in range(3):
                        taps = [conv[:, br, tap, :].unsqueeze(1).broadcast_to([P, WIN, HCH]) for br in range(2)]
                        nc.vector.tensor_tensor(bd2[:, 3 + tap], bd2[:, 2], taps[1], ALU.mult)
                        ins = nc.vector.tensor_tensor(shifted[:, tap], shifted[:, tap], taps[0], ALU.mult)
                    link(ins)
                    nc.vector.tensor_copy(conv_bias_wide[:], conv_bias[:].broadcast_to([CH, P])
                                          ).then_inc(s["conv_bias_ready"], 1)
                    link(nc.vector.tensor_tensor(bd1[:, 3], shifted[:, 0], shifted[:, 1], ALU.add))
                    nc.vector.tensor_tensor(bd1[:, 3], bd1[:, 3], shifted[:, 2], ALU.add
                                            ).then_inc(s["blocks_ready"], 1)
                    for i in range(1, A_STEPS):
                        a_vector(dve, link, 0, i)
                        weights_vector(dve, link, (0, i))
                    dve.wait_ge(s["conv_bias_projected"], 1)
                    link(nc.vector.tensor_tensor(pb_, pb_, bank(0)[:, 0:CH], ALU.add))
                    for rows, w, mean in ((bdp[:], WIN, centre[:]),
                                          (pb_.unsqueeze(1), 1, centre[:, 0:1])):
                        n = rows.shape[0]
                        link(nc.vector.tensor_reduce(mean, rows, AX.X, ALU.add))
                        link(nc.vector.tensor_scalar(mean, mean, -1.0 / CH, None, ALU.mult))
                        link(nc.vector.tensor_tensor(rows, rows, mean.unsqueeze(2).broadcast_to([n, w, CH]), ALU.add))
                    dve.wait_ge(s["consts_in"], 16)
                    nc.vector.tensor_copy(masks[:, 0, :], ident)
                    link(nc.vector.tensor_copy(masks[:, 1:3, :],
                                               con[:, C_MQK:C_MQK + 2 * P].rearrange("p (a b) -> p a b", a=2)))
                    back = 2.0 ** -(X_EXP + W_EXP)
                    link(nc.vector.tensor_scalar(c_th[:], pow2[:, 0:1], 0.7978845608028654 * back, None, ALU.mult))
                    link(nc.vector.tensor_scalar(c_sq[:], pow2[:, 0:1], 0.044715 ** 0.5 * back, None, ALU.mult))
                    link(nc.vector.tensor_tensor(c_dn[:], pow2[:, 0:1], pow2[:, 1:2], ALU.mult))
                    link(nc.vector.tensor_scalar(c_dn[:], c_dn[:], pow2[:, 2:3], 2.0 ** -(W_EXP + I_EXP),
                                                 ALU.mult, ALU.mult))
                    dve.wait_ge(s["attn_b_weights_in"], 16 * 2)
                    link(nc.vector.tensor_scalar(bqk[:], bqk[:], 2.0 ** (X_EXP + WB_EXP), None, ALU.mult))
                    dve.wait_ge(s["a_xn_biased"], 1)
                    for i in range(A_STEPS):
                        a_vector(dve, link, 1, i)
                        weights_vector(dve, link, (1, i))
            nc.all_engine_barrier(sems_to_clear=stage_signals)

        def feed_forward(b, stage, next_b):
            last = stage == 1
            side = next_b is not None
            with nc.Block() as block:
                @block.sync
                def _(sp):
                    if side:
                        a_sync(sp, stage, next_b, True)
                    if last:
                        sp.wait_ge(s["f_done"], RT)
                        sp.dma_start(out[bass.ds(b, 1)].rearrange("o (j p) w -> p (o j) w", p=P), xn
                                     ).then_inc(s["x_out_stored"], 16)
                        if not side:
                            sp.wait_ge(s["x_out_stored"], 16)

                @block.gpsimd
                def _(pool):
                    ln_root(pool)
                    for i in range(NCH):
                        if i < NCH - 1:
                            pool.wait_ge(s["inter_hi_ready"], i + 1)
                            if i >= R:
                                pool.wait_ge(s["down_used"], i - R + 1)
                            nc.gpsimd.tensor_tensor(il[i % R], inter[i % R], ih[i % R], ALU.subtract
                                                    ).then_inc(s["inter_lo_ready"], 1)
                        if side:
                            a_gpsimd(pool, stage, i)

                @block.scalar
                def _(act):
                    act.wait_ge(s["xt_ready"], 1)
                    for kt in range(KT):
                        nc.scalar.copy(xh[:, kt, :], bank(6 + kt)).then_inc(s["xt_evacuated"], 1)

                    def square(i):
                        act.wait_ge(s["gate_ready"], i + 1)
                        if i >= 2:
                            act.wait_ge(s["cubic_ready"], i - 1)
                        nc.scalar.activation(sq[i % 2], bank(i % 2), ACT.Square, scale=c_sq[:, 0:1]
                                             ).then_inc(s["square_ready"], 1)

                    square(0)
                    for i in range(NCH):
                        act.wait_ge(s["cubic_ready"], i + 1)
                        if i >= 2:
                            act.wait_ge(s["inter_ready"], i - 1)
                        nc.scalar.activation(th[i % 2], cub[i % 2], ACT.Tanh, scale=c_th[:, 0:1]
                                             ).then_inc(s["tanh_ready"], 1)
                        if i + 1 < NCH:
                            square(i + 1)
                        act.wait_ge(s["inter_ready"], i + 1)
                        if i >= R:
                            act.wait_ge(s["down_used"], i - R + 1)
                        nc.scalar.copy(ih[i % R], inter[i % R]).then_inc(s["inter_hi_ready"], 1)
                        if side:
                            a_scalar(act, stage, i)
                    act.wait_ge(s["down_used"], NCH)
                    for m in range(2):
                        half = slice(m * (ROWS // 2), (m + 1) * (ROWS // 2))
                        nc.scalar.activation(yt[:, 0, half], bank(4)[:, half], ACT.Copy, scale=c_dn[:, 0:1]
                                             ).then_inc(s["down_out"], 1)

                @block.tensor
                def _(pe):
                    transpose_rows(pe, lambda r, kt: r.rearrange("p (m k) -> p k m", k=KT)[:, kt],
                                   12 if stage == 0 else 4)

                    def hidden(m, i, o):
                        n = 0
                        for w, xx, ready in ((w_hi[m], xh, "xt_evacuated"), (w_lo[m], xh, None),
                                             (w_hi[m], xl, "xt_lo_ready")):
                            for kt in range(KT):
                                if i == m == 0 and ready:
                                    pe.wait_ge(s[ready], kt + 1)
                                c = kt * F + i * P
                                ins = nc.tensor.matmul(o, w[:, c:c + P], xx[:, kt, :],
                                                       start=n == 0, stop=n == 3 * KT - 1)
                                n += 1
                        return ins

                    def down(i):
                        c = i * D
                        pe.wait_ge(s["inter_hi_ready"], i + 1)
                        for n, (w, v) in enumerate(((w_hi[2], ih), (w_lo[2], ih), (w_hi[2], il))):
                            if n == 2:
                                pe.wait_ge(s["inter_lo_ready"], i + 1)
                            for ht in range(KT):
                                ins = nc.tensor.matmul(bank(4 + ht), w[:, c + ht * P:c + (ht + 1) * P], v[i % R],
                                                       start=i == 0 and n == 0, stop=i == NCH - 1 and n == 2)
                        ins.then_inc(s["down_used"], 1)

                    for i in range(NCH + LAG):
                        if i < NCH:
                            if i >= 2:
                                pe.wait_ge(s["inter_ready"], i - 1)
                            hidden(0, i, bank(i % 2)).then_inc(s["gate_ready"], 1)
                            hidden(1, i, bank(2 + i % 2)).then_inc(s["up_ready"], 1)
                        if i >= LAG:
                            down(i - LAG)
                        if side and i < A_STEPS:
                            a_tensor(pe, stage, i)
                    for j in range(RT):
                        pe.wait_ge(s["down_out"], j // 2 + 1)
                        pe.wait_ge(s["down_out_v"], j // 2 + 1)
                        for ht in range(KT):
                            ins = nc.tensor.transpose(bank(j)[:, ht * P:(ht + 1) * P],
                                                      yt[:, ht, j * P:(j + 1) * P], ident)
                        ins.then_inc(s["down_t_ready"], 1)

                @block.vector
                def _(dve):
                    link = chain(dve, s["dve_chain"])
                    if stage == 0:
                        dve.wait_ge(s["a_back"], 16)
                        for j in range(RT):
                            nc.vector.tensor_tensor(X[:, j], xa[:, j], a_back[:, j], ALU.add
                                                    ).then_inc(s["x_taken"], 1)
                        for j in range(RT):
                            dve.wait_ge(s["x_taken"], j + 1)
                            ins = nc.vector.bn_stats(stats[:, j, :], X[:, j, :])
                        link(ins)
                    ln_gather(dve, link)
                    if stage == 0:
                        dve.wait_ge(s["x_out_stored"], 16)
                    ln_apply(dve, X)
                    for kt in range(KT):
                        dve.wait_ge(s["xt_evacuated"], kt + 1)
                        nc.vector.tensor_tensor(xl[:, kt, :], bank(6 + kt), xh[:, kt, :], ALU.subtract
                                                ).then_inc(s["xt_lo_ready"], 1)

                    def cubic(i):
                        dve.wait_ge(s["square_ready"], i + 1)
                        if i >= 2:
                            dve.wait_ge(s["tanh_ready"], i - 1)
                        nc.vector.scalar_tensor_tensor(cub[i % 2], sq[i % 2], 1.0, bank(i % 2), ALU.add, ALU.mult
                                                       ).then_inc(s["cubic_ready"], 1)

                    cubic(0)
                    for i in range(NCH):
                        dve.wait_ge(s["tanh_ready"], i + 1)
                        link(nc.vector.scalar_tensor_tensor(gl[i % 2], th[i % 2], 1.0, bank(i % 2),
                                                            ALU.add, ALU.mult))
                        dve.wait_ge(s["up_ready"], i + 1)
                        if i >= R:
                            dve.wait_ge(s["inter_lo_ready"], i - R + 1)
                        nc.vector.scalar_tensor_tensor(inter[i % R], gl[i % 2],
                                                       0.5 * 2.0 ** (I_EXP - 2 * (X_EXP + W_EXP)),
                                                       bank(2 + i % 2), ALU.mult, ALU.mult
                                                       ).then_inc(s["inter_ready"], 1)
                        if i + 1 < NCH:
                            cubic(i + 1)
                        if i == NCH - 1:
                            dve.wait_ge(s["inter_lo_ready"], i)
                            dve.wait_ge(s["inter_hi_ready"], i + 1)
                            dve.wait_ge(s["down_used"], i - R + 1)
                            nc.vector.tensor_tensor(il[i % R], inter[i % R], ih[i % R], ALU.subtract
                                                    ).then_inc(s["inter_lo_ready"], 1)
                        if side:
                            a_vector(dve, link, stage, i)
                    dve.wait_ge(s["down_used"], NCH)
                    for m in range(2):
                        half = slice(m * (ROWS // 2), (m + 1) * (ROWS // 2))
                        nc.vector.tensor_scalar(yt[:, 1, half], bank(5)[:, half], c_dn[:, 0:1], None, ALU.mult
                                                ).then_inc(s["down_out_v"], 1)
                    for j in range(RT):
                        dve.wait_ge(s["down_t_ready"], j + 1)
                        nc.vector.tensor_tensor((xn if last else X)[:, j], X[:, j], bank(j)[:, 0:D], ALU.add
                                                ).then_inc(s["f_done"], 1)
                        if stage == 0 and j:
                            dve.wait_ge(s["f_done"], j)
                            nc.vector.bn_stats(stats[:, j - 1, :], X[:, j - 1, :])
                    if stage == 0:
                        dve.wait_ge(s["f_done"], RT)
                        link(nc.vector.bn_stats(stats[:, RT - 1, :], X[:, RT - 1, :]))
            nc.all_engine_barrier(sems_to_clear=all_signals if stage == 0 or not side else stage_signals)

        arena_at[0] = 0
        qs = part([66, NH, ROWS], f16)
        ks = part([66, NH, ROWS], f16)
        heads_at = arena_at[0]
        qf = part([P, 4, ROWS])
        rsin = part([P, 4, ROWS])
        rh = part([P, 4, ROWS], f16)
        rl = part([P, 4, ROWS], f16)
        vf = part([P, RT, NH, HD])
        arena_at[0] = heads_at
        pt = [part([P, STRIPS]) for _ in range(PR)]
        ph = [part([P, STRIPS], f16) for _ in range(PR)]
        pl = [part([P, STRIPS], f16) for _ in range(PR)]
        ot = [row_memory[:, 2 * RT * D + n * ROWS:2 * RT * D + (n + 1) * ROWS] for n in range(2)]
        nmax = sb("nmax", [P, NH * RT])
        mxh = sb("mxh", [2 * RT, 2, 2, P], f16)
        rec = sb("rec", [P, RT, 2])
        osc = sb("osc", [P, RT, 2, HD])
        ring = 3
        steps = NH + 4
        LEAD = 4

        def act_strips(n):
            return 896 if n < NH - LEAD else 896

        def pool_strips(n):
            return 1152 if n < NH - LEAD else 896

        def max_bank(q):
            return bank(6 + q) if q < 2 else bank(2)[:, 256:]

        def score_base(n):
            return ring * (n % 2) if n < LEAD else 0

        def attention_b():
            with nc.Block() as block:
                @block.sync
                def _(sp):
                    sp.dma_start(ks[64:66], ring_rows).then_inc(s["b_max_row_in"], 16)

                    def spill_out(t):
                        g, which = divmod(t, 2)
                        for lo, src, ready in ((0, rh, "b_hi_ready"), (1, rl, "b_lo_ready")):
                            sp.wait_ge(s[ready], t + 1)
                            sp.dma_start(spill[which, HG * g:HG * g + HG, lo], src[:, t, :]
                                         ).then_inc(s[f"b_spilled{t}"], 16)

                    def stack(t):
                        g, which = divmod(t, 2)
                        heads = slice(HG * g, HG * g + HG)
                        sp.wait_ge(s[f"b_spilled{t}"], 32)
                        stacked = s[f"b_stacked{g}"]
                        both = spill[which, heads].rearrange("n l c r -> (l c) n r")
                        dst = (qs, ks)[which]
                        sp.dma_start(dst[0:2 * HD, heads, :], both).then_inc(stacked, 16)
                        if which:
                            sp.dma_start(dst[2 * HD:4 * HD, heads, :], both).then_inc(stacked, 16)
                        else:
                            for c, lo in ((2, 1), (3, 0)):
                                sp.dma_start(dst[HD * c:HD * c + HD, heads, :],
                                             spill[which, heads, lo].rearrange("n c r -> c n r")
                                             ).then_inc(stacked, 16)

                    spill_out(0)
                    spill_out(1)
                    stack(0)
                    stack(1)
                    spill_out(2)
                    spill_out(3)
                    stack(2)
                    stack(3)
                    for q in range(NH // 2):
                        max_in = s[f"b_max_in{q % 2}"]
                        if q >= 2:
                            sp.wait_ge(max_in, 32 * (q // 2))
                        for lo in range(2):
                            sp.wait_ge(s["b_max_lo"] if lo else s["b_max_hi"], q + 1)
                            sp.dma_start(qs[64 + lo:65 + lo, 2 * q:2 * q + 2, :].rearrange(
                                "o n (t r) -> o (n t) r", r=P), mxh[:, q % 2, lo, :]).then_inc(max_in, 16)

                @block.gpsimd
                def _(pool):
                    ln_root(pool)
                    for t in range(4):
                        pool.wait_ge(s["b_hi_ready"], t + 1)
                        nc.gpsimd.tensor_tensor(rl[:, t, :], qf[:, t, :], rh[:, t, :], ALU.subtract
                                                ).then_inc(s["b_lo_ready"], 1)
                    pool.wait_ge(s["b_vhi_ready"], 1)
                    nc.gpsimd.tensor_tensor(va[:, :, :, HD:2 * HD], vf, va[:, :, :, 0:HD], ALU.subtract
                                            ).then_inc(s["b_vlo_ready"], 1)
                    for n in range(NH):
                        pool.wait_ge(s["b_phi_ready"], n + 1)
                        if n >= PR:
                            pool.wait_ge(s["b_av_done"], n - PR + 1)
                        pool.wait_ge(s["b_phi_end_ready"], n + 1)
                        nc.gpsimd.tensor_tensor(pl[n % PR][:, 0:pool_strips(n)], pt[n % PR][:, 0:pool_strips(n)],
                                                ph[n % PR][:, 0:pool_strips(n)], ALU.subtract
                                                ).then_inc(s["b_plo_ready"], 1)

                @block.scalar
                def _(act):
                    act.wait_ge(s["xt_ready"], 1)
                    for kt in range(KT):
                        nc.scalar.copy(xh[:, kt, :], bank(6 + kt)).then_inc(s["xt_evacuated"], 1)
                    for t in range(4):
                        act.wait_ge(s["b_rope_ready"], t + 1)
                        nc.scalar.copy(rh[:, t, :], qf[:, t, :]).then_inc(s["b_hi_ready"], 1)
                    act.wait_ge(s["b_v_out"], 1)
                    nc.scalar.copy(va[:, :, :, 0:HD], vf).then_inc(s["b_vhi_ready"], 1)

                    def max_hi(q):
                        act.wait_ge(s["b_max_t_ready"], q + 1)
                        if q >= 2:
                            act.wait_ge(s[f"b_max_in{q % 2}"], 32 * (q // 2))
                        nc.scalar.copy(mxh[:, q % 2, 0, :], max_bank(q)[0:2 * RT, 0:P]
                                       ).then_inc(s["b_max_hi"], 1)

                    max_hi(0)
                    max_hi(1)
                    for n in range(steps):
                        if n < NH:
                            act.wait_ge(s["b_kq_ready"], n + 1)
                            if n >= PR:
                                act.wait_ge(s["b_plo_ready"], n - PR + 1)
                                act.wait_ge(s["b_plo_end_ready"], n - PR + 1)
                            elif n == 0:
                                act.wait_ge(s["b_vlo_ready"], 1)
                                act.wait_ge(s["b_spilled3"], 32)
                            nc.scalar.activation(pt[n % PR], bank(3, 3)[:, 0:STRIPS], ACT.Exp,
                                                 scale=float(HD) ** -0.5).then_inc(s["b_exp_ready"], 1)
                            if n % 2 and (n + 1) // 2 + 1 < NH // 2:
                                max_hi((n + 1) // 2 + 1)
                            act.wait_ge(s["b_exp_ready"], n + 1)
                            if n >= PR:
                                act.wait_ge(s["b_av_done"], n - PR + 1)
                            nc.scalar.copy(ph[n % PR][:, 0:act_strips(n)], pt[n % PR][:, 0:act_strips(n)]
                                           ).then_inc(s["b_phi_ready"], 1)
                        if n % 2 == 0 and n >= 4:
                            p = (n - 4) // 2
                            act.wait_ge(s["b_av_done"], 2 * p + 2)
                            if p >= 2:
                                act.wait_ge(s["b_o_t_ready"], p - 1)
                            if p < NH // 2:
                                nc.scalar.copy(ot[p % 2], bank(6 + p % 2)).then_inc(s["b_o_out"], 1)

                @block.tensor
                def _(pe):
                    transpose_rows(pe, lambda r, kt: r[:, kt * P:(kt + 1) * P], 4)

                    def three(o, left, right, wait=False):
                        n = 0
                        for a, b_, ready in ((0, 0, "xt_evacuated"), (1, 0, None), (0, 1, "xt_lo_ready")):
                            for kt in range(KT):
                                if wait and ready:
                                    pe.wait_ge(s[ready], kt + 1)
                                ins = nc.tensor.matmul(o, left(a, kt), right(b_, kt),
                                                       start=n == 0, stop=n == 3 * KT - 1)
                                n += 1
                        return ins

                    for t in range(4):
                        g, which = divmod(t, 2)
                        if t == 3:
                            pe.wait_ge(s["b_rope_sum"], 2)
                        for swap in range(2):
                            three(bank(2 * (t % 3) + swap),
                                  lambda a, kt: (wb_hi, wb_lo)[a][:, kt, 2 * which + swap, g * P:(g + 1) * P],
                                  lambda a, kt: (xh, xl)[a][:, kt, :], wait=t == swap == 0).then_inc(s["b_qk_projected"], 1)
                    for j in range(RT):
                        ins = three(bank(6 + j // 2)[:, (j % 2) * D:(j % 2 + 1) * D],
                                    lambda a, kt: (xh, xl)[a][:, kt, j * P:(j + 1) * P],
                                    lambda a, kt: (wb_hi, wb_lo)[a][:, kt, 4, :])
                    ins.then_inc(s["b_v_ready"], 1)
                    pe.wait_ge(s["b_rope_sum"], 8)
                    keep_clock(bank(0), 16)
                    pe.wait_ge(s["b_stacked0"], 16 * 5)
                    pe.wait_ge(s["b_rope_ready"], 4)
                    pe.wait_ge(s["b_max_row_in"], 16)

                    def row_scores(n):
                        if n == HG:
                            pe.wait_ge(s["b_stacked1"], 16 * 5)
                        S = bank(score_base(n), ring)
                        for k, (t, (o, w)) in enumerate(QK_STRIP.items()):
                            if n >= 1 and (n >= LEAD or n % 2 == 0 or n == 3):
                                pe.wait_ge(s["b_max_taken"], RT * (n - 1 if n >= LEAD else n - 2) + TAKEN[k])
                            if o >= 1024 and n >= LEAD + 2:
                                pe.wait_ge(s["b_max_lo"], n // 2)
                            nc.tensor.matmul(S[:, o:o + w], qs[0:64, n, t * P:(t + 1) * P], ks[0:64, n, 0:w],
                                             start=True, stop=False, skip_group_check=True)
                            ins = nc.tensor.matmul(S[:, o + w - P:o + w], masks[:, 0, :], masks[:, 1, :],
                                                   start=False, stop=True, skip_group_check=True)
                            if k in (0, 2, 3):
                                ins.then_inc(s["b_qk_ready"], 1)

                    def max_turn(q):
                        pe.wait_ge(s["b_max_scaled"], q + 1)
                        if q >= 3:
                            pe.wait_ge(s["b_max_lo"], q)
                        nc.tensor.transpose(max_bank(q)[0:2 * RT, 0:P],
                                            nmax[:, 2 * RT * q:2 * RT * (q + 1)], ident
                                            ).then_inc(s["b_max_t_ready"], 1)

                    def column_scores(n):
                        if n % 2 == 0:
                            pe.wait_ge(s[f"b_max_in{n // 2 % 2}"], 32 * (n // 4 + 1))
                        if n >= 1:
                            pe.wait_ge(s["b_exp_ready"], n)
                        else:
                            pe.wait_ge(s["b_max_taken"], RT * LEAD)
                        S = bank(3, 3)
                        for t, (o, w) in KQ_STRIP.items():
                            nc.tensor.matmul(S[:, o:o + w], ks[0:66, n, t * P:(t + 1) * P],
                                             qs[0:66, n, t * P:ROWS], start=True, stop=False,
                                             skip_group_check=True)
                            ins = nc.tensor.matmul(S[:, o:o + P], masks[:, 0, :], masks[:, 2, :],
                                                   start=False, stop=True, skip_group_check=True)
                        ins.then_inc(s["b_kq_ready"], 1)

                    def values(n):
                        p, r = divmod(n, 2)
                        if r == 0 and p < 2:
                            pe.wait_ge(s["b_max_lo"], p + 1)
                        if r == 0 and p >= 2:
                            pe.wait_ge(s["b_o_added"], p - 1)
                        pe.wait_ge(s["b_plo_ready"], n + 1)
                        pe.wait_ge(s["b_plo_end_ready"], n + 1)
                        for t in range(RT):
                            o, w = KQ_STRIP[t]
                            for x, part_ in enumerate((ph, pl)):
                                ins = nc.tensor.matmul(bank(6 + p % 2)[OW * r:OW * r + OW, t * P:ROWS],
                                                       va[:, t, n, :], part_[n % PR][:, o:o + w],
                                                       start=t == 0 and x == 0, stop=t == RT - 1 and x == 1,
                                                       skip_group_check=True)
                        ins.then_inc(s["b_av_done"], 1)

                    def turn(p):
                        pe.wait_ge(s["b_o_out"], p + 1)
                        for j in range(RT):
                            ins = nc.tensor.matmul(bank(6 + p % 2)[:, j * OUT:(j + 1) * OUT],
                                                   ot[p % 2][:, j * P:(j + 1) * P], both_parts,
                                                   start=True, stop=True)
                        ins.then_inc(s["b_o_t_ready"], 1)

                    row_scores(0)
                    row_scores(1)
                    row_scores(2)
                    pe.wait_ge(s["b_v_out"], 1)
                    keep_clock(bank(7), 4)
                    max_turn(0)
                    row_scores(3)
                    keep_clock(bank(7), 10)
                    max_turn(1)
                    pe.wait_ge(s["b_vlo_ready"], 1)
                    for n in range(steps):
                        if n % 2 == 0 and 2 <= n and n // 2 + 1 < NH // 2:
                            max_turn(n // 2 + 1)
                        if n % 2 and n + LEAD < NH:
                            row_scores(n + LEAD)
                        if n < NH:
                            column_scores(n)
                        if n % 2 == 0 and n + LEAD < NH:
                            row_scores(n + LEAD)
                        if n < 2:
                            pe.wait_ge(s["b_max_lo"], 2)
                            keep_clock(bank(7), 4)
                        if n % 2 and n >= 5:
                            turn((n - 5) // 2)
                        if 0 <= n - 2 < NH:
                            values(n - 2)

                @block.vector
                def _(dve):
                    link = chain(dve, s["dve_chain"])
                    ln_gather(dve, link)
                    ln_apply(dve, X)
                    for kt in range(KT):
                        dve.wait_ge(s["xt_evacuated"], kt + 1)
                        nc.vector.tensor_tensor(xl[:, kt, :], bank(6 + kt), xh[:, kt, :], ALU.subtract
                                                ).then_inc(s["xt_lo_ready"], 1)
                    for t in range(4):
                        g, which = divmod(t, 2)
                        for swap, (dst, table) in enumerate(((qf, cos_t), (rsin, sin_t))):
                            dve.wait_ge(s["b_qk_projected"], 2 * t + swap + 1)
                            nc.vector.scalar_tensor_tensor(dst[:, t, :], bank(2 * (t % 3) + swap),
                                                           bqk[:, which, swap, g:g + 1], table, ALU.add, ALU.mult
                                                           ).then_inc(s["b_rope_sum"], 1)
                        dve.wait_ge(s["b_rope_sum"], 2 * t + 2)
                        nc.vector.tensor_tensor(qf[:, t, :], qf[:, t, :], rsin[:, t, :], ALU.add
                                                ).then_inc(s["b_rope_ready"], 1)
                    dve.wait_ge(s["b_v_ready"], 1)
                    for j in range(RT):
                        ins = nc.vector.scalar_tensor_tensor(
                            vf[:, j],
                            bank(6 + j // 2)[:, (j % 2) * D:(j % 2 + 1) * D].rearrange(
                                "p (n c) -> p n c", c=HD), 2.0 ** -(X_EXP + WB_EXP), bv[:], ALU.mult, ALU.add)
                    ins.then_inc(s["b_v_out"], 1)

                    def maxima(n):
                        for k, (t, (o, w)) in enumerate(QK_STRIP.items()):
                            if k != 2:
                                dve.wait_ge(s["b_qk_ready"], 3 * n + (1, 2, 2, 3)[k])
                            nc.vector.tensor_reduce(nmax[:, RT * n + t:RT * n + t + 1],
                                                    bank(score_base(n), ring)[:, o:o + w], AX.X, ALU.max,
                                                    negate=True).then_inc(s["b_max_taken"], 1)
                        if n % 2:
                            m = nmax[:, RT * (n - 1):RT * (n + 1)]
                            dve.wait_ge(s["b_max_taken"], RT * (n + 1))
                            nc.vector.tensor_scalar(m, m, 2.0 ** -MAX_EXP, None, ALU.mult
                                                    ).then_inc(s["b_max_scaled"], 1)

                    def max_lo(q):
                        dve.wait_ge(s["b_max_hi"], q + 1)
                        if q >= 2:
                            dve.wait_ge(s[f"b_max_in{q % 2}"], 32 * (q // 2))
                        nc.vector.tensor_tensor(mxh[:, q % 2, 1, :], max_bank(q)[0:2 * RT, 0:P],
                                                mxh[:, q % 2, 0, :], ALU.subtract).then_inc(s["b_max_lo"], 1)

                    def split(n):
                        if n >= NH:
                            return
                        dve.wait_ge(s["b_exp_ready"], n + 1)
                        if n >= PR:
                            dve.wait_ge(s["b_av_done"], n - PR + 1)
                        nc.vector.tensor_copy(ph[n % PR][:, act_strips(n):], pt[n % PR][:, act_strips(n):]
                                              ).then_inc(s["b_phi_end_ready"], 1)
                        dve.wait_ge(s["b_phi_end_ready"], n + 1)
                        nc.vector.tensor_tensor(pl[n % PR][:, pool_strips(n):], pt[n % PR][:, pool_strips(n):],
                                                ph[n % PR][:, pool_strips(n):], ALU.subtract
                                                ).then_inc(s["b_plo_end_ready"], 1)

                    def rows_out(n):
                        if n % 2 == 0 or n < 5:
                            return
                        p = (n - 5) // 2
                        dve.wait_ge(s["b_o_t_ready"], p + 1)
                        T = bank(6 + p % 2)[:, 0:RT * OUT].rearrange("p (j r c) -> p j r c", j=RT, r=2)
                        link(nc.vector.reciprocal(rec[:], T[:, :, :, HD]))
                        link(nc.vector.tensor_tensor(osc[:], T[:, :, :, 0:HD],
                                                     rec[:].unsqueeze(3).broadcast_to([P, RT, 2, HD]),
                                                     ALU.mult))
                        xo = X[:, :, 2 * HD * p:2 * HD * (p + 1)].rearrange("p j (r c) -> p j r c", c=HD)
                        nc.vector.tensor_tensor(xo, xo, osc[:], ALU.add).then_inc(s["b_o_added"], 1)
                        dve.wait_ge(s["b_o_added"], p + 1)

                    maxima(0)
                    maxima(1)
                    max_lo(0)
                    maxima(2)
                    maxima(3)
                    max_lo(1)
                    for n in range(steps):
                        if n + LEAD < NH:
                            maxima(n + LEAD)
                        if n + LEAD < NH:
                            split(n)
                            if n % 2 and (n + 1) // 2 + 1 < NH // 2:
                                max_lo((n + 1) // 2 + 1)
                            rows_out(n)
                        else:
                            rows_out(n)
                            split(n)
                    for j in range(RT):
                        ins = nc.vector.bn_stats(stats[:, j, :], X[:, j, :])
                    link(ins)
            nc.all_engine_barrier(sems_to_clear=stage_signals)

        prepare(0)
        with nc.Fori(0, B - 1) as b:
            feed_forward(None, 0, b + 1)
            attention_b()
            feed_forward(b, 1, b + 1)
        feed_forward(None, 0, None)
        attention_b()
        feed_forward(B - 1, 1, None)


def shape_constants():
    c = np.zeros((P, C_ALL), np.float32)
    i = np.arange(P)
    c[i, C_ID + i] = 1
    c[:, C_MQK:C_MQK + P] = np.where(i[None, :] > i[:, None], NEG, 0)
    c[:, C_MKQ:C_MKQ + P] = np.where(i[:, None] > i[None, :], NEG, 0)
    for r in range(2):
        n = np.arange(HD)
        c[OW * r + n, C_BOTH + r * (HD + 1) + n] = 1
        c[OW * r + HD + n, C_BOTH + r * (HD + 1) + n] = 1
        c[OW * r + 2 * HD, C_BOTH + r * (HD + 1) + HD] = 1
    inv = (1.0 / np.float32(10000.0) ** (np.arange(0, HD, 2, dtype=np.float32) / np.float32(HD))).astype(np.float32)
    angle = (np.arange(ROWS, dtype=np.float32)[None, :] * inv[i % (HD // 2)][:, None]).astype(np.float32)
    back = 2.0 ** -(X_EXP + WB_EXP)
    sign = np.where(i % HD < HD // 2, -1.0, 1.0)[:, None]
    c[:, C_COS:C_COS + ROWS] = np.cos(angle.astype(np.float64)).astype(np.float32) * back
    c[:, C_SIN:C_SIN + ROWS] = np.sin(angle.astype(np.float64)).astype(np.float32) * sign * back
    return c


def kernel(**inputs):
    import concourse.bacc as bacc
    from concourse.bass_utils import run_bass_kernel_spmd

    given = {n: np.asarray(v) for n, v in inputs.items()}
    a, f = "L0_attn_a_", "L0_ffn_"
    arrays = {"x": np.ascontiguousarray(given[a + "x"])}
    w, pw = given[a + "qkv_w"], given[a + "proj_w"]
    blocks = np.zeros((WIN, CH, 2, 3, WIN, HCH), w.dtype)
    shifted = np.zeros((WIN, CH, 3, WIN, HCH), w.dtype)
    proj = np.zeros((2, WIN, HCH, WIN, CH), pw.dtype)
    for t in range(WIN):
        blocks[t, :, :, :, t, :] = w.reshape(CH, 3, 2, HCH).transpose(0, 2, 1, 3)
        proj[:, t, :, t, :] = pw.reshape(2, HCH, CH)
        for tap in range(3):
            if 0 <= t + tap - 1 < WIN:
                shifted[t + tap - 1, :, tap, t, :] = w[:, 2 * CH:2 * CH + HCH]
    arrays["a_qkv_blocks"] = blocks.reshape(P, -1)
    arrays["a_shifted_blocks"] = shifted.reshape(P, -1)
    arrays["a_proj_blocks"] = proj.reshape(P, -1)
    arrays["a_taps"] = np.stack([given[a + "conv_w0"][:, 0, 1, :].T, given[a + "conv_w1"][:, 0, :, 1].T]).reshape(-1)
    arrays["a_conv_bias"] = np.concatenate([given[a + "conv_b0"], given[a + "conv_b1"]]).reshape(CH, 1)
    arrays["a_proj_w"] = np.ascontiguousarray(pw)
    arrays["a_rows"] = np.concatenate([given[a + n] for n in ("proj_b", "ln_w", "ln_b")])
    w = given["L0_attn_b_w_qkv"].reshape(NH, 3, HD, D).transpose(3, 1, 0, 2).reshape(D, 3, NH * HD)
    bias = given["L0_attn_b_b_qkv"].reshape(2, HG, 3, HD)
    swapped = np.arange(NH * HD).reshape(NH, 2, HD // 2)[:, ::-1].reshape(-1)
    arrays["b_qkv_t"] = np.ascontiguousarray(
        np.stack([w[:, 0], w[:, 0][:, swapped], w[:, 1], w[:, 1][:, swapped], w[:, 2]], 1))
    both = np.stack([bias[:, :, 0:2], np.roll(bias[:, :, 0:2], HD // 2, -1)])
    arrays["b_bias_t"] = np.ascontiguousarray(both.transpose(2, 4, 3, 0, 1)).reshape(P, 8)
    arrays["bv_row"] = np.ascontiguousarray(bias[:, :, 2]).reshape(-1)
    arrays["ring_rows"] = np.full((2, NH, ROWS), 2.0 ** MAX_EXP, np.float16)
    for n in MATRICES:
        arrays[n + "_words"] = np.ascontiguousarray(given[f + n + "_W_packed"].T)
        arrays[n + "_scale_t"] = np.ascontiguousarray(given[f + n + "_scales"].T)
    arrays["consts"] = shape_constants()

    nc = bacc.Bacc("TRN2", target_bir_lowering=False, num_devices=1)
    aps = [nc.dram_tensor(f"in_{n}", v.shape, mybir.dt.from_np(v.dtype), kind="ExternalInput").ap()
           for n, v in arrays.items()]
    scratch = nc.dram_tensor("scratch", (CH, ROWS * CH), mybir.dt.float32, kind="Internal").ap()
    spill = nc.dram_tensor("spill", (2, NH, 2, HD, ROWS), mybir.dt.float16, kind="Internal").ap()
    out = nc.dram_tensor("out_dram", (B, ROWS, D), mybir.dt.float32, kind="ExternalOutput").ap()
    program(nc, *aps, scratch, spill, out)
    r = run_bass_kernel_spmd(nc, [{f"in_{n}": v for n, v in arrays.items()}], core_ids=[0])
    return r.results[0]["out_dram"]
```
